# Optimizing a Trainium2 kernel written in Bass

```python
import numpy as np
import jax
import jax.numpy as jnp

def _softmax(x, axis=-1):
    return jax.nn.softmax(x, axis=axis)

def _gelu(x):
    return jax.nn.gelu(x, approximate=True)

def _silu(x):
    return jax.nn.silu(x)

def _sigmoid(x):
    return jax.nn.sigmoid(x)

def _layernorm(x, axis=-1, eps=1e-05):
    m = jnp.mean(x, axis=axis, keepdims=True)
    v = jnp.var(x, axis=axis, keepdims=True)
    return (x - m) / jnp.sqrt(v + eps)

def _scatter_add(tgt, idx, src, axis=0):
    return tgt.at[idx].add(src)

def _segment_sum(src, seg, n):
    return jax.ops.segment_sum(src, seg, n)
kernel_name = 'mk_hybrid_d2_jaxref_r8_95c5ce'

def setup_inputs(seed: int=0):
    np.random.seed(seed)
    _w = jnp.asarray

    def _L0_attn_a_setup():
        import jax, jax.numpy as jnp
        import numpy as np
        H, D, CR, SEL_K = (8, 64, 32, 16)
        ROPE_DIM, THETA, WINDOW, GROUPS = (32, 10000.0, 64, 2)
        INTER, HID, QC = (64, 128, 32)
        NEG = -1e+30

        def _rope_cache(t):
            half = ROPE_DIM // 2
            inv = 1.0 / THETA ** (jnp.arange(half, dtype=jnp.float32) * 2.0 / ROPE_DIM)
            ang = jnp.arange(t, dtype=jnp.float32)[:, None] * inv[None, :]
            return (jnp.cos(ang), jnp.sin(ang))

        def _apply_partial_rope(x, cos, sin):
            half = ROPE_DIM // 2
            x1, x2, rest = (x[..., :half], x[..., half:ROPE_DIM], x[..., ROPE_DIM:])
            return jnp.concatenate([x1 * cos - x2 * sin, x1 * sin + x2 * cos, rest], -1)

        def _rmsnorm(x, g, eps=1e-06):
            return x * jax.lax.rsqrt(jnp.mean(x * x, -1, keepdims=True) + eps) * g
        key = jax.random.key(seed)
        ks = jax.random.split(key, 9)
        f = lambda k, shp, s: jax.random.normal(k, shp, jnp.float32) * s
        return {'h': f(ks[0], (1, 256, HID), 1.0), 'w_qc': f(ks[1], (HID, QC), QC ** (-0.5)), 'w_qup': f(ks[2], (QC, H * D), (H * D) ** (-0.5)), 'w_k': f(ks[3], (HID, D), HID ** (-0.5)), 'w_v': f(ks[4], (HID, D), HID ** (-0.5)), 'g_qnorm': jnp.ones((D,), jnp.float32), 'g_knorm': jnp.ones((D,), jnp.float32), 'w_gate': f(ks[5], (D, 3), 0.05), 'b_gate': jnp.zeros((3,), jnp.float32), 'sink_logit': f(ks[6], (H,), 0.1), 'w_out_group': f(ks[7], (GROUPS, H // GROUPS * D, INTER), 0.05), 'w_out': f(ks[8], (GROUPS * INTER, HID), 0.03)}
    _L0_attn_a_in = _L0_attn_a_setup()

    def _L0_attn_b_setup():
        import jax, jax.numpy as jnp
        import numpy as np
        D_IN, HEAD_DIM = (128, 128)
        key = jax.random.key(seed)
        ks = jax.random.split(key, 9)
        s = 0.02
        return {'x': jax.random.normal(ks[0], (4, 512, D_IN), dtype=jnp.float32), 'Wq': jax.random.normal(ks[1], (HEAD_DIM, D_IN), dtype=jnp.float32) * s, 'bq': jnp.zeros((HEAD_DIM,), dtype=jnp.float32), 'Wk': jax.random.normal(ks[2], (HEAD_DIM, D_IN), dtype=jnp.float32) * s, 'bk': jnp.zeros((HEAD_DIM,), dtype=jnp.float32), 'Wv': jax.random.normal(ks[3], (HEAD_DIM, D_IN), dtype=jnp.float32) * s, 'bv': jnp.zeros((HEAD_DIM,), dtype=jnp.float32), 'Wo': jax.random.normal(ks[4], (D_IN, HEAD_DIM), dtype=jnp.float32) * s, 'bo': jnp.zeros((D_IN,), dtype=jnp.float32)}
    _L0_attn_b_in = _L0_attn_b_setup()

    def _L0_ffn_setup():
        import jax, jax.numpy as jnp
        import numpy as np
        TOP_K = 2
        key = jax.random.key(seed)
        ks = jax.random.split(key, 5)
        B, S, D, I, E = (4, 64, 128, 512, 8)
        x = jax.random.normal(ks[0], (B, S, D), dtype=jnp.float32)
        gate_w = jax.random.normal(ks[1], (E, D), dtype=jnp.float32) * 0.02
        w1 = jax.random.normal(ks[2], (E, I, D), dtype=jnp.float32) * 0.02
        w2 = jax.random.normal(ks[3], (E, D, I), dtype=jnp.float32) * 0.02
        w3 = jax.random.normal(ks[4], (E, I, D), dtype=jnp.float32) * 0.02
        return {'x': x, 'gate_w': gate_w, 'w1': w1, 'w2': w2, 'w3': w3}
    _L0_ffn_in = _L0_ffn_setup()

    def _L1_attn_a_setup():
        import jax, jax.numpy as jnp
        import numpy as np
        B, T = (2, 256)
        TOK, POS = (64, 64)
        H, D, KVH = (16, 64, 4)
        key = jax.random.key(seed)
        ks = jax.random.split(key, 7)

        def w(k, shape, fan_in):
            return jax.random.normal(k, shape, jnp.float32) / np.float32(np.sqrt(fan_in))
        x = jax.random.normal(ks[0], (B, T, TOK + POS), jnp.float32)
        Wq = w(ks[1], (POS, H * D), POS)
        Wk = w(ks[2], (POS, KVH * D), POS)
        Wv = w(ks[3], (TOK, KVH * D), TOK)
        Wo = w(ks[4], (H * D, TOK + POS), H * D)
        q_phase_angle = 0.1 * jax.random.normal(ks[5], (H,), jnp.float32)
        alibi_log_slopes = jnp.full((H,), np.float32(np.log(np.log(10.0))))
        return dict(x=x, Wq=Wq, Wk=Wk, Wv=Wv, Wo=Wo, q_phase_angle=q_phase_angle, alibi_log_slopes=alibi_log_slopes)
    _L1_attn_a_in = _L1_attn_a_setup()

    def _L1_attn_b_setup():
        import jax, jax.numpy as jnp
        import numpy as np
        L, E, H = (4, 128, 16)
        HD = E // H
        EPS_LN = 1e-05

        def _layernorm(x, w, b):
            m = jnp.mean(x, axis=-1, keepdims=True)
            v = jnp.mean((x - m) ** 2, axis=-1, keepdims=True)
            return (x - m) / jnp.sqrt(v + EPS_LN) * w + b

        def _to_quaternion(x):
            p1 = jnp.diff(x, axis=1, prepend=x[:, :1])
            p2 = jnp.roll(x, 1, axis=2)
            p3 = jnp.cos(x)
            return jnp.stack([x, p1, p2, p3], axis=-1)

        def _hamilton(a, b):
            a0, a1, a2, a3 = (a[..., 0], a[..., 1], a[..., 2], a[..., 3])
            b0, b1, b2, b3 = (b[..., 0], b[..., 1], b[..., 2], b[..., 3])
            return jnp.stack([a0 * b0 - a1 * b1 - a2 * b2 - a3 * b3, a0 * b1 + a1 * b0 + a2 * b3 - a3 * b2, a0 * b2 - a1 * b3 + a2 * b0 + a3 * b1, a0 * b3 + a1 * b2 - a2 * b1 + a3 * b0], axis=-1)

        def _spectral_filter(S):
            ks = jnp.fft.fftfreq(S).astype(jnp.float32)[:, None, None]
            kh = jnp.fft.fftfreq(H).astype(jnp.float32)[None, :, None]
            kd = jnp.fft.fftfreq(HD).astype(jnp.float32)[None, None, :]
            km = jnp.sqrt(ks ** 2 + kh ** 2 + kd ** 2 + 1e-10)
            f = jnp.exp(1j * jnp.arctan(jnp.log(km + 1e-10)))
            return f[None, :, :, :, None].astype(jnp.complex64)

        def _modulation(S):
            lam = jnp.arange(S, dtype=jnp.float32) / S
            t = jnp.arange(S, dtype=jnp.float32) * 0.1
            probe = jnp.sin(t + lam)
            phase = t - 2.0 * lam + 0.5 * lam ** 2
            return (probe * jnp.cos(phase))[None, :, None, None]

        def _attention(x, aw, ab, pw, pb):
            B, S, _ = x.shape
            qkv = (x @ aw + ab).reshape(B, S, H, 3 * HD)
            q, k, v = jnp.split(qkv, 3, axis=-1)
            qk = _hamilton(_to_quaternion(q), _to_quaternion(k))
            qkv_p = _hamilton(qk, _to_quaternion(v))
            f = jnp.fft.fftn(qkv_p.astype(jnp.complex64), axes=(-3, -2))
            out = jnp.fft.ifftn(f * _spectral_filter(S), axes=(-3, -2)).real
            a = out[..., 0] * (1.0 + 0.1 * _modulation(S))
            return a.reshape(B, S, E) @ pw + pb

        def _layer(x, p):
            ln1w, ln1b, aw, ab, pw, pb, ln2w, ln2b, fw, fb, mw, mb = p
            x = x + _attention(_layernorm(x, ln1w, ln1b), aw, ab, pw, pb)
            h = _layernorm(x, ln2w, ln2b)
            h = jax.nn.gelu(h @ fw + fb, approximate=False) @ mw + mb
            return x + h
        key = jax.random.key(seed)
        ks = jax.random.split(key, 6)
        s = 0.02
        return {'x': jax.random.normal(ks[0], (2, 256, E), jnp.float32), 'ln1_w': jnp.ones((L, E), jnp.float32), 'ln1_b': jnp.zeros((L, E), jnp.float32), 'attn_w': jax.random.normal(ks[1], (L, E, 3 * E), jnp.float32) * s, 'attn_b': jnp.zeros((L, 3 * E), jnp.float32), 'aproj_w': jax.random.normal(ks[2], (L, E, E), jnp.float32) * s, 'aproj_b': jnp.zeros((L, E), jnp.float32), 'ln2_w': jnp.ones((L, E), jnp.float32), 'ln2_b': jnp.zeros((L, E), jnp.float32), 'fc_w': jax.random.normal(ks[3], (L, E, 4 * E), jnp.float32) * s, 'fc_b': jnp.zeros((L, 4 * E), jnp.float32), 'mproj_w': jax.random.normal(ks[4], (L, 4 * E, E), jnp.float32) * s, 'mproj_b': jnp.zeros((L, E), jnp.float32)}
    _L1_attn_b_in = _L1_attn_b_setup()

    def _L1_ffn_setup():
        import jax, jax.numpy as jnp
        import numpy as np
        DIM = 128
        HIDDEN = 384
        SCALE = 1.0 / 127.0

        def _dequant(w_int, dtype):
            return w_int.astype(dtype) * jnp.asarray(SCALE, dtype)
        key = jax.random.key(seed)
        k_x, k_g, k_u, k_d = jax.random.split(key, 4)
        x = jax.random.normal(k_x, (4, 256, DIM), dtype=jnp.float32)
        w_gate = jax.random.randint(k_g, (HIDDEN, DIM), -127, 128, dtype=jnp.int32)
        w_up = jax.random.randint(k_u, (HIDDEN, DIM), -127, 128, dtype=jnp.int32)
        w_down = jax.random.randint(k_d, (DIM, HIDDEN), -127, 128, dtype=jnp.int32)
        return {'x': x, 'w_gate': w_gate, 'w_up': w_up, 'w_down': w_down}
    _L1_ffn_in = _L1_ffn_setup()
    _d = {'L0_attn_a_h': _L0_attn_a_in['h'], 'L0_attn_a_w_qc': _L0_attn_a_in['w_qc'], 'L0_attn_a_w_qup': _L0_attn_a_in['w_qup'], 'L0_attn_a_w_k': _L0_attn_a_in['w_k'], 'L0_attn_a_w_v': _L0_attn_a_in['w_v'], 'L0_attn_a_g_qnorm': _L0_attn_a_in['g_qnorm'], 'L0_attn_a_g_knorm': _L0_attn_a_in['g_knorm'], 'L0_attn_a_w_gate': _L0_attn_a_in['w_gate'], 'L0_attn_a_b_gate': _L0_attn_a_in['b_gate'], 'L0_attn_a_sink_logit': _L0_attn_a_in['sink_logit'], 'L0_attn_a_w_out_group': _L0_attn_a_in['w_out_group'], 'L0_attn_a_w_out': _L0_attn_a_in['w_out'], 'L0_attn_b_Wq': _L0_attn_b_in['Wq'], 'L0_attn_b_bq': _L0_attn_b_in['bq'], 'L0_attn_b_Wk': _L0_attn_b_in['Wk'], 'L0_attn_b_bk': _L0_attn_b_in['bk'], 'L0_attn_b_Wv': _L0_attn_b_in['Wv'], 'L0_attn_b_bv': _L0_attn_b_in['bv'], 'L0_attn_b_Wo': _L0_attn_b_in['Wo'], 'L0_attn_b_bo': _L0_attn_b_in['bo'], 'L0_ffn_gate_w': _L0_ffn_in['gate_w'], 'L0_ffn_w1': _L0_ffn_in['w1'], 'L0_ffn_w2': _L0_ffn_in['w2'], 'L0_ffn_w3': _L0_ffn_in['w3'], 'L1_attn_a_Wq': _L1_attn_a_in['Wq'], 'L1_attn_a_Wk': _L1_attn_a_in['Wk'], 'L1_attn_a_Wv': _L1_attn_a_in['Wv'], 'L1_attn_a_Wo': _L1_attn_a_in['Wo'], 'L1_attn_a_q_phase_angle': _L1_attn_a_in['q_phase_angle'], 'L1_attn_a_alibi_log_slopes': _L1_attn_a_in['alibi_log_slopes'], 'L1_attn_b_ln1_w': _L1_attn_b_in['ln1_w'], 'L1_attn_b_ln1_b': _L1_attn_b_in['ln1_b'], 'L1_attn_b_attn_w': _L1_attn_b_in['attn_w'], 'L1_attn_b_attn_b': _L1_attn_b_in['attn_b'], 'L1_attn_b_aproj_w': _L1_attn_b_in['aproj_w'], 'L1_attn_b_aproj_b': _L1_attn_b_in['aproj_b'], 'L1_attn_b_ln2_w': _L1_attn_b_in['ln2_w'], 'L1_attn_b_ln2_b': _L1_attn_b_in['ln2_b'], 'L1_attn_b_fc_w': _L1_attn_b_in['fc_w'], 'L1_attn_b_fc_b': _L1_attn_b_in['fc_b'], 'L1_attn_b_mproj_w': _L1_attn_b_in['mproj_w'], 'L1_attn_b_mproj_b': _L1_attn_b_in['mproj_b'], 'L1_ffn_w_gate': _L1_ffn_in['w_gate'], 'L1_ffn_w_up': _L1_ffn_in['w_up'], 'L1_ffn_w_down': _L1_ffn_in['w_down']}
    _x0 = _d['L0_attn_a_h']
    _d['L0_attn_a_h'] = jax.random.normal(jax.random.fold_in(jax.random.key(seed), 1), (16, 256, 128), dtype=_x0.dtype)
    del _x0
    return _d

def reference(L0_attn_a_h, L0_attn_a_w_qc, L0_attn_a_w_qup, L0_attn_a_w_k, L0_attn_a_w_v, L0_attn_a_g_qnorm, L0_attn_a_g_knorm, L0_attn_a_w_gate, L0_attn_a_b_gate, L0_attn_a_sink_logit, L0_attn_a_w_out_group, L0_attn_a_w_out, L0_attn_b_Wq, L0_attn_b_bq, L0_attn_b_Wk, L0_attn_b_bk, L0_attn_b_Wv, L0_attn_b_bv, L0_attn_b_Wo, L0_attn_b_bo, L0_ffn_gate_w, L0_ffn_w1, L0_ffn_w2, L0_ffn_w3, L1_attn_a_Wq, L1_attn_a_Wk, L1_attn_a_Wv, L1_attn_a_Wo, L1_attn_a_q_phase_angle, L1_attn_a_alibi_log_slopes, L1_attn_b_ln1_w, L1_attn_b_ln1_b, L1_attn_b_attn_w, L1_attn_b_attn_b, L1_attn_b_aproj_w, L1_attn_b_aproj_b, L1_attn_b_ln2_w, L1_attn_b_ln2_b, L1_attn_b_fc_w, L1_attn_b_fc_b, L1_attn_b_mproj_w, L1_attn_b_mproj_b, L1_ffn_w_gate, L1_ffn_w_up, L1_ffn_w_down):

    def _L0_attn_a_ref(h, w_qc, w_qup, w_k, w_v, g_qnorm, g_knorm, w_gate, b_gate, sink_logit, w_out_group, w_out):
        import jax, jax.numpy as jnp
        import numpy as np
        H, D, CR, SEL_K = (8, 64, 32, 16)
        ROPE_DIM, THETA, WINDOW, GROUPS = (32, 10000.0, 64, 2)
        INTER, HID, QC = (64, 128, 32)
        NEG = -1e+30

        def _rope_cache(t):
            half = ROPE_DIM // 2
            inv = 1.0 / THETA ** (jnp.arange(half, dtype=jnp.float32) * 2.0 / ROPE_DIM)
            ang = jnp.arange(t, dtype=jnp.float32)[:, None] * inv[None, :]
            return (jnp.cos(ang), jnp.sin(ang))

        def _apply_partial_rope(x, cos, sin):
            half = ROPE_DIM // 2
            x1, x2, rest = (x[..., :half], x[..., half:ROPE_DIM], x[..., ROPE_DIM:])
            return jnp.concatenate([x1 * cos - x2 * sin, x1 * sin + x2 * cos, rest], -1)

        def _rmsnorm(x, g, eps=1e-06):
            return x * jax.lax.rsqrt(jnp.mean(x * x, -1, keepdims=True) + eps) * g
        b, t, _ = h.shape
        cos, sin = _rope_cache(t)
        q = (h @ w_qc @ w_qup).reshape(b, t, H, D).transpose(0, 2, 1, 3)
        q = _rmsnorm(_apply_partial_rope(q, cos, sin), g_qnorm)
        k = _rmsnorm(_apply_partial_rope(h @ w_k, cos, sin), g_knorm)
        v = h @ w_v
        scale = 1.0 / np.sqrt(D).astype(np.float32)
        qpos = jnp.arange(t)
        sink = jnp.broadcast_to(sink_logit[None, :, None, None], (b, H, t, 1))
        nb = t // CR
        kc = k[:, :nb * CR].reshape(b, nb, CR, D).mean(2)
        vc = v[:, :nb * CR].reshape(b, nb, CR, D).mean(2)
        comp_valid = ((jnp.arange(nb) + 1) * CR - 1)[None, :] <= qpos[:, None]
        any_blk = comp_valid.any(-1, keepdims=True)
        safe = jnp.where(any_blk, comp_valid, True)
        sc_raw = jnp.einsum('bhqd,bnd->bhqn', q, kc) * scale
        pc = jax.nn.softmax(jnp.concatenate([jnp.where(safe, sc_raw, NEG), sink], -1), -1)
        comp_out = jnp.einsum('bhqn,bnd->bhqd', pc[..., :nb], vc)
        comp_out = jnp.where(any_blk[None, None], comp_out, 0.0)
        sel_sc = jnp.where(comp_valid, sc_raw, -jnp.inf)
        top_idx = jax.lax.top_k(sel_sc, min(SEL_K, nb))[1]
        sel_blocks = (top_idx[..., :, None] == jnp.arange(nb)).any(-2)
        block_of = jnp.minimum(qpos // CR, nb - 1)
        causal = qpos[:, None] >= qpos[None, :]
        in_range = qpos < nb * CR
        tok_sel = sel_blocks[..., block_of] & (causal & in_range[None, :])[None, None]
        scores_full = jnp.einsum('bhqd,bkd->bhqk', q, k) * scale
        ps = jax.nn.softmax(jnp.where(tok_sel, scores_full, NEG), -1)
        sel_out = jnp.einsum('bhqk,bkd->bhqd', ps, v)
        sw = causal & (qpos[:, None] - qpos[None, :] < WINDOW)
        pw = jax.nn.softmax(jnp.concatenate([jnp.where(sw[None, None], scores_full, NEG), sink], -1), -1)
        sw_out = jnp.einsum('bhqk,bkd->bhqd', pw[..., :t], v)
        g = jax.nn.sigmoid(q @ w_gate + b_gate)
        g = g / jnp.clip(g.sum(-1, keepdims=True), 1e-06)
        mixed = g[..., 0:1] * comp_out + g[..., 1:2] * sel_out + g[..., 2:3] * sw_out
        x = mixed.transpose(0, 2, 1, 3).reshape(b, t, GROUPS, H // GROUPS * D)
        y = jnp.einsum('btgf,gfi->btgi', x, w_out_group).reshape(b, t, GROUPS * INTER)
        return y @ w_out

    def _L0_attn_b_ref(x, Wq, bq, Wk, bk, Wv, bv, Wo, bo):
        import jax, jax.numpy as jnp
        import numpy as np
        D_IN, HEAD_DIM = (128, 128)
        B, S, D = x.shape
        Q = jnp.einsum('bsd,hd->bsh', x, Wq) + bq
        K = jnp.einsum('bsd,hd->bsh', x, Wk) + bk
        V = jnp.einsum('bsd,hd->bsh', x, Wv) + bv
        scores = jnp.einsum('bqh,bkh->bqk', Q, K)
        causal = jnp.tril(jnp.ones((S, S), dtype=bool))
        scores = jnp.where(causal, scores, -jnp.inf)
        scale = jnp.float32(HEAD_DIM) ** (-0.5)
        attn = jax.nn.softmax(scores * scale, axis=-1)
        out = jnp.einsum('bqk,bkh->bqh', attn, V)
        return jnp.einsum('bsh,dh->bsd', out, Wo) + bo

    def _L0_ffn_ref(x, gate_w, w1, w2, w3):
        import jax, jax.numpy as jnp
        import numpy as np
        TOP_K = 2
        bsz, seq, dim = x.shape
        xt = x.reshape(-1, dim)
        scores = jnp.einsum('td,ed->te', xt, gate_w)
        probs = jax.nn.softmax(scores, axis=-1)
        expert_weights, expert_indices = jax.lax.top_k(probs, TOP_K)
        expert_weights = expert_weights / expert_weights.sum(-1, keepdims=True)
        x1 = jax.nn.silu(jnp.einsum('ti,eoi->teo', xt, w1))
        x3 = jnp.einsum('ti,eoi->teo', xt, w3)
        expert_outs = jnp.einsum('teo,eio->tei', x1 * x3, w2)
        sel = jnp.take_along_axis(expert_outs, expert_indices[:, :, None], axis=1)
        out = jnp.einsum('tai,ta->ti', sel, expert_weights)
        return out.reshape(bsz, seq, dim)

    def _L1_attn_a_ref(x, Wq, Wk, Wv, Wo, q_phase_angle, alibi_log_slopes):
        import jax, jax.numpy as jnp
        import numpy as np
        B, T = (2, 256)
        TOK, POS = (64, 64)
        H, D, KVH = (16, 64, 4)
        b, t, _ = x.shape
        x_tok = x[:, :, :TOK]
        x_pos = x[:, :, TOK:]
        q = (x_pos @ Wq).reshape(b, t, H, D).transpose(0, 2, 1, 3)
        k = (x_pos @ Wk).reshape(b, t, KVH, D).transpose(0, 2, 1, 3)
        v = (x_tok @ Wv).reshape(b, t, KVH, D).transpose(0, 2, 1, 3)
        c = jnp.cos(q_phase_angle)[None, :, None, None]
        s = jnp.sin(q_phase_angle)[None, :, None, None]
        q2 = q.reshape(b, H, t, D // 2, 2)
        q0, q1 = (q2[..., 0], q2[..., 1])
        q = jnp.stack([q0 * c - q1 * s, q0 * s + q1 * c], axis=-1).reshape(b, H, t, D)
        rep = H // KVH
        k = jnp.repeat(k, rep, axis=1)
        v = jnp.repeat(v, rep, axis=1)
        att = jnp.einsum('bhqd,bhkd->bhqk', q, k) / np.float32(np.sqrt(D))
        pos = jnp.arange(t)
        rel = (pos[:, None] - pos[None, :]).astype(jnp.float32)
        att = att + jnp.exp(alibi_log_slopes)[None, :, None, None] * rel[None, None]
        mask = pos[:, None] >= pos[None, :]
        att = jnp.where(mask[None, None], att, -jnp.inf)
        m = jnp.max(att, axis=-1, keepdims=True)
        e = jnp.exp(att - m)
        att = e / (1.0 + jnp.sum(e, axis=-1, keepdims=True))
        out = jnp.einsum('bhqk,bhkd->bhqd', att, v)
        out = out.transpose(0, 2, 1, 3).reshape(b, t, H * D)
        return out @ Wo

    def _L1_attn_b_ref(x, ln1_w, ln1_b, attn_w, attn_b, aproj_w, aproj_b, ln2_w, ln2_b, fc_w, fc_b, mproj_w, mproj_b):
        import jax, jax.numpy as jnp
        import numpy as np
        L, E, H = (4, 128, 16)
        HD = E // H
        EPS_LN = 1e-05

        def _layernorm(x, w, b):
            m = jnp.mean(x, axis=-1, keepdims=True)
            v = jnp.mean((x - m) ** 2, axis=-1, keepdims=True)
            return (x - m) / jnp.sqrt(v + EPS_LN) * w + b

        def _to_quaternion(x):
            p1 = jnp.diff(x, axis=1, prepend=x[:, :1])
            p2 = jnp.roll(x, 1, axis=2)
            p3 = jnp.cos(x)
            return jnp.stack([x, p1, p2, p3], axis=-1)

        def _hamilton(a, b):
            a0, a1, a2, a3 = (a[..., 0], a[..., 1], a[..., 2], a[..., 3])
            b0, b1, b2, b3 = (b[..., 0], b[..., 1], b[..., 2], b[..., 3])
            return jnp.stack([a0 * b0 - a1 * b1 - a2 * b2 - a3 * b3, a0 * b1 + a1 * b0 + a2 * b3 - a3 * b2, a0 * b2 - a1 * b3 + a2 * b0 + a3 * b1, a0 * b3 + a1 * b2 - a2 * b1 + a3 * b0], axis=-1)

        def _spectral_filter(S):
            ks = jnp.fft.fftfreq(S).astype(jnp.float32)[:, None, None]
            kh = jnp.fft.fftfreq(H).astype(jnp.float32)[None, :, None]
            kd = jnp.fft.fftfreq(HD).astype(jnp.float32)[None, None, :]
            km = jnp.sqrt(ks ** 2 + kh ** 2 + kd ** 2 + 1e-10)
            f = jnp.exp(1j * jnp.arctan(jnp.log(km + 1e-10)))
            return f[None, :, :, :, None].astype(jnp.complex64)

        def _modulation(S):
            lam = jnp.arange(S, dtype=jnp.float32) / S
            t = jnp.arange(S, dtype=jnp.float32) * 0.1
            probe = jnp.sin(t + lam)
            phase = t - 2.0 * lam + 0.5 * lam ** 2
            return (probe * jnp.cos(phase))[None, :, None, None]

        def _attention(x, aw, ab, pw, pb):
            B, S, _ = x.shape
            qkv = (x @ aw + ab).reshape(B, S, H, 3 * HD)
            q, k, v = jnp.split(qkv, 3, axis=-1)
            qk = _hamilton(_to_quaternion(q), _to_quaternion(k))
            qkv_p = _hamilton(qk, _to_quaternion(v))
            f = jnp.fft.fftn(qkv_p.astype(jnp.complex64), axes=(-3, -2))
            out = jnp.fft.ifftn(f * _spectral_filter(S), axes=(-3, -2)).real
            a = out[..., 0] * (1.0 + 0.1 * _modulation(S))
            return a.reshape(B, S, E) @ pw + pb

        def _layer(x, p):
            ln1w, ln1b, aw, ab, pw, pb, ln2w, ln2b, fw, fb, mw, mb = p
            x = x + _attention(_layernorm(x, ln1w, ln1b), aw, ab, pw, pb)
            h = _layernorm(x, ln2w, ln2b)
            h = jax.nn.gelu(h @ fw + fb, approximate=False) @ mw + mb
            return x + h
        for i in range(L):
            x = _layer(x, (ln1_w[i], ln1_b[i], attn_w[i], attn_b[i], aproj_w[i], aproj_b[i], ln2_w[i], ln2_b[i], fc_w[i], fc_b[i], mproj_w[i], mproj_b[i]))
        return x

    def _L1_ffn_ref(x, w_gate, w_up, w_down):
        import jax, jax.numpy as jnp
        import numpy as np
        DIM = 128
        HIDDEN = 384
        SCALE = 1.0 / 127.0

        def _dequant(w_int, dtype):
            return w_int.astype(dtype) * jnp.asarray(SCALE, dtype)
        wg = _dequant(w_gate, x.dtype)
        wu = _dequant(w_up, x.dtype)
        wd = _dequant(w_down, x.dtype)
        gate = jnp.einsum('bsd,hd->bsh', x, wg)
        up = jnp.einsum('bsd,hd->bsh', x, wu)
        h = jax.nn.silu(gate) * up
        return jnp.einsum('bsh,dh->bsd', h, wd)
    x = L0_attn_a_h
    x = x + _L0_attn_a_ref(_layernorm(x, axis=-1), L0_attn_a_w_qc, L0_attn_a_w_qup, L0_attn_a_w_k, L0_attn_a_w_v, L0_attn_a_g_qnorm, L0_attn_a_g_knorm, L0_attn_a_w_gate, L0_attn_a_b_gate, L0_attn_a_sink_logit, L0_attn_a_w_out_group, L0_attn_a_w_out)
    x = x + _L0_ffn_ref(_layernorm(x, axis=-1), L0_ffn_gate_w, L0_ffn_w1, L0_ffn_w2, L0_ffn_w3)
    x = x + _L0_attn_b_ref(_layernorm(x, axis=-1), L0_attn_b_Wq, L0_attn_b_bq, L0_attn_b_Wk, L0_attn_b_bk, L0_attn_b_Wv, L0_attn_b_bv, L0_attn_b_Wo, L0_attn_b_bo)
    x = x + _L0_ffn_ref(_layernorm(x, axis=-1), L0_ffn_gate_w, L0_ffn_w1, L0_ffn_w2, L0_ffn_w3)
    x = x + _L1_attn_a_ref(_layernorm(x, axis=-1), L1_attn_a_Wq, L1_attn_a_Wk, L1_attn_a_Wv, L1_attn_a_Wo, L1_attn_a_q_phase_angle, L1_attn_a_alibi_log_slopes)
    x = x + _L1_ffn_ref(_layernorm(x, axis=-1), L1_ffn_w_gate, L1_ffn_w_up, L1_ffn_w_down)
    x = x + _L1_attn_b_ref(_layernorm(x, axis=-1), L1_attn_b_ln1_w, L1_attn_b_ln1_b, L1_attn_b_attn_w, L1_attn_b_attn_b, L1_attn_b_aproj_w, L1_attn_b_aproj_b, L1_attn_b_ln2_w, L1_attn_b_ln2_b, L1_attn_b_fc_w, L1_attn_b_fc_b, L1_attn_b_mproj_w, L1_attn_b_mproj_b)
    x = x + _L1_ffn_ref(_layernorm(x, axis=-1), L1_ffn_w_gate, L1_ffn_w_up, L1_ffn_w_down)
    return x

_drawn_inputs = setup_inputs


def setup_inputs(seed=0):
    import zlib

    import numpy as np

    out = dict(_drawn_inputs(seed))
    spreads = {'L0_attn_a_g_qnorm': (1.0, 0.6),
     'L0_attn_a_g_knorm': (1.0, 0.6),
     'L0_attn_a_b_gate': (0.0, 0.8),
     'L0_attn_b_bq': (0.0, 0.8),
     'L0_attn_b_bk': (0.0, 2.0),
     'L0_attn_b_bv': (0.0, 0.1),
     'L0_attn_b_bo': (0.0, 0.1),
     'L1_attn_a_alibi_log_slopes': (0.834032416343689, 0.2),
     'L1_attn_b_ln1_w': (1.0, 0.6),
     'L1_attn_b_ln1_b': (0.0, 0.8),
     'L1_attn_b_attn_b': (0.0, 0.8),
     'L1_attn_b_aproj_b': (0.0, 2.0),
     'L1_attn_b_ln2_w': (1.0, 0.6),
     'L1_attn_b_ln2_b': (0.0, 0.8),
     'L1_attn_b_fc_b': (0.0, 2.0),
     'L1_attn_b_mproj_b': (0.0, 2.0)}
    factors = {'L0_attn_a_w_gate': 4.671,
     'L0_attn_a_sink_logit': 8.0,
     'L0_attn_b_Wq': 8.0,
     'L0_attn_b_Wk': 8.0,
     'L1_attn_b_attn_w': 8.0,
     'L1_attn_b_aproj_w': 8.0,
     'L1_attn_b_fc_w': 8.0,
     'L1_attn_b_mproj_w': 8.0}
    for name, (base, spread) in spreads.items():
        noise = np.random.default_rng([zlib.crc32(name.encode()), seed]).standard_normal(out[name].shape)
        drawn = base * np.exp(spread * noise) if base else spread * noise
        out[name] = jnp.asarray(drawn.astype(out[name].dtype))
    for name, factor in factors.items():
        out[name] = (out[name] * factor).astype(out[name].dtype)
    return out
```

```python
import math
from contextlib import ExitStack

import numpy as np

import concourse.bass as bass
from concourse import mybir

ALU = mybir.AluOpType
ACT = mybir.ActivationFunctionType
AX_X = mybir.AxisListType.X
F32 = mybir.dt.float32
I32 = mybir.dt.int32

P = 128
D = 128
SEQ = 256
TOKENS = 16 * SEQ
TILES = TOKENS // P
CT = 4
CHUNKS = TILES // CT
CW = CT * P
SEQS = TOKENS // SEQ
ST = SEQ // P
BIG = 1e30
LN_EPS = 1e-5
ROUND = 1.5 * 2.0 ** 23
TURN_HIGH = 6.28125
TURN_LOW = 2 * math.pi - TURN_HIGH
HALF_TURN = 3.1415925


class Signal:

    def __init__(self, sem, per):
        self.sem, self.per = sem, per

    def start(self, eng):
        eng.sem_inc(self.sem, 2 * self.per)

    def at(self, chunk, n):
        return (chunk + 2) * self.per + n


class Phase(ExitStack):

    def __init__(self):
        super().__init__()
        self.used = []
        self.main = ExitStack()

    def main_block(self, nc):
        return self.main.enter_context(nc.Block())

    def semaphore(self, nc, name):
        self.used.append(self.enter_context(nc.semaphore(name)))
        return self.used[-1]

    def clear(self, nc):
        self.main.close()
        with nc.Block() as block:
            @block.gpsimd
            def _(pool):
                for s in self.used:
                    pool.sem_clear(s)


def in_pairs(eng, chunks, fronts, main):
    for front in fronts:
        front(0, 0)
    with eng.Fori(0, chunks // 2) as j:
        for u in range(2):
            c = j * 2 + u
            main(c, u, *[lambda c=c, u=u, front=front: front(c + 1, 1 - u) for front in fronts])


def in_threes(eng, chunks, a, b, body):
    a(0, 0)
    a(1, 1)
    b(0, 0)
    with eng.Fori(0, chunks // 2) as j:
        for u in range(2):
            body(j * 2 + u, u)


class Norm:

    def __init__(self, nc, ctx, name, x, ident, tiles, ps=None, bank_free=None, gain=None, shift=None):
        CT = self.tiles = tiles
        CW = CT * P

        def sb(n, shape):
            return ctx.enter_context(nc.sbuf_tensor(f"{name}_{n}", shape, F32))

        def signal(n, per):
            return Signal(ctx.semaphore(nc, f"{name}_{n}"), per)

        self.x, self.ident, self.gain, self.shift = x, ident, gain, shift
        self.stats = sb("stats", [P, CT, 6])
        self.mv = sb("mean_var", [P, CT, 2])
        self.veps = sb("var_eps", [P, CT])
        self.power = sb("power", [P, CT])
        self.rstd = sb("rstd", [P, CT])
        self.xn = sb("xn", [P, CT, D])
        self.xT = sb("xT", [P, 2, CW])
        self.bank_free = bank_free
        self.ps = ctx.enter_context(nc.psum_tensor(f"{name}_psT", [P, CW], F32)) if ps is None else ps[:, 0:CW]
        self.stat_done = signal("stat_done", CT)
        self.mv_done = signal("mv_done", CT)
        self.pow_done = signal("pow_done", 2)
        self.xn_done = signal("xn_done", CT)
        self.tr_done = signal("tr_done", 1)
        self.xT_done = signal("xT_done", 1)
        self.turns = ctx.semaphore(nc, f"{name}_turns")
        self.power_set = ctx.semaphore(nc, f"{name}_power_set")

    def start(self, nc, dve=None, pool=None, pe=None, act=None):
        if dve is not None:
            for s in (self.stat_done, self.mv_done, self.xn_done):
                s.start(dve)
        if pool is not None:
            self.pow_done.start(pool)
            pool.memset(self.power[:], -0.5).then_inc(self.power_set, 1)
            pool.wait_ge(self.power_set, 1)
        if pe is not None:
            self.tr_done.start(pe)
        if act is not None:
            self.xT_done.start(act)

    def on_vector(self, dve, c):
        CT = self.tiles
        for t in range(CT):
            dve.bn_stats(self.stats[:, t, :], self.x[:, c * CT + t, :]).then_inc(self.stat_done.sem, 1)
        dve.wait_ge(self.pow_done.sem, self.pow_done.at(c - 1, 1))
        dve.wait_ge(self.xn_done.sem, self.xn_done.at(c - 1, CT))
        dve.wait_ge(self.stat_done.sem, self.stat_done.at(c, CT))
        dve.sem_inc(self.turns, 1)
        for t in range(CT):
            dve.bn_aggr(self.mv[:, t, :], self.stats[:, t, :]).then_inc(self.mv_done.sem, 1)

    def on_pool(self, pool, c):
        CT = self.tiles
        pool.wait_ge(self.mv_done.sem, self.mv_done.at(c, CT))
        pool.sem_inc(self.turns, 1)
        pool.tensor_scalar(self.veps[:], self.mv[:, :, 1], LN_EPS, None, ALU.add).then_inc(self.pow_done.sem, 1)
        pool.wait_ge(self.pow_done.sem, self.pow_done.at(c, 1))
        pool.wait_ge(self.xn_done.sem, self.xn_done.at(c - 1, CT))
        pool.tensor_tensor(self.rstd[:], self.veps[:], self.power[:], ALU.pow).then_inc(self.pow_done.sem, 1)

    def on_vector_scale(self, dve, c):
        CT = self.tiles
        dve.wait_ge(self.mv_done.sem, self.mv_done.at(c, CT))
        dve.wait_ge(self.pow_done.sem, self.pow_done.at(c, 2))
        dve.wait_ge(self.tr_done.sem, self.tr_done.at(c - 1, 1))
        for t in range(CT):
            dve.tensor_scalar(self.xn[:, t, :], self.x[:, c * CT + t, :], self.mv[:, t, 0:1],
                              self.rstd[:, t:t + 1], ALU.subtract, ALU.mult).then_inc(self.xn_done.sem, 1)

    def on_tensor(self, pe, c):
        CT = self.tiles
        pe.wait_ge(self.xT_done.sem, self.xT_done.at(c - 1, 1))
        if self.bank_free is not None:
            pe.wait_ge(*self.bank_free(c))
        for t in range(CT):
            pe.wait_ge(self.xn_done.sem, self.xn_done.at(c, t + 1))
            last = pe.transpose(self.ps[:, t * P:(t + 1) * P], self.xn[:, t, :], self.ident[:])
        last.then_inc(self.tr_done.sem, 1)

    def on_scalar(self, act, c, u, xT_free):
        act.wait_ge(self.tr_done.sem, self.tr_done.at(c, 1))
        act.wait_ge(*xT_free)
        if self.gain is None:
            last = act.activation(self.xT[:, u, :], self.ps[:, :], ACT.Copy)
        else:
            last = act.activation(self.xT[:, u, :], self.ps[:, :], ACT.Identity,
                                  bias=self.shift, scale=self.gain)
        last.then_inc(self.xT_done.sem, 1)


def feed_forward(nc, name, x, ident, w1, w3, w2, experts, blocks, gate_w=None, order=None):
    units = experts * blocks
    with Phase() as ctx:
        def sb(n, shape):
            return ctx.enter_context(nc.sbuf_tensor(f"{name}_{n}", shape, F32))

        def ps(n, shape):
            return ctx.enter_context(nc.psum_tensor(f"{name}_{n}", shape, F32))

        def signal(n, per):
            return Signal(ctx.semaphore(nc, f"{name}_{n}"), per)

        norm = Norm(nc, ctx, name, x, ident, CT)
        ps_a = [ps(f"ps_a{i}", [P, CW]) for i in range(2)]
        ps_b = [ps(f"ps_b{i}", [P, CW]) for i in range(2)]
        ps_o = [ps(f"ps_o{i}", [P, CT, D]) for i in range(2)]
        silu = sb("silu", [P, 2, CW])
        hidden = sb("hidden", [P, 2, blocks, CW])
        up_done = signal("up_done", 2 * units)
        silu_done = signal("silu_done", units)
        hid_done = signal("hid_done", units)
        down_done = signal("down_done", experts)
        comb_done = signal("comb_done", CT * experts)
        if gate_w is not None:
            E = experts
            ps_g = ps("ps_g", [P, CT, E])
            score = sb("score", [P, CT, E])
            same = sb("same", [P, CT, E])
            place = sb("place", [P, CT, E])
            best = sb("best", [P, 2, CT, E])
            top = sb("top", [P, 2, CT])
            first = sb("first", [P, CT])
            gap = sb("gap", [P, CT])
            half = sb("half", [P, CT])
            share = sb("share", [P, 2, CT])
            gate = sb("gate", [P, 2, CT, E])
            GATE_STEPS = 18
            score_mm = signal("score_mm", 1)
            gate_step = signal("gate_step", GATE_STEPS)
            tanh_done = signal("tanh_done", 1)

        block = ctx.main_block(nc)

        @block.gpsimd
        def _(pool):
            norm.start(nc, pool=pool)
            in_pairs(pool, CHUNKS, [lambda c, u: norm.on_pool(pool, c)], lambda c, u, nxt: nxt())

        @block.tensor
        def _(pe):
            norm.start(nc, pe=pe)
            up_done.start(pe)
            down_done.start(pe)
            if gate_w is not None:
                score_mm.start(pe)

            def scores(c, u):
                pe.wait_ge(gate_step.sem, gate_step.at(c - 1, 1))
                for t in range(CT):
                    last = pe.matmul(ps_g[:, t, :], norm.xT[:, u, t * P:(t + 1) * P], gate_w[:],
                                     start=True, stop=True)
                last.then_inc(score_mm.sem, 1)

            def up(c, u, e):
                for b in range(blocks):
                    n = e * blocks + b
                    i = n % 2 if units % 2 == 0 else (u * units + n) % 2
                    pe.wait_ge(hid_done.sem, hid_done.at(c, n - 1))
                    pe.matmul(ps_a[i][:], w1[:, n * P:(n + 1) * P], norm.xT[:, u, :],
                              start=True, stop=True).then_inc(up_done.sem, 1)
                    pe.matmul(ps_b[i][:], w3[:, n * P:(n + 1) * P], norm.xT[:, u, :],
                              start=True, stop=True).then_inc(up_done.sem, 1)

            def down(c, u, e):
                g = (u * experts + e) % 2
                pe.wait_ge(hid_done.sem, hid_done.at(c, (e + 1) * blocks))
                pe.wait_ge(comb_done.sem, comb_done.at(c, CT * (e - 1)))
                for t in range(CT):
                    for b in range(blocks):
                        last = pe.matmul(ps_o[g][:, t, :], hidden[:, g, b, t * P:(t + 1) * P],
                                         w2[:, e * blocks + b, :], start=(b == 0), stop=(b == blocks - 1))
                last.then_inc(down_done.sem, 1)

            def main(c, u, nxt):
                pe.wait_ge(norm.xT_done.sem, norm.xT_done.at(c, 1))
                if gate_w is not None:
                    scores(c, u)
                for e in range(experts):
                    up(c, u, e)
                    if e == experts - 1:
                        nxt()
                    if e >= 1:
                        down(c, u, e - 1)
                down(c, u, experts - 1)

            in_pairs(pe, CHUNKS, [lambda c, u: norm.on_tensor(pe, c)], main)

        @block.scalar
        def _(act):
            norm.start(nc, act=act)
            silu_done.start(act)
            if gate_w is not None:
                tanh_done.start(act)

            def main(c, u, nxt):
                for e in range(experts):
                    for b in range(blocks):
                        n = e * blocks + b
                        i = n % 2 if units % 2 == 0 else (u * units + n) % 2
                        act.wait_ge(up_done.sem, up_done.at(c, 2 * n + 1))
                        act.wait_ge(hid_done.sem, hid_done.at(c, n - 1))
                        act.activation(silu[:, i, :], ps_a[i][:], ACT.Silu).then_inc(silu_done.sem, 1)
                        if gate_w is not None and n == 1:
                            act.wait_ge(gate_step.sem, gate_step.at(c, 13))
                            act.activation(half[:], gap[:], ACT.Tanh, scale=0.5).then_inc(tanh_done.sem, 1)
                nxt()

            in_pairs(act, CHUNKS, [lambda c, u: norm.on_scalar(
                act, c, u, (down_done.sem, down_done.at(c - 2, experts)))], main)

        @block.vector
        def _(dve):
            norm.start(nc, dve=dve)
            hid_done.start(dve)
            comb_done.start(dve)
            if gate_w is not None:
                gate_step.start(dve)

            def best_two(c, u):
                k = 0

                def step(ins):
                    nonlocal k
                    k += 1
                    ins.then_inc(gate_step.sem, 1)
                    dve.wait_ge(gate_step.sem, gate_step.at(c, k))

                def wide(a):
                    return a.unsqueeze(2).to_broadcast([P, CT, experts])

                dve.wait_ge(score_mm.sem, score_mm.at(c, 1))
                step(dve.tensor_copy(score[:], ps_g[:]))
                for r in range(2):
                    step(dve.tensor_reduce(top[:, r, :], score[:], AX_X, ALU.max))
                    step(dve.tensor_tensor(same[:], score[:], wide(top[:, r, :]), ALU.is_equal))
                    step(dve.tensor_tensor(place[:], same[:], order[:], ALU.mult))
                    step(dve.tensor_reduce(first[:], place[:], AX_X, ALU.max))
                    step(dve.tensor_tensor(best[:, r, :, :], place[:], wide(first[:]), ALU.is_equal))
                    if r == 0:
                        step(dve.scalar_tensor_tensor(score[:], best[:, 0, :, :], -1e30, score[:],
                                                      ALU.mult, ALU.add))
                step(dve.tensor_tensor(gap[:], top[:, 1, :], top[:, 0, :], ALU.subtract))
                assert k == 13
                dve.wait_ge(tanh_done.sem, tanh_done.at(c, 1))
                step(dve.tensor_scalar(share[:, 0, :], half[:], -0.5, 0.5, ALU.mult, ALU.add))
                step(dve.tensor_scalar(share[:, 1, :], half[:], 0.5, 0.5, ALU.mult, ALU.add))
                step(dve.tensor_tensor(best[:, 0, :, :], best[:, 0, :, :], wide(share[:, 0, :]), ALU.mult))
                step(dve.tensor_tensor(best[:, 1, :, :], best[:, 1, :, :], wide(share[:, 1, :]), ALU.mult))
                step(dve.tensor_tensor(gate[:, u, :, :], best[:, 0, :, :], best[:, 1, :, :], ALU.add))
                assert k == GATE_STEPS

            def unit(c, u, e, b):
                n = e * blocks + b
                i = n % 2 if units % 2 == 0 else (u * units + n) % 2
                g = (u * experts + e) % 2
                dve.wait_ge(silu_done.sem, silu_done.at(c, n + 1))
                dve.wait_ge(up_done.sem, up_done.at(c, 2 * n + 2))
                if b == 0:
                    dve.wait_ge(down_done.sem, down_done.at(c, e - 1))
                dve.tensor_tensor(hidden[:, g, b, :], silu[:, i, :], ps_b[i][:],
                                  ALU.mult).then_inc(hid_done.sem, 1)

            def combine(c, u, e):
                g = (u * experts + e) % 2
                dve.wait_ge(down_done.sem, down_done.at(c, e + 1))
                for t in range(CT):
                    rows = x[:, c * CT + t, :]
                    if e >= 1:
                        dve.wait_ge(comb_done.sem, comb_done.at(c, CT * (e - 1) + t + 1))
                    if gate_w is not None:
                        last = dve.scalar_tensor_tensor(rows, ps_o[g][:, t, :], gate[:, u, t, e:e + 1], rows,
                                                        ALU.mult, ALU.add)
                    else:
                        last = dve.tensor_tensor(rows, ps_o[g][:, t, :], rows, ALU.add)
                    last.then_inc(comb_done.sem, 1)

            def front(c, u):
                norm.on_vector(dve, c)
                norm.on_vector_scale(dve, c)

            def main(c, u, nxt):
                for e in range(experts):
                    for b in range(blocks):
                        unit(c, u, e, b)
                        if gate_w is not None and e == 0 and b == 1:
                            best_two(c, u)
                    if e == max(0, experts - 3):
                        nxt()
                    if e >= 1:
                        combine(c, u, e - 1)
                combine(c, u, experts - 1)

            in_pairs(dve, CHUNKS, [front], main)

        ctx.clear(nc)



class A0:
    H, HD, QC, CR = 8, 64, 32, 32
    NB = SEQ // CR
    WINDOW = 64
    W1 = P + WINDOW
    X = 16
    SINK, GATE = NB, NB + 1
    C = NB + 4


def mixed_attention(nc, x, ident, w):
    H, HD, NB, X, C = A0.H, A0.HD, A0.NB, A0.X, A0.C
    HP = H // 2
    with Phase() as ctx:
        def sb(n, shape):
            return ctx.enter_context(nc.sbuf_tensor(f"mix_{n}", shape, F32))

        def ps(n, shape):
            return ctx.enter_context(nc.psum_tensor(f"mix_{n}", shape, F32))

        def sem(n):
            return ctx.semaphore(nc, f"mix_{n}")

        def signal(n, per):
            return Signal(sem(n), per)

        ps_f = ps("ps_f", [P, 512])
        ps_q = ps("ps_q", [P, H, HD])
        ps_kv = ps("ps_kv", [P, 512])
        ps_s = [ps(f"ps_s{i}", [P, X + SEQ]) for i in range(2)]
        ps_t = [ps(f"ps_t{i}", [P, 512]) for i in range(2)]
        ps_o = ps("ps_o", [P, H, HD])

        qc_w = sb("qc_w", [A0.QC, D])
        qup_w = sb("qup_w", [A0.QC, H * HD])
        group_w = sb("group_w", [64, 2, 2 * P])
        out_w = sb("out_w", [64, 2, D])
        q_w = sb("q_w", [D, H * HD])
        kv_w = sb("kv_w", [D, 2 * HD])
        y_w = sb("y_w", [P, HP, D])
        gain_q = sb("gain_q", [P, 2, HD])
        gain_k = sb("gain_k", [P, 2, HD])
        gain_qk = sb("gain_qk", [P, 2, HD])
        gain_col = sb("gain_col", [P, 1])
        gate_w = sb("gate_w", [P, 3])
        gate_b = sb("gate_b", [P, 3])
        sink = sb("sink", [P, H])
        rope = sb("rope", [P, ST, 2, 32])
        causal = sb("causal", [P, P + SEQ])
        window = sb("window", [P, P + A0.W1])
        extra = sb("extra", [P, ST, H, C])
        any_block = sb("any_block", [P, ST])
        mean_w = sb("mean_w", [P, ST, H * NB])
        diagonal = sb("diagonal", [H * NB, H])

        qk = sb("qk", [P, ST, H + 1, HD])
        sq = sb("sq", [P, ST, H + 1, HD])
        ss = sb("ss", [P, ST, H + 1])
        ms = sb("ms", [P, ST, H + 1])
        rms = sb("rms", [P, ST, H + 1])
        half = sb("half", [P, ST, H + 1])
        rc = sb("rc", [P, H + 1, 32])
        rs = sb("rs", [P, H + 1, 32])
        kd = sb("kd", [P, ST, 2, HD])
        v = sb("v", [P, 2, ST, HD])
        vc = sb("vc", [H * NB, 2, H, HD])
        kc = sb("kc", [P, NB])
        kx = sb("kx", [P, 2, X + SEQ])
        qT = sb("qT", [P, 2, ST, HP, P])
        s_all = sb("s_all", [P, 2, SEQ])
        s_win = sb("s_win", [P, 2, A0.W1])
        low_all = sb("low_all", [P, ST, H])
        low_win = sb("low_win", [P, ST, H])
        p_all = sb("p_all", [P, ST, H, SEQ])
        p_win = sb("p_win", [P, ST, H, A0.W1])
        cg = sb("cg", [P, ST, H, C])
        low_c = sb("low_c", [P, H])
        e_c = sb("e_c", [P, H, NB + 1])
        e_sink = sb("e_sink", [P, H])
        sig = sb("sig", [P, H, 3])
        total = sb("total", [P, ST, 4, H])
        inverse = sb("inverse", [P, 4, H])
        ratio = sb("ratio", [P, 3, H])
        factor = sb("factor", [P, ST, 3, H])
        p_c = sb("p_c", [P, ST, H, NB])
        p_cT = sb("p_cT", [H * NB, P])
        pT = sb("pT", [P, 2, ST, P])
        o = sb("o", [P, H, HD])
        oT = sb("oT", [P, HP, P])

        loaded, made, multiplied, passed = sem("loaded"), sem("made"), sem("multiplied"), sem("passed")
        kv_mm = signal("kv_mm", 1)
        q_mm = signal("q_mm", ST)
        copied = signal("copied", 4 * ST)
        prepared = signal("prepared", 3 * ST + 3)
        turned = signal("turned", 6 * ST)
        front_mm = signal("front_mm", 4)
        front_ev = signal("front_ev", 3)
        norm = Norm(nc, ctx, "mix", x, ident, ST, ps=ps_f,
                    bank_free=lambda c: (front_ev.sem, front_ev.at(c - 1, 3)))
        U = ST * H
        s_mm = signal("s_mm", U)
        least = signal("least", 3 * U)
        exped = signal("exped", 2 * U)
        MIX = 13
        mixing = signal("mixing", MIX * ST)
        mix_exp = signal("mix_exp", 3 * ST)
        weighed = signal("weighed", 2 * U)
        R = H + 2
        p_tr = signal("p_tr", R * ST)
        p_ev = signal("p_ev", R * ST)
        o_mm = signal("o_mm", R * ST)
        o_ev = signal("o_ev", ST)
        added = signal("added", ST)

        pieces = [(qc_w, "a_qc"), (qup_w, "a_qup"), (group_w, "a_group"), (out_w, "a_out"), (kv_w, "a_kv"),
                  (gain_q, "a_gain_q"), (gain_k, "a_gain_k"), (gain_col, "a_gain_col"), (gate_w, "a_gate_w"),
                  (gate_b, "a_gate_b"), (sink, "a_sink"), (rope, "rope"), (causal, "causal"),
                  (window, "window"), (extra, "blocks"), (any_block, "any_block"), (mean_w, "mean_w"),
                  (diagonal, "diagonal")]

        with nc.Block() as block:
            @block.sync
            def _(sp):
                for to, of in pieces:
                    sp.dma_start(to[:], w[of]).then_inc(loaded, 16)

            @block.gpsimd
            def _(pool):
                pool.memset(half[:], -0.5)

            @block.tensor
            def _(pe):
                pe.wait_ge(loaded, 16 * len(pieces))
                pe.matmul(ps_q[:], qc_w[:], qup_w[:], start=True, stop=True).then_inc(multiplied, 1)
                for b in range(HP):
                    last = pe.matmul(ps_f[:, b * P:(b + 1) * P], group_w[:, b // 2, (b % 2) * P:(b % 2 + 1) * P],
                                     out_w[:, b // 2, :], start=True, stop=True)
                last.then_inc(multiplied, 1)

            @block.vector
            def _(dve):
                dve.wait_ge(loaded, 16 * len(pieces))
                dve.memset(kx[:], 0.0).then_inc(made, 1)
                dve.scalar_tensor_tensor(gain_qk[:], gain_q[:], -(HD ** -0.5), gain_k[:], ALU.mult, ALU.mult)
                dve.wait_ge(made, 1)
                for u in range(2):
                    dve.tensor_scalar(kx[:, u, A0.GATE:A0.GATE + 3], gate_w[:], gain_col[:, 0:1], -1.0,
                                      ALU.mult, ALU.mult)
                for t in range(ST):
                    dve.tensor_scalar(extra[:, t, :, A0.SINK], sink[:], -1.0, None, ALU.mult)
                    dve.tensor_scalar(extra[:, t, :, A0.GATE:A0.GATE + 3],
                                      gate_b[:].unsqueeze(1).to_broadcast([P, H, 3]), -1.0, None, ALU.mult)
                dve.wait_ge(multiplied, 2)
                dve.tensor_copy(q_w[:], ps_q[:].rearrange("p h d -> p (h d)"))
                dve.tensor_copy(y_w[:].rearrange("p b d -> p (b d)"), ps_f[:])

        block = ctx.main_block(nc)

        def keys(t):
            return (t + 1) * P

        def reach(t):
            return (0, P, 0) if t == 0 else (P - A0.WINDOW, A0.W1, P)

        @block.gpsimd
        def _(pool):
            norm.start(nc, pool=pool)
            turned.start(pool)

            def project(c, u):
                for t in range(ST):
                    pool.wait_ge(prepared.sem, prepared.at(c, t + 1))
                    pool.sem_inc(norm.turns, 1)
                    pool.tensor_scalar(ms[:, t, :], ss[:, t, :], 1.0 / HD, 1e-6, ALU.mult,
                                       ALU.add).then_inc(turned.sem, 1)
                    pool.wait_ge(turned.sem, turned.at(c, 2 * t + 1))
                    pool.tensor_tensor(rms[:, t, :], ms[:, t, :], half[:, t, :], ALU.pow).then_inc(turned.sem, 1)
                for t in range(ST):
                    k = 2 * ST + 4 * t
                    head = qk[:, t, :, 0:32]
                    pool.wait_ge(prepared.sem, prepared.at(c, ST + t + 1))
                    for n, to in enumerate((rc, rs)):
                        pool.tensor_tensor(to[:], head, rope[:, t, n:n + 1, :].to_broadcast([P, H + 1, 32]),
                                           ALU.mult).then_inc(turned.sem, 1)
                    pool.wait_ge(turned.sem, turned.at(c, k + 2))
                    pool.tensor_tensor(qk[:, t, :, 0:16], rc[:, :, 0:16], rs[:, :, 16:32],
                                       ALU.subtract).then_inc(turned.sem, 1)
                    pool.tensor_tensor(qk[:, t, :, 16:32], rc[:, :, 16:32], rs[:, :, 0:16],
                                       ALU.add).then_inc(turned.sem, 1)
                    pool.wait_ge(turned.sem, turned.at(c, k + 4))

            def main(c, u, f1, f2, f3):
                f1()
                f2()
                f3()

            in_pairs(pool, SEQS, [lambda c, u: norm.on_pool(pool, c), project, lambda c, u: None], main)

        @block.tensor
        def _(pe):
            norm.start(nc, pe=pe)
            for s in (kv_mm, q_mm, front_mm, s_mm, p_tr, o_mm):
                s.start(pe)

            def project(c, u):
                pe.wait_ge(norm.xT_done.sem, norm.xT_done.at(c, 1))
                pe.wait_ge(prepared.sem, prepared.at(c - 1, 3 * ST + 1))
                for t in range(ST):
                    last = pe.matmul(ps_kv[:, t * P:(t + 1) * P], norm.xT[:, u, t * P:(t + 1) * P], kv_w[:],
                                     start=True, stop=True)
                last.then_inc(kv_mm.sem, 1)
                for t in range(ST):
                    pe.wait_ge(copied.sem, copied.at(c, 4 * (t - 1) + 3))
                    pe.matmul(ps_q[:], norm.xT[:, u, t * P:(t + 1) * P], q_w[:], start=True,
                              stop=True).then_inc(q_mm.sem, 1)
                pe.wait_ge(copied.sem, copied.at(c, 4 * (ST - 1) + 2))
                for t in range(ST):
                    last = pe.matmul(ps_kv[0:H * NB, 2 * P:2 * P + HD], mean_w[:, t, :], v[:, u, t, :],
                                     start=(t == 0), stop=(t == ST - 1))
                last.then_inc(front_mm.sem, 1)

            def turn(c, u):
                pe.wait_ge(prepared.sem, prepared.at(c, 3 * ST))
                pe.wait_ge(front_ev.sem, front_ev.at(c - 1, 3))
                for t in range(ST):
                    last = pe.transpose(ps_f[:, t * P:(t + 1) * P], kd[:, t, :, :].rearrange("p a d -> p (a d)"),
                                        ident[:])
                last.then_inc(front_mm.sem, 1)
                for t in range(ST):
                    pe.wait_ge(turned.sem, turned.at(c, 2 * ST + 4 * (t + 1)))
                    pe.wait_ge(front_ev.sem, front_ev.at(c, t + 1))
                    for b in range(HP):
                        last = pe.transpose(ps_f[:, b * P:(b + 1) * P],
                                            qk[:, t, 2 * b:2 * b + 2, :].rearrange("p a d -> p (a d)"), ident[:])
                    last.then_inc(front_mm.sem, 1)

            def scores(c, u, t):
                if t == 0:
                    pe.wait_ge(front_ev.sem, front_ev.at(c, 3))
                    pe.wait_ge(prepared.sem, prepared.at(c, 3 * ST + 3))
                for h in range(H):
                    n = t * H + h
                    r = slice(64 * (h % 2), 64 * (h % 2) + 64)
                    pe.wait_ge(least.sem, least.at(c, 3 * (n - 1)))
                    pe.matmul(ps_s[n % 2][:, 0:X + keys(t)], qT[r, u, t, h // 2, :], kx[r, u, 0:X + keys(t)],
                              start=True, stop=True).then_inc(s_mm.sem, 1)

            def values(c, u, t):
                r = R * t
                bank = ps_t
                pe.wait_ge(mixing.sem, mixing.at(c, MIX * (t + 1)))
                pe.wait_ge(p_ev.sem, p_ev.at(c, r - 1))
                pe.sem_inc(passed, 1)
                pe.transpose(bank[r % 2][0:H * NB, 0:P], p_c[:, t, :, :].rearrange("p h n -> p (h n)"),
                             ident[:]).then_inc(p_tr.sem, 1)

                def turn_p(h):
                    i = r + 1 + h
                    pe.wait_ge(weighed.sem, weighed.at(c, 2 * H * t + min(2 * h + 3, 2 * H)))
                    pe.wait_ge(p_ev.sem, p_ev.at(c, i - 1))
                    for b in range(t + 1):
                        last = pe.transpose(bank[i % 2][:, b * P:(b + 1) * P], p_all[:, t, h, b * P:(b + 1) * P],
                                            ident[:])
                    last.then_inc(p_tr.sem, 1)

                turn_p(0)
                pe.wait_ge(p_ev.sem, p_ev.at(c, r + 1))
                pe.wait_ge(added.sem, added.at(c, t))
                pe.matmul(ps_o[:], p_cT[:], vc[:, u, :, :], start=True, stop=False,
                          skip_group_check=True).then_inc(o_mm.sem, 1)
                for h in range(H):
                    if h + 1 < H:
                        turn_p(h + 1)
                    pe.wait_ge(p_ev.sem, p_ev.at(c, r + 2 + h))
                    for b in range(t + 1):
                        last = pe.matmul(ps_o[:, h, :], pT[:, h % 2, b, :], v[:, u, b, :], start=False,
                                         stop=(h == H - 1 and b == t), skip_group_check=True)
                    last.then_inc(o_mm.sem, 1)
                pe.wait_ge(o_ev.sem, o_ev.at(c, t + 1))
                i = r + 1 + H
                pe.wait_ge(p_ev.sem, p_ev.at(c, i - 1))
                for b in range(HP):
                    last = pe.transpose(bank[i % 2][:, b * P:(b + 1) * P],
                                        o[:, 2 * b:2 * b + 2, :].rearrange("p a d -> p (a d)"), ident[:])
                last.then_inc(p_tr.sem, 1)
                pe.wait_ge(p_ev.sem, p_ev.at(c, i + 1))
                for b in range(HP):
                    last = pe.matmul(ps_o[:, 0:2, :], oT[:, b, :], y_w[:, b, :], start=(b == 0),
                                     stop=(b == HP - 1), skip_group_check=True)
                last.then_inc(o_mm.sem, 1)

            def main(c, u, f1, f2, f3):
                scores(c, u, 0)
                f1()
                scores(c, u, 1)
                f2()
                values(c, u, 0)
                f3()
                values(c, u, 1)

            in_pairs(pe, SEQS, [lambda c, u: norm.on_tensor(pe, c), project, turn], main)

        @block.scalar
        def _(act):
            norm.start(nc, act=act)
            for s in (copied, front_ev, exped, mix_exp, p_ev, o_ev):
                s.start(act)

            def project(c, u):
                act.wait_ge(front_mm.sem, front_mm.at(c - 1, 4))
                act.wait_ge(kv_mm.sem, kv_mm.at(c, 1))
                for t in range(ST):
                    act.activation(qk[:, t, H, :], ps_kv[:, t * P:t * P + HD], ACT.Copy).then_inc(copied.sem, 1)
                    act.activation(v[:, u, t, :], ps_kv[:, t * P + HD:(t + 1) * P], ACT.Copy).then_inc(copied.sem, 1)
                    act.wait_ge(q_mm.sem, q_mm.at(c, t + 1))
                    act.activation(qk[:, t, 0:H, :], ps_q[:], ACT.Copy).then_inc(copied.sem, 1)
                    act.wait_ge(copied.sem, copied.at(c, 4 * t + 3))
                    act.activation(sq[:, t, :, :], qk[:, t, :, :], ACT.Square).then_inc(copied.sem, 1)

            def turn(c, u):
                act.wait_ge(front_mm.sem, front_mm.at(c, 2))
                act.activation(kx[:, u, X:X + SEQ], ps_f[:, 0:SEQ], ACT.Copy).then_inc(front_ev.sem, 1)
                for t in range(ST):
                    act.wait_ge(front_mm.sem, front_mm.at(c, 3 + t))
                    act.activation(qT[:, u, t, :, :], ps_f[:].rearrange("p (b q) -> p b q", b=HP),
                                   ACT.Copy).then_inc(front_ev.sem, 1)

            def scores(c, u, t):
                for h in range(H):
                    n = t * H + h
                    act.wait_ge(least.sem, least.at(c, 3 * n + 2))
                    act.activation(p_all[:, t, h, 0:keys(t)], s_all[:, n % 2, 0:keys(t)], ACT.Exp,
                                   bias=low_all[:, t, h:h + 1], scale=-1.0,
                                   accum_out=total[:, t, 2, h:h + 1]).then_inc(exped.sem, 1)
                    act.wait_ge(least.sem, least.at(c, 3 * n + 3))
                    act.activation(p_win[:, t, h, 0:reach(t)[1]], s_win[:, n % 2, 0:reach(t)[1]], ACT.Exp,
                                   bias=low_win[:, t, h:h + 1], scale=-1.0,
                                   accum_out=total[:, t, 3, h:h + 1]).then_inc(exped.sem, 1)

            def mix(c, u, t):
                act.wait_ge(mixing.sem, mixing.at(c, MIX * t + 2))
                act.activation(e_c[:], e_c[:], ACT.Exp).then_inc(mix_exp.sem, 1)
                act.activation(sig[:], cg[:, t, :, A0.GATE:A0.GATE + 3], ACT.Exp).then_inc(mix_exp.sem, 1)
                act.wait_ge(mixing.sem, mixing.at(c, MIX * t + 3))
                act.activation(e_sink[:], e_sink[:], ACT.Exp).then_inc(mix_exp.sem, 1)

            def values(c, u, t):
                bank = ps_t
                r = R * t
                act.wait_ge(p_tr.sem, p_tr.at(c, r + 1))
                act.activation(p_cT[:], bank[r % 2][0:H * NB, 0:P], ACT.Copy).then_inc(p_ev.sem, 1)
                for h in range(H):
                    i = r + 1 + h
                    act.wait_ge(p_tr.sem, p_tr.at(c, i + 1))
                    act.wait_ge(o_mm.sem, o_mm.at(c, i - 1))
                    act.activation(pT[:, h % 2, 0:t + 1, :],
                                   bank[i % 2][:, 0:keys(t)].rearrange("p (b q) -> p b q", b=t + 1),
                                   ACT.Copy).then_inc(p_ev.sem, 1)
                act.wait_ge(o_mm.sem, o_mm.at(c, r + 1 + H))
                act.activation(o[:], ps_o[:], ACT.Copy).then_inc(o_ev.sem, 1)
                i = r + 1 + H
                act.wait_ge(p_tr.sem, p_tr.at(c, i + 1))
                act.activation(oT[:], bank[i % 2][:].rearrange("p (b q) -> p b q", b=HP),
                               ACT.Copy).then_inc(p_ev.sem, 1)

            def main(c, u, f1, f2, f3):
                scores(c, u, 0)
                mix(c, u, 0)
                f1()
                scores(c, u, 1)
                f2()
                mix(c, u, 1)
                values(c, u, 0)
                f3()
                values(c, u, 1)

            in_pairs(act, SEQS, [lambda c, u: norm.on_scalar(act, c, u, (q_mm.sem, q_mm.at(c - 2, ST))),
                                 project, turn], main)

        @block.vector
        def _(dve):
            norm.start(nc, dve=dve)
            for s in (prepared, least, mixing, weighed, added):
                s.start(dve)

            def first(c, u):
                norm.on_vector(dve, c)
                norm.on_vector_scale(dve, c)

            def project(c, u):
                for t in range(ST):
                    dve.wait_ge(copied.sem, copied.at(c, 4 * t + 4))
                    dve.tensor_reduce(ss[:, t, :], sq[:, t, :, :], AX_X, ALU.add).then_inc(prepared.sem, 1)
                for t in range(ST):
                    dve.wait_ge(turned.sem, turned.at(c, 2 * t + 2))
                    dve.tensor_tensor(qk[:, t, :, :], qk[:, t, :, :],
                                      rms[:, t, :].unsqueeze(2).to_broadcast([P, H + 1, HD]),
                                      ALU.mult).then_inc(prepared.sem, 1)
                for t in range(ST):
                    dve.wait_ge(turned.sem, turned.at(c, 2 * ST + 4 * (t + 1)))
                    dve.tensor_tensor(kd[:, t, :, :], qk[:, t, H:H + 1, :].to_broadcast([P, 2, HD]), gain_qk[:],
                                      ALU.mult).then_inc(prepared.sem, 1)
                dve.wait_ge(front_mm.sem, front_mm.at(c, 1))
                dve.tensor_tensor(vc[:, u, :, :],
                                  ps_kv[0:H * NB, 2 * P:2 * P + HD].unsqueeze(1).to_broadcast([H * NB, H, HD]),
                                  diagonal[:].unsqueeze(2).to_broadcast([H * NB, H, HD]),
                                  ALU.mult).then_inc(prepared.sem, 1)

            def turn(c, u):
                dve.wait_ge(front_ev.sem, front_ev.at(c, 1))
                dve.tensor_reduce(kc[:], kx[:, u, X:X + SEQ].rearrange("p (n k) -> p n k", n=NB), AX_X,
                                  ALU.add).then_inc(prepared.sem, 1)
                dve.wait_ge(prepared.sem, prepared.at(c, 3 * ST + 2))
                dve.tensor_scalar(kx[:, u, 0:NB], kc[:], 1.0 / A0.CR, None, ALU.mult).then_inc(prepared.sem, 1)

            def scores(c, u, t):
                k0, count, col = reach(t)
                for h in range(H):
                    n = t * H + h
                    dve.wait_ge(s_mm.sem, s_mm.at(c, n + 1))
                    dve.wait_ge(exped.sem, exped.at(c, 2 * (n - 1)))
                    dve.tensor_tensor(cg[:, t, h, :], ps_s[n % 2][:, 0:C], extra[:, t, h, :],
                                      ALU.add).then_inc(least.sem, 1)
                    dve.tensor_tensor_reduce(s_all[:, n % 2, 0:keys(t)], ps_s[n % 2][:, X:X + keys(t)],
                                             causal[:, P * t:P * t + keys(t)], 1.0, 3.0e38, ALU.add, ALU.min,
                                             low_all[:, t, h:h + 1]).then_inc(least.sem, 1)
                    dve.tensor_tensor_reduce(s_win[:, n % 2, 0:count], ps_s[n % 2][:, X + k0:X + k0 + count],
                                             window[:, col:col + count], 1.0, extra[:, t, h, A0.SINK:A0.SINK + 1],
                                             ALU.add, ALU.min, low_win[:, t, h:h + 1]).then_inc(least.sem, 1)

            def mix(c, u, t):
                k = MIX * t

                def step(ins):
                    nonlocal k
                    k += 1
                    ins.then_inc(mixing.sem, 1)

                def settled():
                    dve.wait_ge(mixing.sem, mixing.at(c, k))

                def wide(a, n):
                    return a.unsqueeze(2).to_broadcast([P, H, n])

                dve.wait_ge(least.sem, least.at(c, 3 * H * (t + 1)))
                step(dve.tensor_reduce(low_c[:], cg[:, t, :, 0:NB + 1], AX_X, ALU.min))
                settled()
                step(dve.tensor_tensor(e_c[:], wide(low_c[:], NB + 1), cg[:, t, :, 0:NB + 1], ALU.subtract))
                step(dve.tensor_tensor(e_sink[:], sink[:], low_win[:, t, :], ALU.add))
                dve.wait_ge(mix_exp.sem, mix_exp.at(c, 3 * t + 2))
                step(dve.tensor_scalar(sig[:], sig[:], 1.0, None, ALU.add))
                settled()
                step(dve.reciprocal(sig[:], sig[:]))
                settled()
                step(dve.tensor_reduce(total[:, t, 0, :], sig[:], AX_X, ALU.add))
                settled()
                step(dve.tensor_scalar(total[:, t, 0, :], total[:, t, 0, :], 1e-6, None, ALU.max))
                step(dve.tensor_reduce(total[:, t, 1, :], e_c[:], AX_X, ALU.add))
                dve.wait_ge(mix_exp.sem, mix_exp.at(c, 3 * t + 3))
                dve.wait_ge(exped.sem, exped.at(c, 2 * H * (t + 1)))
                step(dve.tensor_tensor(total[:, t, 3, :], total[:, t, 3, :], e_sink[:], ALU.add))
                settled()
                step(dve.reciprocal(inverse[:], total[:, t, :, :]))
                settled()
                step(dve.tensor_tensor(ratio[:], inverse[:, 1:4, :], inverse[:, 0:1, :].to_broadcast([P, 3, H]),
                                       ALU.mult))
                settled()
                step(dve.tensor_tensor(factor[:, t, :, :], ratio[:], sig[:].rearrange("p h g -> p g h"), ALU.mult))
                settled()
                step(dve.scalar_tensor_tensor(p_c[:, t, :, :], e_c[:, :, 0:NB], any_block[:, t:t + 1],
                                              wide(factor[:, t, 0, :], NB), ALU.mult, ALU.mult))
                assert k == MIX * (t + 1)

            def weigh(c, u, t):
                k0, count, _ = reach(t)

                def window_part(h):
                    dve.wait_ge(weighed.sem, weighed.at(c, 2 * H * t + max(2 * h, 1)))
                    dve.scalar_tensor_tensor(p_all[:, t, h, k0:k0 + count], p_win[:, t, h, 0:count],
                                             factor[:, t, 2, h:h + 1], p_all[:, t, h, k0:k0 + count],
                                             ALU.mult, ALU.add).then_inc(weighed.sem, 1)

                dve.wait_ge(mixing.sem, mixing.at(c, MIX * (t + 1)))
                for h in range(H):
                    dve.tensor_scalar(p_all[:, t, h, 0:keys(t)], p_all[:, t, h, 0:keys(t)],
                                      factor[:, t, 1, h:h + 1], None, ALU.mult).then_inc(weighed.sem, 1)
                    if h >= 1:
                        window_part(h - 1)
                    if t == 1 and h == H // 2:
                        finish(c, u, 0)
                window_part(H - 1)

            def finish(c, u, t):
                dve.wait_ge(o_mm.sem, o_mm.at(c, R * (t + 1)))
                rows = x[:, c * ST + t, :]
                dve.tensor_tensor(rows, ps_o[:, 0:2, :].rearrange("p a d -> p (a d)"), rows,
                                  ALU.add).then_inc(added.sem, 1)

            def main(c, u, f1, f2, f3):
                scores(c, u, 0)
                mix(c, u, 0)
                f1()
                scores(c, u, 1)
                f2()
                mix(c, u, 1)
                weigh(c, u, 0)
                f3()
                weigh(c, u, 1)
                finish(c, u, 1)

            in_pairs(dve, SEQS, [first, project, turn], main)

        ctx.clear(nc)


def single_attention(nc, x, ident, w):
    HD = D
    with Phase() as ctx:
        def sb(n, shape):
            return ctx.enter_context(nc.sbuf_tensor(f"one_{n}", shape, F32))

        def ps(n, shape):
            return ctx.enter_context(nc.psum_tensor(f"one_{n}", shape, F32))

        def sem(n):
            return ctx.semaphore(nc, f"one_{n}")

        def signal(n, per):
            return Signal(sem(n), per)

        ps_qk = ps("ps_qk", [P, 2, SEQ])
        ps_v = ps("ps_v", [P, ST, HD])
        ps_s = [ps(f"ps_s{i}", [P, SEQ]) for i in range(2)]
        ps_t = ps("ps_t", [P, SEQ])
        ps_o = ps("ps_o", [P, P])
        ps_y = ps("ps_y", [P, D])
        norm = Norm(nc, ctx, "one", x, ident, ST)

        wq, wk, wv, wo = (sb(n, [P, P]) for n in ("wq", "wk", "wv", "wo"))
        bq, bk = sb("bq", [P, 1]), sb("bk", [P, 1])
        bv, bo = sb("bv", [P, HD]), sb("bo", [P, D])
        causal = sb("causal", [P, P + SEQ])
        qT = sb("qT", [P, 2, SEQ])
        kT = sb("kT", [P, 2, SEQ])
        v = sb("v", [P, 2, ST, HD])
        s_all = sb("s_all", [P, ST, SEQ])
        low = sb("low", [P, ST])
        e = sb("e", [P, ST, SEQ])
        total = sb("total", [P, ST])
        inverse = sb("inverse", [P, ST])
        eT = sb("eT", [P, ST, P])
        oT = sb("oT", [P, P])
        loaded = sem("loaded")
        proj_mm = signal("proj_mm", 2)
        biased = signal("biased", 2 + ST)
        s_mm = signal("s_mm", ST)
        least = signal("least", ST)
        exped = signal("exped", ST)
        inverted = signal("inverted", ST)
        e_tr = signal("e_tr", ST)
        e_ev = signal("e_ev", ST)
        o_mm = signal("o_mm", ST)
        o_ev = signal("o_ev", ST)
        y_mm = signal("y_mm", ST)
        added = signal("added", 2 * ST)
        pieces = [(wq, "b_wq"), (wk, "b_wk"), (wv, "b_wv"), (wo, "b_wo"), (bq, "b_bq"), (bk, "b_bk"),
                  (bv, "b_bv"), (bo, "b_bo"), (causal, "causal")]

        with nc.Block() as block:
            @block.sync
            def _(sp):
                for to, of in pieces:
                    sp.dma_start(to[:], w[of]).then_inc(loaded, 16)
                sp.wait_ge(loaded, 16 * len(pieces))

        block = ctx.main_block(nc)

        @block.gpsimd
        def _(pool):
            norm.start(nc, pool=pool)
            in_pairs(pool, SEQS, [lambda c, u: norm.on_pool(pool, c)], lambda c, u, f: f())

        @block.tensor
        def _(pe):
            norm.start(nc, pe=pe)
            for s in (proj_mm, s_mm, e_tr, o_mm, y_mm):
                s.start(pe)

            def project(c, u):
                pe.wait_ge(norm.xT_done.sem, norm.xT_done.at(c, 1))
                pe.wait_ge(biased.sem, biased.at(c - 1, 2 + ST))
                pe.matmul(ps_qk[:, 0, :], wq[:], norm.xT[:, u, :], start=True, stop=True)
                pe.matmul(ps_qk[:, 1, :], wk[:], norm.xT[:, u, :], start=True, stop=True).then_inc(proj_mm.sem, 1)
                for t in range(ST):
                    last = pe.matmul(ps_v[:, t, :], norm.xT[:, u, t * P:(t + 1) * P], wv[:], start=True, stop=True)
                last.then_inc(proj_mm.sem, 1)

            def main(c, u, first, second):
                pe.wait_ge(biased.sem, biased.at(c, 2 + ST))
                for t in range(ST):
                    pe.wait_ge(least.sem, least.at(c - 1, t + 1))
                    pe.matmul(ps_s[t][:, 0:(t + 1) * P], qT[:, u, t * P:(t + 1) * P], kT[:, u, 0:(t + 1) * P],
                              start=True, stop=True).then_inc(s_mm.sem, 1)
                first()
                second()
                for t in range(ST):
                    pe.wait_ge(exped.sem, exped.at(c, t + 1))
                    pe.wait_ge(e_ev.sem, e_ev.at(c, t))
                    for b in range(t + 1):
                        last = pe.transpose(ps_t[:, b * P:(b + 1) * P], e[:, t, b * P:(b + 1) * P], ident[:])
                    last.then_inc(e_tr.sem, 1)
                    pe.wait_ge(e_ev.sem, e_ev.at(c, t + 1))
                    pe.wait_ge(o_ev.sem, o_ev.at(c, t))
                    for b in range(t + 1):
                        last = pe.matmul(ps_o[:], v[:, u, b, :], eT[:, b, :], start=(b == 0), stop=(b == t))
                    last.then_inc(o_mm.sem, 1)
                    pe.wait_ge(o_ev.sem, o_ev.at(c, t + 1))
                    pe.wait_ge(added.sem, added.at(c, 2 * t))
                    pe.matmul(ps_y[:], oT[:], wo[:], start=True, stop=True).then_inc(y_mm.sem, 1)

            in_pairs(pe, SEQS, [lambda c, u: norm.on_tensor(pe, c), project], main)

        @block.scalar
        def _(act):
            norm.start(nc, act=act)
            for s in (exped, e_ev, o_ev):
                s.start(act)

            def main(c, u, first):
                for t in range(ST):
                    act.wait_ge(least.sem, least.at(c, t + 1))
                    act.activation(e[:, t, 0:(t + 1) * P], s_all[:, t, 0:(t + 1) * P], ACT.Exp, bias=low[:, t:t + 1],
                                   scale=-1.0, accum_out=total[:, t:t + 1]).then_inc(exped.sem, 1)
                first()
                for t in range(ST):
                    act.wait_ge(e_tr.sem, e_tr.at(c, t + 1))
                    act.activation(eT[:, 0:t + 1, :], ps_t[:, 0:(t + 1) * P].rearrange("p (b q) -> p b q", b=t + 1),
                                   ACT.Copy).then_inc(e_ev.sem, 1)
                    act.wait_ge(o_mm.sem, o_mm.at(c, t + 1))
                    act.activation(oT[:], ps_o[:], ACT.Copy).then_inc(o_ev.sem, 1)

            in_pairs(act, SEQS, [lambda c, u: norm.on_scalar(act, c, u, (proj_mm.sem, proj_mm.at(c - 2, 2)))], main)

        @block.vector
        def _(dve):
            norm.start(nc, dve=dve)
            for s in (biased, least, inverted, added):
                s.start(dve)

            def first(c, u):
                norm.on_vector(dve, c)
                norm.on_vector_scale(dve, c)

            def project(c, u):
                dve.wait_ge(proj_mm.sem, proj_mm.at(c, 1))
                dve.tensor_scalar(qT[:, u, :], ps_qk[:, 0, :], bq[:, 0:1], -(float(HD) ** -0.5), ALU.add,
                                  ALU.mult).then_inc(biased.sem, 1)
                dve.tensor_scalar(kT[:, u, :], ps_qk[:, 1, :], bk[:, 0:1], None, ALU.add).then_inc(biased.sem, 1)
                dve.wait_ge(proj_mm.sem, proj_mm.at(c, 2))
                for t in range(ST):
                    dve.tensor_tensor(v[:, u, t, :], ps_v[:, t, :], bv[:], ALU.add).then_inc(biased.sem, 1)

            def main(c, u, f1, f2):
                for t in range(ST):
                    dve.wait_ge(s_mm.sem, s_mm.at(c, t + 1))
                    dve.sem_inc(norm.turns, 1)
                    dve.tensor_tensor_reduce(s_all[:, t, 0:(t + 1) * P], ps_s[t][:, 0:(t + 1) * P],
                                             causal[:, P * t:P * t + (t + 1) * P], 1.0, 3.0e38, ALU.add, ALU.min,
                                             low[:, t:t + 1]).then_inc(least.sem, 1)
                f1()
                f2()
                for t in range(ST):
                    dve.tensor_tensor(x[:, c * ST + t, :], x[:, c * ST + t, :], bo[:], ALU.add).then_inc(added.sem, 1)
                    dve.wait_ge(exped.sem, exped.at(c, t + 1))
                    dve.reciprocal(inverse[:, t:t + 1], total[:, t:t + 1]).then_inc(inverted.sem, 1)
                    dve.wait_ge(y_mm.sem, y_mm.at(c, t + 1))
                    dve.wait_ge(inverted.sem, inverted.at(c, t + 1))
                    dve.wait_ge(added.sem, added.at(c, 2 * t + 1))
                    dve.scalar_tensor_tensor(x[:, c * ST + t, :], ps_y[:], inverse[:, t:t + 1], x[:, c * ST + t, :],
                                             ALU.mult, ALU.add).then_inc(added.sem, 1)

            in_pairs(dve, SEQS, [first, project], main)

        ctx.clear(nc)


class G1:
    H, HD, KVH = 16, 64, 4
    HP = H // 2
    IN = 64
    REP = H // KVH
    OH = 8


def grouped_attention(nc, x, ident, w):
    H, HD, KVH, HP, IN, REP, OH = G1.H, G1.HD, G1.KVH, G1.HP, G1.IN, G1.REP, G1.OH
    F = 3 + HP // 2
    with Phase() as ctx:
        def sb(n, shape):
            return ctx.enter_context(nc.sbuf_tensor(f"grp_{n}", shape, F32))

        def ps(n, shape):
            return ctx.enter_context(nc.psum_tensor(f"grp_{n}", shape, F32))

        def sem(n):
            return ctx.semaphore(nc, f"grp_{n}")

        def signal(n, per):
            return Signal(sem(n), per)

        ps_f = ps("ps_f", [P, 512])
        ps_s = [ps(f"ps_s{i}", [P, SEQ]) for i in range(2)]
        ps_t = [ps(f"ps_t{i}", [P, 512]) for i in range(2)]
        ps_o = ps("ps_o", [P, OH, HD])
        ps_y = ps("ps_y", [P, D])
        norm = Norm(nc, ctx, "grp", x, ident, ST)

        wq_in = sb("wq_in", [P, H, HD // 2, 2])
        wq = sb("wq", [P, H * HD])
        turn_a = sb("turn_a", [P, H, HD // 2])
        turn_b = sb("turn_b", [P, H, HD // 2])
        wk = sb("wk", [P, KVH, 2, HD])
        wv = sb("wv", [P, KVH * HD])
        wo = sb("wo", [P, HP, D])
        phase = sb("phase", [P, H])
        wave = sb("wave", [P, 2, H])
        steps = sb("steps", [P, 2, H])
        slope = sb("slope", [P, H])
        keys_at = sb("keys_at", [P, P + SEQ])
        causal = sb("causal", [P, P + SEQ])
        table = sb("table", [P, H, P + SEQ])

        kT = sb("kT", [P, 2, KVH, SEQ])
        v = sb("v", [P, 2, ST, KVH * HD])
        qT = sb("qT", [P, 2, HP, SEQ])
        s_all = sb("s_all", [P, 2, SEQ])
        low = sb("low", [P, ST, H])
        e = sb("e", [P, ST, H, SEQ])
        total = sb("total", [P, ST, H])
        bottom = sb("bottom", [P, ST, H])
        inverse = sb("inverse", [P, ST, H])
        eT = sb("eT", [P, 2, ST, P])
        o = sb("o", [P, OH, HD])
        oT = sb("oT", [P, OH // 2, P])

        loaded, waved, rotated, sloped, passed = (sem(n) for n in ("loaded", "waved", "rotated", "sloped", "passed"))
        front_mm = signal("front_mm", F)
        front_ev = signal("front_ev", F)
        U = ST * H
        s_mm = signal("s_mm", U)
        least = signal("least", U)
        exped = signal("exped", U)
        inverted = signal("inverted", 2 * ST)
        e_tr = signal("e_tr", U)
        e_ev = signal("e_ev", U)
        o_mm = signal("o_mm", U)
        HALVES = ST * H // OH
        o_ev = signal("o_ev", HALVES)
        o_tr = signal("o_tr", HALVES)
        oT_ev = signal("oT_ev", HALVES)
        y_mm = signal("y_mm", HALVES)
        added = signal("added", ST)
        pieces = [(wq_in[IN:P, :, :, :], w["c_wq"]), (wk[IN:P, :, :, :], w["c_wk"]), (wv[0:IN, :], w["c_wv"]),
                  (wo[:], w["c_wo"]), (phase[:], w["c_phase"]), (slope[:], w["c_slope"]),
                  (keys_at[:], w["keys_at"]), (causal[:], w["causal"])]

        with nc.Block() as block:
            @block.sync
            def _(sp):
                for to, of in pieces:
                    sp.dma_start(to, of).then_inc(loaded, 16)

            @block.scalar
            def _(act):
                act.wait_ge(loaded, 16 * len(pieces))
                act.activation(slope[:], slope[:], ACT.Exp).then_inc(sloped, 1)
                act.wait_ge(waved, 7)
                act.activation(wave[:], wave[:], ACT.Sin).then_inc(sloped, 1)

            @block.vector
            def _(dve):
                def step(ins, n):
                    ins.then_inc(waved, 1)
                    dve.wait_ge(waved, n)

                dve.wait_ge(loaded, 16 * len(pieces))
                step(dve.tensor_scalar(wave[:, 0, :], phase[:], 1.0, math.pi / 2, ALU.mult, ALU.add), 1)
                step(dve.tensor_copy(wave[:, 1, :], phase[:]), 2)
                step(dve.tensor_scalar(steps[:], wave[:], 1 / (2 * math.pi), ROUND, ALU.mult, ALU.add), 3)
                step(dve.tensor_scalar(steps[:], steps[:], ROUND, None, ALU.subtract), 4)
                step(dve.scalar_tensor_tensor(wave[:], steps[:], -TURN_HIGH, wave[:], ALU.mult, ALU.add), 5)
                step(dve.scalar_tensor_tensor(wave[:], steps[:], -TURN_LOW, wave[:], ALU.mult, ALU.add), 6)
                step(dve.tensor_scalar(wave[:], wave[:], HALF_TURN, -HALF_TURN, ALU.min, ALU.max), 7)
                dve.wait_ge(sloped, 2)
                step(dve.tensor_scalar(wave[:], wave[:], -(float(HD) ** -0.5), None, ALU.mult), 8)
                even, odd = wq_in[IN:P, :, :, 0], wq_in[IN:P, :, :, 1]
                to = wq[IN:P, :].rearrange("p (h d a) -> p h d a", h=H, a=2)
                cos, sin = (wave[IN:P, n, :].unsqueeze(2).to_broadcast([IN, H, HD // 2]) for n in range(2))
                a, b = turn_a[IN:P, :, :], turn_b[IN:P, :, :]
                step(dve.tensor_tensor(a, even, cos, ALU.mult), 9)
                step(dve.tensor_tensor(b, odd, sin, ALU.mult), 10)
                step(dve.tensor_tensor(to[:, :, :, 0], a, b, ALU.subtract), 11)
                step(dve.tensor_tensor(a, even, sin, ALU.mult), 12)
                step(dve.tensor_tensor(b, odd, cos, ALU.mult), 13)
                step(dve.tensor_tensor(to[:, :, :, 1], a, b, ALU.add), 14)
                for h in range(H):
                    dve.scalar_tensor_tensor(table[:, h, :], keys_at[:], slope[:, h:h + 1], causal[:],
                                             ALU.mult, ALU.add)

        block = ctx.main_block(nc)

        def keys(t):
            return (t + 1) * P

        @block.gpsimd
        def _(pool):
            norm.start(nc, pool=pool)
            in_pairs(pool, SEQS, [lambda c, u: norm.on_pool(pool, c)], lambda c, u, f: f())

        @block.tensor
        def _(pe):
            norm.start(nc, pe=pe)
            for s in (front_mm, s_mm, e_tr, o_mm, o_tr, y_mm):
                s.start(pe)

            def project(c, u):
                pe.wait_ge(norm.xT_done.sem, norm.xT_done.at(c, 1))
                for n in range(F):
                    pe.wait_ge(front_ev.sem, front_ev.at(c, n))
                    for i in range(2):
                        half = ps_f[:, i * SEQ:(i + 1) * SEQ]
                        if n < 2:
                            last = pe.matmul(half, wk[IN:P, 2 * n + i, :, :].rearrange("p a d -> p (a d)"),
                                             norm.xT[IN:P, u, :], start=True, stop=True)
                        elif n == 2:
                            last = pe.matmul(half, norm.xT[0:IN, u, i * P:(i + 1) * P], wv[0:IN, :],
                                             start=True, stop=True)
                        else:
                            b = 2 * (n - 3) + i
                            last = pe.matmul(half, wq[IN:P, b * P:(b + 1) * P], norm.xT[IN:P, u, :],
                                             start=True, stop=True)
                    last.then_inc(front_mm.sem, 1)

            def scores(c, u, t):
                if t == 0:
                    pe.wait_ge(front_ev.sem, front_ev.at(c, F))
                for h in range(H):
                    n = t * H + h
                    r = slice(64 * (h % 2), 64 * (h % 2) + 64)
                    pe.wait_ge(least.sem, least.at(c, n - 1))
                    pe.matmul(ps_s[n % 2][:, 0:keys(t)], qT[r, u, h // 2, t * P:(t + 1) * P],
                              kT[r, u, h // REP, 0:keys(t)], start=True, stop=True).then_inc(s_mm.sem, 1)

            def values(c, u, t):
                def turn_e(h):
                    n = t * H + h
                    if h == 0:
                        pe.wait_ge(exped.sem, exped.at(c, H * (t + 1)))
                    pe.wait_ge(e_ev.sem, e_ev.at(c, n - 1))
                    for b in range(t + 1):
                        last = pe.transpose(ps_t[n % 2][:, b * P:(b + 1) * P], e[:, t, h, b * P:(b + 1) * P],
                                            ident[:])
                    last.then_inc(e_tr.sem, 1)

                turn_e(0)
                for h in range(H):
                    if h + 1 < H:
                        turn_e(h + 1)
                    n = t * H + h
                    m = n // OH
                    pe.wait_ge(e_ev.sem, e_ev.at(c, n + 1))
                    if h % OH == 0:
                        pe.wait_ge(o_ev.sem, o_ev.at(c, m))
                    for b in range(t + 1):
                        g = h // REP
                        last = pe.matmul(ps_o[:, h % OH, :], eT[:, n % 2, b, :], v[:, u, b, g * HD:(g + 1) * HD],
                                         start=(b == 0), stop=(b == t))
                    last.then_inc(o_mm.sem, 1)
                    if h % OH == OH - 1:
                        pe.wait_ge(o_ev.sem, o_ev.at(c, m + 1))
                        pe.wait_ge(oT_ev.sem, oT_ev.at(c, m))
                        pe.wait_ge(front_ev.sem, front_ev.at(c + (1 if t else 0), F))
                        for b in range(OH // 2):
                            last = pe.transpose(ps_f[:, b * P:(b + 1) * P],
                                                o[:, 2 * b:2 * b + 2, :].rearrange("p a d -> p (a d)"), ident[:])
                        last.then_inc(o_tr.sem, 1)
                        pe.wait_ge(oT_ev.sem, oT_ev.at(c, m + 1))
                        if h < OH:
                            pe.wait_ge(added.sem, added.at(c, t))
                        for b in range(OH // 2):
                            last = pe.matmul(ps_y[:], oT[:, b, :], wo[:, h // OH * (OH // 2) + b, :],
                                             start=(h < OH and b == 0), stop=(h > OH and b == OH // 2 - 1))
                        last.then_inc(y_mm.sem, 1)

            def main(c, u, f1, f2):
                scores(c, u, 0)
                f1()
                scores(c, u, 1)
                values(c, u, 0)
                f2()
                values(c, u, 1)

            in_pairs(pe, SEQS, [lambda c, u: norm.on_tensor(pe, c), project], main)

        @block.scalar
        def _(act):
            norm.start(nc, act=act)
            for s in (exped, e_ev):
                s.start(act)

            def scores(c, u, t):
                for h in range(H):
                    n = t * H + h
                    act.wait_ge(least.sem, least.at(c, n + 1))
                    act.activation(e[:, t, h, 0:keys(t)], s_all[:, n % 2, 0:keys(t)], ACT.Exp,
                                   bias=low[:, t, h:h + 1], scale=-1.0,
                                   accum_out=total[:, t, h:h + 1]).then_inc(exped.sem, 1)

            def values(c, u, t):
                for h in range(H):
                    n = t * H + h
                    act.wait_ge(e_tr.sem, e_tr.at(c, n + 1))
                    act.wait_ge(o_mm.sem, o_mm.at(c, n - 1))
                    act.activation(eT[:, n % 2, 0:t + 1, :],
                                   ps_t[n % 2][:, 0:keys(t)].rearrange("p (b q) -> p b q", b=t + 1),
                                   ACT.Copy).then_inc(e_ev.sem, 1)

            def main(c, u, f1):
                scores(c, u, 0)
                f1()
                scores(c, u, 1)
                values(c, u, 0)
                values(c, u, 1)

            in_pairs(act, SEQS, [lambda c, u: norm.on_scalar(act, c, u, (front_mm.sem, front_mm.at(c - 2, F)))],
                     main)

        @block.vector
        def _(dve):
            norm.start(nc, dve=dve)
            for s in (front_ev, least, inverted, o_ev, oT_ev, added):
                s.start(dve)

            def first(c, u):
                norm.on_vector(dve, c)
                norm.on_vector_scale(dve, c)

            def project(c, u):
                for n in range(F):
                    if n < 2:
                        to = kT[:, u, 2 * n:2 * n + 2, :]
                    elif n == 2:
                        to = v[:, u, :, :]
                    else:
                        to = qT[:, u, 2 * (n - 3):2 * (n - 3) + 2, :]
                    dve.wait_ge(front_mm.sem, front_mm.at(c, n + 1))
                    dve.tensor_copy(to.rearrange("p a k -> p (a k)"), ps_f[:]).then_inc(front_ev.sem, 1)

            def scores(c, u, t):
                for h in range(H):
                    n = t * H + h
                    dve.wait_ge(s_mm.sem, s_mm.at(c, n + 1))
                    dve.wait_ge(exped.sem, exped.at(c, n - 1))
                    dve.sem_inc(norm.turns, 1)
                    dve.tensor_tensor_reduce(s_all[:, n % 2, 0:keys(t)], ps_s[n % 2][:, 0:keys(t)],
                                             table[:, h, P * t:P * t + keys(t)], 1.0, 3.0e38, ALU.add, ALU.min,
                                             low[:, t, h:h + 1]).then_inc(least.sem, 1)

            def values(c, u, t):
                dve.wait_ge(exped.sem, exped.at(c, H * (t + 1)))
                dve.sem_inc(norm.turns, 1)
                dve.tensor_scalar(bottom[:, t, :], total[:, t, :], 1.0, None, ALU.add).then_inc(inverted.sem, 1)
                dve.wait_ge(inverted.sem, inverted.at(c, 2 * t + 1))
                dve.reciprocal(inverse[:, t, :], bottom[:, t, :]).then_inc(inverted.sem, 1)
                dve.wait_ge(inverted.sem, inverted.at(c, 2 * t + 2))
                for i in range(H // OH):
                    m = t * (H // OH) + i
                    dve.wait_ge(o_mm.sem, o_mm.at(c, (m + 1) * OH))
                    if m:
                        dve.wait_ge(o_tr.sem, o_tr.at(c, m))
                    dve.tensor_tensor(o[:], ps_o[:],
                                      inverse[:, t, i * OH:(i + 1) * OH].unsqueeze(2).to_broadcast([P, OH, HD]),
                                      ALU.mult).then_inc(o_ev.sem, 1)
                    dve.wait_ge(o_tr.sem, o_tr.at(c, m + 1))
                    dve.wait_ge(y_mm.sem, y_mm.at(c, m))
                    dve.tensor_copy(oT[:].rearrange("p b q -> p (b q)"), ps_f[:]).then_inc(oT_ev.sem, 1)
                dve.wait_ge(y_mm.sem, y_mm.at(c, (H // OH) * (t + 1)))
                dve.tensor_tensor(x[:, c * ST + t, :], ps_y[:], x[:, c * ST + t, :], ALU.add).then_inc(added.sem, 1)

            def main(c, u, f1, f2):
                scores(c, u, 0)
                f1()
                scores(c, u, 1)
                values(c, u, 0)
                f2()
                values(c, u, 1)

            in_pairs(dve, SEQS, [first, project], main)

        ctx.clear(nc)


class H1:
    LAYERS, H, HD = 4, 16, 8
    WRAP = D + HD
    HB = 4 * D // P


def spectral_layers(nc, rows_x, ident, w):
    HD, WRAP, HB = H1.HD, H1.WRAP, H1.HB
    with Phase() as ctx:
        def sb(n, shape):
            return ctx.enter_context(nc.sbuf_tensor(f"spec_{n}", shape, F32))

        def ps(n, shape):
            return ctx.enter_context(nc.psum_tensor(f"spec_{n}", shape, F32))

        def sem(n):
            return ctx.semaphore(nc, f"spec_{n}")

        def signal(n, per):
            return Signal(sem(n), per)

        ps_n = ps("ps_n", [P, SEQ])
        ps_x = ps("ps_x", [P, 3, WRAP])
        ps_d = ps("ps_d", [P, 3, D])
        ps_w = ps("ps_w", [P, SEQ])
        ps_z = ps("ps_z", [P, SEQ])
        ps_y = ps("ps_y", [P, ST, D])
        ps_h = [ps(f"ps_h{i}", [P, 2, SEQ]) for i in range(2)]

        x = sb("y", [P, TILES + CT, D])
        ln = sb("ln", [P, 4])
        qkv_w = sb("qkv_w", [P, 3, WRAP])
        qkv_b = sb("qkv_b", [P, 3, WRAP])
        proj_w = sb("proj_w", [P, D])
        head_proj = sb("head_proj", [P, D])
        proj_b = sb("proj_b", [P, D])
        fc_w = sb("fc_w", [P, 4 * D])
        fc_b = sb("fc_b", [P, HB])
        mp_w = sb("mp_w", [P, HB, D])
        mp_b = sb("mp_b", [P, D])
        hartley = sb("hartley", [P, P])
        filt = sb("filt", [P, SEQ])
        quarter = sb("quarter", [P, 1])

        dT = sb("dT", [P, 2, SEQ])
        rows = sb("rows", [P, 2, ST, 3, WRAP])
        diff = sb("diff", [P, 2, ST, 3, D])
        cosine = sb("cosine", [P, 2, ST, 3, D])
        turns_of = sb("turns_of", [P, ST, 3, D])
        whole = sb("whole", [P, ST, 3, D])
        part = sb("part", [P, 8, ST, D])
        comp = sb("comp", [P, 4, ST, D])
        product = sb("product", [P, ST, D])
        wT = sb("wT", [P, SEQ])
        z = sb("z", [P, SEQ])
        hT = sb("hT", [P, HB, SEQ])

        tables = sem("tables")
        zeroed, loaded, made = sem("zeroed"), sem("loaded"), sem("made")
        norm_a = Norm(nc, ctx, "spec_a", x, ident, ST, ps=ps_n, gain=ln[:, 0:1], shift=ln[:, 1:2])
        norm_c = Norm(nc, ctx, "spec_c", x, ident, ST, ps=ps_n, gain=ln[:, 2:3], shift=ln[:, 3:4])
        norm_a.bank_free = lambda c: (norm_c.xT_done.sem, norm_c.xT_done.at(c - 2, 1))
        norm_c.bank_free = lambda c: (norm_a.xT_done.sem, norm_a.xT_done.at(c + 1, 1))
        diffed = signal("diffed", 1)
        xd_mm = signal("xd_mm", 2 * ST)
        d_ev = signal("d_ev", ST)
        x_ev = signal("x_ev", ST)
        scaled = signal("scaled", 2)
        parted = signal("parted", 1)
        cosined = signal("cosined", 2)
        HAM = 35
        hamilton = signal("hamilton", HAM)
        w_mm = signal("w_mm", 1)
        w_ev = signal("w_ev", 1)
        z_mm = signal("z_mm", 1)
        filtered = signal("filtered", 1)
        y_mm = signal("y_mm", 1)
        m_mm = signal("m_mm", 1)
        bias_a = signal("bias_a", 1)
        bias_c = signal("bias_c", 1)
        y_add = signal("y_add", 1)
        m_add = signal("m_add", 1)
        h_mm = signal("h_mm", 2)
        h_ev = signal("h_ev", HB)

        row_stats, row_mv, row_rstd = sem("row_stats"), sem("row_mv"), sem("row_rstd")
        stats = sb("stats", [P, TILES, 6])
        mean_var = sb("mean_var", [P, TILES, 2])
        veps = sb("veps", [P, TILES])
        power = sb("power", [P, TILES])
        rstd = sb("rstd", [P, TILES])
        fixed = [(hartley[:], w["hartley"]), (filt[:], w["filter"])]
        with nc.Block() as block:
            @block.sync
            def _(sp):
                for to, of in fixed:
                    sp.dma_start(to, of).then_inc(tables, 16)
                sp.wait_ge(tables, 16 * len(fixed))

            @block.vector
            def _(dve):
                dve.memset(quarter[:], math.pi / 2)
                dve.memset(dT[:], 0.0)
                dve.memset(x[:, TILES:TILES + CT, :], 0.0)
                for t in range(TILES):
                    dve.bn_stats(stats[:, t, :], rows_x[:, t, :]).then_inc(row_stats, 1)
                for t in range(TILES):
                    dve.wait_ge(row_stats, t + 1)
                    dve.bn_aggr(mean_var[:, t, :], stats[:, t, :]).then_inc(row_mv, 1)
                dve.wait_ge(row_rstd, 3)
                for t in range(TILES):
                    dve.tensor_scalar(x[:, t, :], rows_x[:, t, :], mean_var[:, t, 0:1], rstd[:, t:t + 1],
                                      ALU.subtract, ALU.mult)

            @block.gpsimd
            def _(pool):
                pool.memset(power[:], -0.5).then_inc(row_rstd, 1)
                pool.wait_ge(row_mv, TILES)
                pool.tensor_scalar(veps[:], mean_var[:, :, 1], LN_EPS, None, ALU.add).then_inc(row_rstd, 1)
                pool.wait_ge(row_rstd, 2)
                pool.tensor_tensor(rstd[:], veps[:], power[:], ALU.pow).then_inc(row_rstd, 1)

        with nc.Fori(0, H1.LAYERS) as layer:
            layer_w = [(ln, "d_ln"), (qkv_w, "d_qkv_w"), (qkv_b, "d_qkv_b"), (proj_w, "d_proj_w"),
                       (proj_b, "d_proj_b"), (fc_w, "d_fc_w"), (fc_b, "d_fc_b"), (mp_w, "d_mp_w"), (mp_b, "d_mp_b")]
            with nc.Block() as block:
                @block.sync
                def _(sp):
                    for to, of in layer_w:
                        sp.dma_start(to[:], w[of][layer]).then_inc(loaded, 16)
                    sp.wait_ge(loaded, 16 * len(layer_w))

                @block.tensor
                def _(pe):
                    pe.wait_ge(loaded, 16 * len(layer_w))
                    pe.matmul(ps_y[:, 0, :], hartley[:], proj_w[:], start=True, stop=True).then_inc(made, 1)

                @block.vector
                def _(dve):
                    dve.wait_ge(made, 1)
                    dve.tensor_copy(head_proj[:], ps_y[:, 0, :])

            with nc.Block() as block:
                @block.gpsimd
                def _(pool):
                    norm_a.start(nc, pool=pool)
                    norm_c.start(nc, pool=pool)
                    diffed.start(pool)

                    def a(c, u):
                        norm_a.on_pool(pool, c)
                        pool.wait_ge(norm_a.xT_done.sem, norm_a.xT_done.at(c, 1))
                        pool.wait_ge(xd_mm.sem, xd_mm.at(c - 2, 2 * ST))
                        pool.tensor_tensor(dT[:, u, 1:SEQ], norm_a.xT[:, u, 1:SEQ], norm_a.xT[:, u, 0:SEQ - 1],
                                           ALU.subtract).then_inc(diffed.sem, 1)

                    def body(c, u):
                        norm_c.on_pool(pool, c)
                        a(c + 2, u)

                    in_threes(pool, SEQS, a, lambda c, u: None, body)

                @block.tensor
                def _(pe):
                    norm_a.start(nc, pe=pe)
                    norm_c.start(nc, pe=pe)
                    for s in (xd_mm, w_mm, z_mm, y_mm, m_mm, h_mm):
                        s.start(pe)

                    def a1(c, u):
                        norm_a.on_tensor(pe, c)

                    def a2(c, u):
                        pe.wait_ge(norm_a.xT_done.sem, norm_a.xT_done.at(c, 1))
                        for t in range(ST):
                            pe.wait_ge(x_ev.sem, x_ev.at(c, t))
                            pe.matmul(ps_x[:], norm_a.xT[:, u, t * P:(t + 1) * P], qkv_w[:], start=True,
                                      stop=True).then_inc(xd_mm.sem, 1)
                            pe.wait_ge(diffed.sem, diffed.at(c, 1))
                            pe.wait_ge(d_ev.sem, d_ev.at(c, t))
                            pe.matmul(ps_d[:], dT[:, u, t * P:(t + 1) * P], qkv_w[:, :, HD:WRAP], start=True,
                                      stop=True).then_inc(xd_mm.sem, 1)

                    def b1(c):
                        pe.wait_ge(hamilton.sem, hamilton.at(c, HAM))
                        pe.wait_ge(w_ev.sem, w_ev.at(c - 1, 1))
                        for t in range(ST):
                            last = pe.transpose(ps_w[:, t * P:(t + 1) * P], product[:, t, :], ident[:])
                        last.then_inc(w_mm.sem, 1)

                    def b2(c):
                        pe.wait_ge(w_ev.sem, w_ev.at(c, 1))
                        pe.wait_ge(filtered.sem, filtered.at(c - 1, 1))
                        pe.matmul(ps_z[:], hartley[:], wT[:], start=True, stop=True).then_inc(z_mm.sem, 1)

                    def b4(c):
                        pe.wait_ge(filtered.sem, filtered.at(c, 1))
                        pe.wait_ge(m_add.sem, m_add.at(c - 1, 1))
                        for t in range(ST):
                            last = pe.matmul(ps_y[:, t, :], z[:, t * P:(t + 1) * P], head_proj[:], start=True,
                                             stop=True)
                        last.then_inc(y_mm.sem, 1)

                    def c1(c):
                        norm_c.on_tensor(pe, c)

                    def c2(c, u):
                        pe.wait_ge(norm_c.xT_done.sem, norm_c.xT_done.at(c, 1))
                        for i in range(2):
                            pe.wait_ge(h_ev.sem, h_ev.at(c - 1, 2 * i + 2))
                            for b in range(2 * i, 2 * i + 2):
                                last = pe.matmul(ps_h[i][:, b % 2, :], fc_w[:, b * P:(b + 1) * P],
                                                 norm_c.xT[:, u, :], start=True, stop=True)
                            last.then_inc(h_mm.sem, 1)

                    def c3(c):
                        pe.wait_ge(h_ev.sem, h_ev.at(c, HB))
                        pe.wait_ge(y_add.sem, y_add.at(c, 1))
                        for t in range(ST):
                            for b in range(HB):
                                last = pe.matmul(ps_y[:, t, :], hT[:, b, t * P:(t + 1) * P], mp_w[:, b, :],
                                                 start=(b == 0), stop=(b == HB - 1))
                        last.then_inc(m_mm.sem, 1)

                    def a(c, u):
                        a1(c, u)
                        a2(c, u)

                    def b(c, u):
                        b1(c)
                        b2(c)
                        b4(c)

                    def body(c, u):
                        c1(c)
                        c2(c, u)
                        c3(c)
                        b1(c + 1)
                        b2(c + 1)
                        a1(c + 2, u)
                        a2(c + 2, u)
                        b4(c + 1)

                    in_threes(pe, SEQS, a, b, body)

                @block.scalar
                def _(act):
                    norm_a.start(nc, act=act)
                    norm_c.start(nc, act=act)
                    for s in (d_ev, scaled, cosined, w_ev, h_ev):
                        s.start(act)

                    def a1(c, u):
                        act.wait_ge(diffed.sem, diffed.at(c - 2, 1))
                        norm_a.on_scalar(act, c, u, (xd_mm.sem, xd_mm.at(c - 2, 2 * ST)))

                    def a2(c, u):
                        act.wait_ge(hamilton.sem, hamilton.at(c - 2, HAM))
                        for t in range(ST):
                            act.wait_ge(xd_mm.sem, xd_mm.at(c, 2 * t + 2))
                            act.activation(diff[:, u, t, :, :], ps_d[:], ACT.Copy).then_inc(d_ev.sem, 1)
                        act.wait_ge(x_ev.sem, x_ev.at(c, ST))
                        values = rows[:, u, :, :, HD:WRAP]
                        act.activation(turns_of[:], values, ACT.Copy, scale=1 / (2 * math.pi)).then_inc(scaled.sem, 1)
                        act.activation(whole[:], values, ACT.Copy, scale=1 / (2 * math.pi),
                                       bias=ROUND).then_inc(scaled.sem, 1)

                    def a3(c, u):
                        act.wait_ge(parted.sem, parted.at(c, 1))
                        act.activation(whole[:], turns_of[:], ACT.Abs).then_inc(cosined.sem, 1)
                        act.wait_ge(cosined.sem, cosined.at(c, 1))
                        act.activation(cosine[:, u, :, :, :], whole[:], ACT.Sin, bias=quarter[:, 0:1],
                                       scale=-2 * math.pi).then_inc(cosined.sem, 1)

                    def b1(c):
                        act.wait_ge(w_mm.sem, w_mm.at(c, 1))
                        act.wait_ge(z_mm.sem, z_mm.at(c - 1, 1))
                        act.activation(wT[:], ps_w[:], ACT.Copy).then_inc(w_ev.sem, 1)

                    def c1(c, u):
                        norm_c.on_scalar(act, c, u, (h_mm.sem, h_mm.at(c - 2, 2)))

                    def c2(c):
                        act.wait_ge(m_mm.sem, m_mm.at(c - 1, 1))
                        for b in range(HB):
                            act.wait_ge(h_mm.sem, h_mm.at(c, b // 2 + 1))
                            act.activation(hT[:, b, :], ps_h[b // 2][:, b % 2, :], ACT.Gelu,
                                           bias=fc_b[:, b:b + 1]).then_inc(h_ev.sem, 1)

                    def a(c, u):
                        a1(c, u)
                        a2(c, u)
                        a3(c, u)

                    def b(c, u):
                        b1(c)

                    def body(c, u):
                        c1(c, u)
                        c2(c)
                        b1(c + 1)
                        a1(c + 2, u)
                        a2(c + 2, u)
                        a3(c + 2, u)

                    in_threes(act, SEQS, a, b, body)

                @block.vector
                def _(dve):
                    norm_a.start(nc, dve=dve)
                    norm_c.start(nc, dve=dve)
                    for s in (x_ev, parted, hamilton, filtered, bias_a, bias_c, y_add, m_add):
                        s.start(dve)

                    def two(c):
                        return x[:, bass.ts(c, ST), :]

                    def wide(b):
                        return b[:].unsqueeze(1).to_broadcast([P, ST, D])

                    def a1(c):
                        norm_a.on_vector(dve, c)
                        norm_a.on_vector_scale(dve, c)
                        dve.wait_ge(norm_a.xn_done.sem, norm_a.xn_done.at(c, ST))
                        dve.tensor_tensor(two(c), two(c), wide(proj_b), ALU.add).then_inc(bias_a.sem, 1)

                    def a2(c, u):
                        for t in range(ST):
                            dve.wait_ge(xd_mm.sem, xd_mm.at(c, 2 * t + 1))
                            dve.tensor_tensor(rows[:, u, t, :, :], ps_x[:], qkv_b[:], ALU.add).then_inc(x_ev.sem, 1)

                    def a3(c):
                        dve.wait_ge(scaled.sem, scaled.at(c, 2))
                        dve.scalar_tensor_tensor(turns_of[:].rearrange("p t a d -> p (t a d)"),
                                                 whole[:].rearrange("p t a d -> p (t a d)"), ROUND,
                                                 turns_of[:].rearrange("p t a d -> p (t a d)"), ALU.subtract,
                                                 ALU.subtract).then_inc(parted.sem, 1)

                    def b1(c, u):
                        k = 0

                        def step(ins):
                            nonlocal k
                            k += 1
                            ins.then_inc(hamilton.sem, 1)
                            return k

                        def after(n):
                            dve.wait_ge(hamilton.sem, hamilton.at(c, n))

                        def part_of(i, n):
                            return (rows[:, u, :, n, HD:WRAP], diff[:, u, :, n, :], rows[:, u, :, n, 0:D],
                                    cosine[:, u, :, n, :])[i]

                        dve.wait_ge(cosined.sem, cosined.at(c, 2))
                        dve.wait_ge(w_mm.sem, w_mm.at(c - 1, 1))
                        signs = [(ALU.subtract, ALU.add, ALU.subtract), (ALU.add, ALU.subtract, ALU.add),
                                 (ALU.subtract, ALU.add, ALU.add), (ALU.add, ALU.subtract, ALU.subtract)]
                        for i in range(4):
                            p0 = 4 * (i % 2)
                            for j in range(4):
                                step(dve.tensor_tensor(part[:, p0 + j, :, :], part_of(j, 0), part_of(i ^ j, 1),
                                                       ALU.mult))
                            after(k - 2)
                            step(dve.tensor_tensor(part[:, p0, :, :], part[:, p0, :, :], part[:, p0 + 1, :, :],
                                                   signs[i][0]))
                            after(k - 1)
                            step(dve.tensor_tensor(part[:, p0 + 2, :, :], part[:, p0 + 2, :, :],
                                                   part[:, p0 + 3, :, :], signs[i][1]))
                            after(k)
                            step(dve.tensor_tensor(comp[:, i, :, :], part[:, p0, :, :], part[:, p0 + 2, :, :],
                                                   signs[i][2]))
                        for i in range(4):
                            after(k if i == 3 else 7 * (i + 1))
                            step(dve.tensor_tensor(comp[:, i, :, :], comp[:, i, :, :], part_of(i, 2), ALU.mult))
                        after(k - 2)
                        step(dve.tensor_tensor(comp[:, 0, :, :], comp[:, 0, :, :], comp[:, 1, :, :], ALU.subtract))
                        after(k - 1)
                        step(dve.tensor_tensor(comp[:, 2, :, :], comp[:, 2, :, :], comp[:, 3, :, :], ALU.add))
                        after(k)
                        step(dve.tensor_tensor(product[:], comp[:, 0, :, :], comp[:, 2, :, :], ALU.subtract))
                        assert k == HAM

                    def b2(c):
                        dve.wait_ge(z_mm.sem, z_mm.at(c, 1))
                        dve.wait_ge(y_mm.sem, y_mm.at(c - 1, 1))
                        dve.tensor_tensor(z[:], ps_z[:], filt[:], ALU.mult).then_inc(filtered.sem, 1)

                    def b4(c):
                        dve.wait_ge(y_mm.sem, y_mm.at(c, 1))
                        dve.wait_ge(bias_a.sem, bias_a.at(c, 1))
                        dve.tensor_tensor(two(c), ps_y[:], two(c), ALU.add).then_inc(y_add.sem, 1)

                    def c1(c):
                        dve.wait_ge(y_add.sem, y_add.at(c, 1))
                        dve.sem_inc(norm_c.turns, 1)
                        norm_c.on_vector(dve, c)
                        norm_c.on_vector_scale(dve, c)
                        dve.wait_ge(norm_c.xn_done.sem, norm_c.xn_done.at(c, ST))
                        dve.tensor_tensor(two(c), two(c), wide(mp_b), ALU.add).then_inc(bias_c.sem, 1)

                    def c3(c):
                        dve.wait_ge(m_mm.sem, m_mm.at(c, 1))
                        dve.wait_ge(bias_c.sem, bias_c.at(c, 1))
                        dve.tensor_tensor(two(c), ps_y[:], two(c), ALU.add).then_inc(m_add.sem, 1)

                    def a(c, u):
                        a1(c)
                        a2(c, u)
                        a3(c)

                    def b(c, u):
                        b1(c, u)
                        b2(c)
                        b4(c)

                    def body(c, u):
                        c1(c)
                        b1(c + 1, 1 - u)
                        c3(c)
                        a1(c + 2)
                        b2(c + 1)
                        a2(c + 2, u)
                        b4(c + 1)
                        a3(c + 2)

                    in_threes(dve, SEQS, a, b, body)

            ctx.clear(nc)

        with nc.Block() as block:
            @block.vector
            def _(dve):
                dve.tensor_tensor(rows_x[:, 0:TILES, :], rows_x[:, 0:TILES, :], x[:, 0:TILES, :], ALU.add)

        ctx.clear(nc)


def build(nc, a, phases):
    with ExitStack() as ctx:
        def sb(n, shape, dt=F32):
            return ctx.enter_context(nc.sbuf_tensor(n, shape, dt))

        def sem(n):
            return ctx.enter_context(nc.semaphore(n))

        E, EH = 8, 512
        EB = EH // P
        F_H = 384
        FB = F_H // P
        x = sb("x", [P, TILES + CT, D])
        ident = sb("ident", [P, P])
        order = sb("order", [P, CT, E])
        moe_gate = sb("moe_gate", [P, E])
        moe_w1 = sb("moe_w1", [P, E * EH])
        moe_w3 = sb("moe_w3", [P, E * EH])
        moe_w2 = sb("moe_w2", [P, E * EB, D])
        ff_w1 = sb("ff_w1", [P, F_H])
        ff_w3 = sb("ff_w3", [P, F_H])
        ff_w2 = sb("ff_w2", [P, FB, D])
        ff_i1 = sb("ff_i1", [P, F_H], I32)
        ff_i3 = sb("ff_i3", [P, F_H], I32)
        ff_i2 = sb("ff_i2", [P, FB, D], I32)
        loaded = sem("loaded")
        dequant = sem("dequant")
        pad_set = sem("pad_set")
        stored = sem("stored")

        rows = a["h"].rearrange("b (t p) d -> p (b t) d", p=P)

        pieces = [(x[:, 0:TILES, :], rows), (ident[:], a["ident"]), (order[:], a["order"]),
                  (moe_gate[:], a["moe_gate"]), (moe_w1[:], a["moe_w1"]), (moe_w3[:], a["moe_w3"]),
                  (moe_w2[:], a["moe_w2"].rearrange("(n p) d -> p n d", p=P)),
                  (ff_i1[:], a["ff_w1"]), (ff_i3[:], a["ff_w3"]),
                  (ff_i2[:], a["ff_w2"].rearrange("(n p) d -> p n d", p=P))]
        with nc.Block() as block:
            @block.sync
            def _(sp):
                for to, of in pieces:
                    sp.dma_start(to, of).then_inc(loaded, 16)
                sp.wait_ge(loaded, 16 * len(pieces))

            @block.gpsimd
            def _(pool):
                pool.memset(x[:, TILES:TILES + CT, :], 0.0).then_inc(pad_set, 1)

            @block.vector
            def _(dve):
                dve.wait_ge(loaded, 16 * len(pieces))
                for to, of in ((ff_w1, ff_i1), (ff_w3, ff_i3), (ff_w2, ff_i2)):
                    dve.tensor_scalar(to[:], of[:], float(np.float32(1.0 / 127.0)), None,
                                      ALU.mult).then_inc(dequant, 1)

        for n, phase in enumerate(phases):
            if phase == "moe":
                feed_forward(nc, f"moe{n}", x, ident, moe_w1, moe_w3, moe_w2, E, EB, moe_gate, order)
            if phase == "mix":
                mixed_attention(nc, x, ident, a)
            if phase == "one":
                single_attention(nc, x, ident, a)
            if phase == "grp":
                grouped_attention(nc, x, ident, a)
            if phase == "spec":
                spectral_layers(nc, x, ident, a)
            if phase == "ff":
                feed_forward(nc, f"ff{n}", x, ident, ff_w1, ff_w3, ff_w2, 1, FB)

        with nc.Block() as block:
            @block.sync
            def _(sp):
                sp.dma_start(a["out"].rearrange("b (t p) d -> p (b t) d", p=P),
                             x[:, 0:TILES, :]).then_inc(stored, 16)
                sp.wait_ge(stored, 16)


def kernel(**inputs):
    import concourse.bacc as bacc
    from concourse.bass_utils import run_bass_kernel_spmd

    np_in = {k: np.asarray(v) for k, v in inputs.items()}
    f32 = np.float32

    def turned(a, *axes):
        return np.ascontiguousarray(np.transpose(a, axes))

    arrays = {
        "h": np_in["L0_attn_a_h"],
        "ident": np.eye(P, dtype=f32),
        "order": np.broadcast_to(np.arange(8, 0, -1, dtype=f32), (P, CT, 8)).copy(),
        "moe_gate": turned(np_in["L0_ffn_gate_w"], 1, 0),
        "moe_w1": turned(np_in["L0_ffn_w1"], 2, 0, 1).reshape(D, -1),
        "moe_w3": turned(np_in["L0_ffn_w3"], 2, 0, 1).reshape(D, -1),
        "moe_w2": turned(np_in["L0_ffn_w2"], 0, 2, 1).reshape(-1, D),
        "ff_w1": turned(np_in["L1_ffn_w_gate"], 1, 0),
        "ff_w3": turned(np_in["L1_ffn_w_up"], 1, 0),
        "ff_w2": turned(np_in["L1_ffn_w_down"], 1, 0),
    }
    def rows(a):
        return np.broadcast_to(a, (P,) + a.shape).copy()

    q_at = np.arange(SEQ)[:, None]
    k_at = np.arange(SEQ)[None, :]
    masked = np.where(q_at >= k_at, f32(0), f32(BIG)).reshape(ST, P, SEQ)
    outside = np.where((q_at >= k_at) & (q_at - k_at < A0.WINDOW), f32(0), f32(BIG)).reshape(ST, P, SEQ)
    valid = (np.arange(A0.NB)[None, :] + 1) * A0.CR - 1 <= q_at
    some = valid.any(-1, keepdims=True)
    blocks = np.zeros((SEQ, A0.H, A0.C), f32)
    blocks[:, :, 0:A0.NB] = np.where(np.where(some, valid, True), f32(0), f32(BIG))[:, None, :]
    turn = 1.0 / 10000.0 ** (np.arange(16, dtype=f32) * 2.0 / 32)
    angle = (np.arange(SEQ, dtype=f32)[:, None] * turn.astype(f32)[None, :]).astype(f32)
    cs = np.stack([np.tile(np.cos(angle), (1, 2)), np.tile(np.sin(angle), (1, 2))], 1)
    mean_w = np.zeros((SEQ, A0.H, A0.NB), f32)
    mean_w[np.arange(SEQ), :, np.arange(SEQ) // A0.CR] = 1.0 / A0.CR

    def tiled(a):
        return np.ascontiguousarray(a.reshape((ST, P) + a.shape[1:]).swapaxes(0, 1)).astype(f32)

    q_gain = np_in["L0_attn_a_g_qnorm"]
    arrays.update({
        "a_qc": turned(np_in["L0_attn_a_w_qc"], 1, 0),
        "a_qup": np_in["L0_attn_a_w_qup"],
        "a_group": turned(np_in["L0_attn_a_w_out_group"], 2, 0, 1),
        "a_out": turned(np_in["L0_attn_a_w_out"].reshape(2, 64, D), 1, 0, 2),
        "a_kv": np.concatenate([np_in["L0_attn_a_w_k"], np_in["L0_attn_a_w_v"]], 1),
        "a_gain_q": rows(np.stack([q_gain, q_gain])),
        "a_gain_k": rows(np.stack([np_in["L0_attn_a_g_knorm"]] * 2)),
        "a_gain_col": np.concatenate([q_gain, q_gain])[:, None].copy(),
        "a_gate_w": np.concatenate([np_in["L0_attn_a_w_gate"]] * 2, 0),
        "a_gate_b": rows(np_in["L0_attn_a_b_gate"]),
        "a_sink": rows(np_in["L0_attn_a_sink_logit"]),
        "rope": tiled(cs),
        "causal": np.concatenate([masked[0][:, 0:P], masked[1]], 1),
        "window": np.concatenate([outside[0][:, 0:P], outside[1][:, P - A0.WINDOW:]], 1),
        "blocks": tiled(blocks),
        "any_block": tiled(some.astype(f32))[:, :, 0].copy(),
        "mean_w": tiled(mean_w.reshape(SEQ, -1)),
        "diagonal": np.repeat(np.eye(A0.H, dtype=f32), A0.NB, 0),
    })
    b = "L0_attn_b_"
    arrays.update({
        "b_wq": turned(np_in[b + "Wq"], 1, 0), "b_wk": turned(np_in[b + "Wk"], 1, 0),
        "b_wv": turned(np_in[b + "Wv"], 1, 0), "b_wo": turned(np_in[b + "Wo"], 1, 0),
        "b_bq": np_in[b + "bq"][:, None].copy(), "b_bk": np_in[b + "bk"][:, None].copy(),
        "b_bv": rows(np_in[b + "bv"]), "b_bo": rows(np_in[b + "bo"]),
    })
    g = "L1_attn_a_"
    keys_at = np.broadcast_to(np.concatenate([np.arange(P), np.arange(SEQ)]).astype(f32), (P, P + SEQ))
    arrays.update({
        "c_wq": np_in[g + "Wq"].reshape(G1.IN, G1.H, G1.HD // 2, 2),
        "c_wk": np.repeat(np_in[g + "Wk"].reshape(G1.IN, G1.KVH, 1, G1.HD), 2, 2),
        "c_wv": np_in[g + "Wv"],
        "c_wo": turned(np_in[g + "Wo"].reshape(G1.HP, P, D), 1, 0, 2),
        "c_phase": rows(np_in[g + "q_phase_angle"]),
        "c_slope": rows(np_in[g + "alibi_log_slopes"]),
        "keys_at": keys_at.copy(),
    })
    e = "L1_attn_b_"
    LAY = H1.LAYERS

    def spread(a):
        return np.broadcast_to(a[:, None], (LAY, P) + a.shape[1:]).copy()

    def by_part(a):
        a = a.reshape(a.shape[:-1] + (H1.H, 3, H1.HD)).swapaxes(-3, -2)
        return np.concatenate([a[..., -1:, :], a], -2).reshape(a.shape[:-3] + (3, H1.WRAP))

    def hartley(n):
        at = 2 * np.pi * (np.arange(n)[:, None] * np.arange(n)[None, :] % n) / n
        return np.cos(at) + np.sin(at)

    ks = np.fft.fftfreq(SEQ)[:, None, None]
    kh = np.fft.fftfreq(H1.H)[None, :, None]
    kd = np.fft.fftfreq(H1.HD)[None, None, :]
    even = np.cos(np.arctan(np.log(np.sqrt(ks ** 2 + kh ** 2 + kd ** 2 + 1e-10) + 1e-10)))
    lam = np.arange(SEQ, dtype=f32) / f32(SEQ)
    tau = np.arange(SEQ, dtype=f32) * f32(0.1)
    modulation = np.sin(tau + lam) * np.cos(tau - f32(2) * lam + f32(0.5) * lam ** 2)
    filt = even.reshape(SEQ, D) * (1.0 + 0.1 * modulation.astype(np.float64))[:, None] / (H1.H * H1.HD)
    arrays.update({
        "d_ln": np.stack([np_in[e + n] for n in ("ln1_w", "ln1_b", "ln2_w", "ln2_b")], -1),
        "d_qkv_w": np.ascontiguousarray(by_part(np_in[e + "attn_w"])),
        "d_qkv_b": spread(by_part(np_in[e + "attn_b"])),
        "d_proj_w": np_in[e + "aproj_w"],
        "d_proj_b": spread(np_in[e + "aproj_b"]),
        "d_fc_w": np_in[e + "fc_w"],
        "d_fc_b": turned(np_in[e + "fc_b"].reshape(LAY, H1.HB, P), 0, 2, 1),
        "d_mp_w": turned(np_in[e + "mproj_w"].reshape(LAY, H1.HB, P, D), 0, 2, 1, 3),
        "d_mp_b": spread(np_in[e + "mproj_b"]),
        "hartley": np.kron(hartley(H1.H), hartley(H1.HD)).astype(f32),
        "filter": np.ascontiguousarray(filt.T).astype(f32),
    })
    nc = bacc.Bacc("TRN2", target_bir_lowering=False, num_devices=1)
    aps = {k: nc.dram_tensor(f"in_{k}", v.shape, mybir.dt.from_np(v.dtype), kind="ExternalInput").ap()
           for k, v in arrays.items()}
    aps["out"] = nc.dram_tensor("out", (16, SEQ, D), F32, kind="ExternalOutput").ap()
    build(nc, aps, PHASES)
    r = run_bass_kernel_spmd(nc, [{f"in_{k}": v for k, v in arrays.items()}], core_ids=[0])
    return r.results[0]["out"]


PHASES = ['mix', 'moe', 'one', 'moe', 'grp', 'ff', 'spec', 'ff']
```

```python
import math
from contextlib import ExitStack

import numpy as np

import concourse.bass as bass
from concourse import mybir

ALU = mybir.AluOpType
ACT = mybir.ActivationFunctionType
AX_X = mybir.AxisListType.X
F32 = mybir.dt.float32
I32 = mybir.dt.int32

P = 128
D = 128
SEQ = 256
TOKENS = 16 * SEQ
TILES = TOKENS // P
CT = 4
CHUNKS = TILES // CT
CW = CT * P
SEQS = TOKENS // SEQ
ST = SEQ // P
BIG = 1e30
LN_EPS = 1e-5
ROUND = 1.5 * 2.0 ** 23
TURN_HIGH = 6.28125
TURN_LOW = 2 * math.pi - TURN_HIGH
HALF_TURN = 3.1415925


class Signal:

    def __init__(self, sem, per):
        self.sem, self.per = sem, per

    def start(self, eng):
        eng.sem_inc(self.sem, 2 * self.per)

    def at(self, chunk, n):
        return (chunk + 2) * self.per + n


class Phase(ExitStack):

    def __init__(self):
        super().__init__()
        self.used = []
        self.main = ExitStack()

    def main_block(self, nc):
        return self.main.enter_context(nc.Block())

    def semaphore(self, nc, name):
        self.used.append(self.enter_context(nc.semaphore(name)))
        return self.used[-1]

    def clear(self, nc):
        self.main.close()
        with nc.Block() as block:
            @block.gpsimd
            def _(pool):
                for s in self.used:
                    pool.sem_clear(s)


def in_pairs(eng, chunks, fronts, main):
    for front in fronts:
        front(0, 0)
    with eng.Fori(0, chunks // 2) as j:
        for u in range(2):
            c = j * 2 + u
            main(c, u, *[lambda c=c, u=u, front=front: front(c + 1, 1 - u) for front in fronts])


def pairs(eng, body):
    with eng.Fori(0, SEQS // 2) as j:
        for u in range(2):
            body(j * 2 + u, u)


class Norm:

    def __init__(self, nc, ctx, name, x, ident, tiles, ps=None, bank_free=None, gain=None, shift=None):
        CT = self.tiles = tiles
        CW = CT * P

        def sb(n, shape):
            return ctx.enter_context(nc.sbuf_tensor(f"{name}_{n}", shape, F32))

        def signal(n, per):
            return Signal(ctx.semaphore(nc, f"{name}_{n}"), per)

        self.x, self.ident, self.gain, self.shift = x, ident, gain, shift
        self.stats = sb("stats", [P, CT, 6])
        self.mv = sb("mean_var", [P, CT, 2])
        self.veps = sb("var_eps", [P, CT])
        self.power = sb("power", [P, CT])
        self.rstd = sb("rstd", [P, CT])
        self.xn = sb("xn", [P, CT, D])
        self.xT = sb("xT", [P, 2, CW])
        self.bank_free = bank_free
        self.ps = ctx.enter_context(nc.psum_tensor(f"{name}_psT", [P, CW], F32)) if ps is None else ps[:, 0:CW]
        self.stat_done = signal("stat_done", CT)
        self.mv_done = signal("mv_done", CT)
        self.pow_done = signal("pow_done", 2)
        self.xn_done = signal("xn_done", CT)
        self.tr_done = signal("tr_done", 1)
        self.xT_done = signal("xT_done", 1)
        self.turns = ctx.semaphore(nc, f"{name}_turns")
        self.power_set = ctx.semaphore(nc, f"{name}_power_set")

    def start(self, nc, dve=None, pool=None, pe=None, act=None):
        if dve is not None:
            for s in (self.stat_done, self.mv_done, self.xn_done):
                s.start(dve)
        if pool is not None:
            self.pow_done.start(pool)
            pool.memset(self.power[:], -0.5).then_inc(self.power_set, 1)
            pool.wait_ge(self.power_set, 1)
        if pe is not None:
            self.tr_done.start(pe)
        if act is not None:
            self.xT_done.start(act)

    def on_vector(self, dve, c):
        CT = self.tiles
        for t in range(CT):
            dve.bn_stats(self.stats[:, t, :], self.x[:, c * CT + t, :]).then_inc(self.stat_done.sem, 1)
        dve.wait_ge(self.pow_done.sem, self.pow_done.at(c - 1, 1))
        dve.wait_ge(self.xn_done.sem, self.xn_done.at(c - 1, CT))
        dve.wait_ge(self.stat_done.sem, self.stat_done.at(c, CT))
        dve.sem_inc(self.turns, 1)
        for t in range(CT):
            dve.bn_aggr(self.mv[:, t, :], self.stats[:, t, :]).then_inc(self.mv_done.sem, 1)

    def on_pool(self, pool, c):
        CT = self.tiles
        pool.wait_ge(self.mv_done.sem, self.mv_done.at(c, CT))
        pool.sem_inc(self.turns, 1)
        pool.tensor_scalar(self.veps[:], self.mv[:, :, 1], LN_EPS, None, ALU.add).then_inc(self.pow_done.sem, 1)
        pool.wait_ge(self.pow_done.sem, self.pow_done.at(c, 1))
        pool.wait_ge(self.xn_done.sem, self.xn_done.at(c - 1, CT))
        pool.tensor_tensor(self.rstd[:], self.veps[:], self.power[:], ALU.pow).then_inc(self.pow_done.sem, 1)

    def on_vector_scale(self, dve, c):
        CT = self.tiles
        dve.wait_ge(self.mv_done.sem, self.mv_done.at(c, CT))
        dve.wait_ge(self.pow_done.sem, self.pow_done.at(c, 2))
        dve.wait_ge(self.tr_done.sem, self.tr_done.at(c - 1, 1))
        for t in range(CT):
            dve.tensor_scalar(self.xn[:, t, :], self.x[:, c * CT + t, :], self.mv[:, t, 0:1],
                              self.rstd[:, t:t + 1], ALU.subtract, ALU.mult).then_inc(self.xn_done.sem, 1)

    def on_tensor(self, pe, c):
        CT = self.tiles
        pe.wait_ge(self.xT_done.sem, self.xT_done.at(c - 1, 1))
        if self.bank_free is not None:
            pe.wait_ge(*self.bank_free(c))
        for t in range(CT):
            pe.wait_ge(self.xn_done.sem, self.xn_done.at(c, t + 1))
            last = pe.transpose(self.ps[:, t * P:(t + 1) * P], self.xn[:, t, :], self.ident[:])
        last.then_inc(self.tr_done.sem, 1)

    def on_scalar(self, act, c, u, xT_free):
        act.wait_ge(self.tr_done.sem, self.tr_done.at(c, 1))
        act.wait_ge(*xT_free)
        if self.gain is None:
            last = act.activation(self.xT[:, u, :], self.ps[:, :], ACT.Copy)
        else:
            last = act.activation(self.xT[:, u, :], self.ps[:, :], ACT.Identity,
                                  bias=self.shift, scale=self.gain)
        last.then_inc(self.xT_done.sem, 1)


def feed_forward(nc, name, x, ident, w1, w3, w2, experts, blocks, gate_w=None, order=None):
    units = experts * blocks
    with Phase() as ctx:
        def sb(n, shape):
            return ctx.enter_context(nc.sbuf_tensor(f"{name}_{n}", shape, F32))

        def ps(n, shape):
            return ctx.enter_context(nc.psum_tensor(f"{name}_{n}", shape, F32))

        def signal(n, per):
            return Signal(ctx.semaphore(nc, f"{name}_{n}"), per)

        norm = Norm(nc, ctx, name, x, ident, CT)
        ps_a = [ps(f"ps_a{i}", [P, CW]) for i in range(2)]
        ps_b = [ps(f"ps_b{i}", [P, CW]) for i in range(2)]
        ps_o = [ps(f"ps_o{i}", [P, CT, D]) for i in range(2)]
        silu = sb("silu", [P, 2, CW])
        hidden = sb("hidden", [P, 2, blocks, CW])
        up_done = signal("up_done", 2 * units)
        silu_done = signal("silu_done", units)
        hid_done = signal("hid_done", units)
        down_done = signal("down_done", experts)
        comb_done = signal("comb_done", CT * experts)
        if gate_w is not None:
            E = experts
            ps_g = ps("ps_g", [P, CT, E])
            score = sb("score", [P, CT, E])
            same = sb("same", [P, CT, E])
            place = sb("place", [P, CT, E])
            best = sb("best", [P, 2, CT, E])
            top = sb("top", [P, 2, CT])
            first = sb("first", [P, CT])
            gap = sb("gap", [P, CT])
            half = sb("half", [P, CT])
            share = sb("share", [P, 2, CT])
            gate = sb("gate", [P, 2, CT, E])
            GATE_STEPS = 18
            score_mm = signal("score_mm", 1)
            gate_step = signal("gate_step", GATE_STEPS)
            tanh_done = signal("tanh_done", 1)

        block = ctx.main_block(nc)

        @block.gpsimd
        def _(pool):
            norm.start(nc, pool=pool)
            in_pairs(pool, CHUNKS, [lambda c, u: norm.on_pool(pool, c)], lambda c, u, nxt: nxt())

        @block.tensor
        def _(pe):
            norm.start(nc, pe=pe)
            up_done.start(pe)
            down_done.start(pe)
            if gate_w is not None:
                score_mm.start(pe)

            def scores(c, u):
                pe.wait_ge(gate_step.sem, gate_step.at(c - 1, 1))
                for t in range(CT):
                    last = pe.matmul(ps_g[:, t, :], norm.xT[:, u, t * P:(t + 1) * P], gate_w[:],
                                     start=True, stop=True)
                last.then_inc(score_mm.sem, 1)

            def up(c, u, e):
                for b in range(blocks):
                    n = e * blocks + b
                    i = n % 2 if units % 2 == 0 else (u * units + n) % 2
                    pe.wait_ge(hid_done.sem, hid_done.at(c, n - 1))
                    pe.matmul(ps_a[i][:], w1[:, n * P:(n + 1) * P], norm.xT[:, u, :],
                              start=True, stop=True).then_inc(up_done.sem, 1)
                    pe.matmul(ps_b[i][:], w3[:, n * P:(n + 1) * P], norm.xT[:, u, :],
                              start=True, stop=True).then_inc(up_done.sem, 1)

            def down(c, u, e):
                g = (u * experts + e) % 2
                pe.wait_ge(hid_done.sem, hid_done.at(c, (e + 1) * blocks))
                pe.wait_ge(comb_done.sem, comb_done.at(c, CT * (e - 1)))
                for t in range(CT):
                    for b in range(blocks):
                        last = pe.matmul(ps_o[g][:, t, :], hidden[:, g, b, t * P:(t + 1) * P],
                                         w2[:, e * blocks + b, :], start=(b == 0), stop=(b == blocks - 1))
                last.then_inc(down_done.sem, 1)

            def main(c, u, nxt):
                pe.wait_ge(norm.xT_done.sem, norm.xT_done.at(c, 1))
                if gate_w is not None:
                    scores(c, u)
                for e in range(experts):
                    up(c, u, e)
                    if e == experts - 1:
                        nxt()
                    if e >= 1:
                        down(c, u, e - 1)
                down(c, u, experts - 1)

            in_pairs(pe, CHUNKS, [lambda c, u: norm.on_tensor(pe, c)], main)

        @block.scalar
        def _(act):
            norm.start(nc, act=act)
            silu_done.start(act)
            if gate_w is not None:
                tanh_done.start(act)

            def main(c, u, nxt):
                for e in range(experts):
                    for b in range(blocks):
                        n = e * blocks + b
                        i = n % 2 if units % 2 == 0 else (u * units + n) % 2
                        act.wait_ge(up_done.sem, up_done.at(c, 2 * n + 1))
                        act.wait_ge(hid_done.sem, hid_done.at(c, n - 1))
                        act.activation(silu[:, i, :], ps_a[i][:], ACT.Silu).then_inc(silu_done.sem, 1)
                        if gate_w is not None and n == 1:
                            act.wait_ge(gate_step.sem, gate_step.at(c, 13))
                            act.activation(half[:], gap[:], ACT.Tanh, scale=0.5).then_inc(tanh_done.sem, 1)
                nxt()

            in_pairs(act, CHUNKS, [lambda c, u: norm.on_scalar(
                act, c, u, (down_done.sem, down_done.at(c - 2, experts)))], main)

        @block.vector
        def _(dve):
            norm.start(nc, dve=dve)
            hid_done.start(dve)
            comb_done.start(dve)
            if gate_w is not None:
                gate_step.start(dve)

            def best_two(c, u):
                k = 0

                def step(ins):
                    nonlocal k
                    k += 1
                    ins.then_inc(gate_step.sem, 1)
                    dve.wait_ge(gate_step.sem, gate_step.at(c, k))

                def wide(a):
                    return a.unsqueeze(2).to_broadcast([P, CT, experts])

                dve.wait_ge(score_mm.sem, score_mm.at(c, 1))
                step(dve.tensor_copy(score[:], ps_g[:]))
                for r in range(2):
                    step(dve.tensor_reduce(top[:, r, :], score[:], AX_X, ALU.max))
                    step(dve.tensor_tensor(same[:], score[:], wide(top[:, r, :]), ALU.is_equal))
                    step(dve.tensor_tensor(place[:], same[:], order[:], ALU.mult))
                    step(dve.tensor_reduce(first[:], place[:], AX_X, ALU.max))
                    step(dve.tensor_tensor(best[:, r, :, :], place[:], wide(first[:]), ALU.is_equal))
                    if r == 0:
                        step(dve.scalar_tensor_tensor(score[:], best[:, 0, :, :], -1e30, score[:],
                                                      ALU.mult, ALU.add))
                step(dve.tensor_tensor(gap[:], top[:, 1, :], top[:, 0, :], ALU.subtract))
                assert k == 13
                dve.wait_ge(tanh_done.sem, tanh_done.at(c, 1))
                step(dve.tensor_scalar(share[:, 0, :], half[:], -0.5, 0.5, ALU.mult, ALU.add))
                step(dve.tensor_scalar(share[:, 1, :], half[:], 0.5, 0.5, ALU.mult, ALU.add))
                step(dve.tensor_tensor(best[:, 0, :, :], best[:, 0, :, :], wide(share[:, 0, :]), ALU.mult))
                step(dve.tensor_tensor(best[:, 1, :, :], best[:, 1, :, :], wide(share[:, 1, :]), ALU.mult))
                step(dve.tensor_tensor(gate[:, u, :, :], best[:, 0, :, :], best[:, 1, :, :], ALU.add))
                assert k == GATE_STEPS

            def unit(c, u, e, b):
                n = e * blocks + b
                i = n % 2 if units % 2 == 0 else (u * units + n) % 2
                g = (u * experts + e) % 2
                dve.wait_ge(silu_done.sem, silu_done.at(c, n + 1))
                dve.wait_ge(up_done.sem, up_done.at(c, 2 * n + 2))
                if b == 0:
                    dve.wait_ge(down_done.sem, down_done.at(c, e - 1))
                dve.tensor_tensor(hidden[:, g, b, :], silu[:, i, :], ps_b[i][:],
                                  ALU.mult).then_inc(hid_done.sem, 1)

            def combine(c, u, e):
                g = (u * experts + e) % 2
                dve.wait_ge(down_done.sem, down_done.at(c, e + 1))
                for t in range(CT):
                    rows = x[:, c * CT + t, :]
                    if e >= 1:
                        dve.wait_ge(comb_done.sem, comb_done.at(c, CT * (e - 1) + t + 1))
                    if gate_w is not None:
                        last = dve.scalar_tensor_tensor(rows, ps_o[g][:, t, :], gate[:, u, t, e:e + 1], rows,
                                                        ALU.mult, ALU.add)
                    else:
                        last = dve.tensor_tensor(rows, ps_o[g][:, t, :], rows, ALU.add)
                    last.then_inc(comb_done.sem, 1)

            def front(c, u):
                norm.on_vector(dve, c)
                norm.on_vector_scale(dve, c)

            def main(c, u, nxt):
                for e in range(experts):
                    for b in range(blocks):
                        unit(c, u, e, b)
                        if gate_w is not None and e == 0 and b == 1:
                            best_two(c, u)
                    if e == max(0, experts - 3):
                        nxt()
                    if e >= 1:
                        combine(c, u, e - 1)
                combine(c, u, experts - 1)

            in_pairs(dve, CHUNKS, [front], main)

        ctx.clear(nc)



class A0:
    H, HD, QC, CR = 8, 64, 32, 32
    NB = SEQ // CR
    WINDOW = 64
    W1 = P + WINDOW
    X = 16
    SINK, GATE = NB, NB + 1
    C = NB + 4


def mixed_attention(nc, x, ident, w):
    H, HD, NB, X, C = A0.H, A0.HD, A0.NB, A0.X, A0.C
    HP = H // 2
    with Phase() as ctx:
        def sb(n, shape):
            return ctx.enter_context(nc.sbuf_tensor(f"mix_{n}", shape, F32))

        def ps(n, shape):
            return ctx.enter_context(nc.psum_tensor(f"mix_{n}", shape, F32))

        def sem(n):
            return ctx.semaphore(nc, f"mix_{n}")

        def signal(n, per):
            return Signal(sem(n), per)

        ps_f = ps("ps_f", [P, 512])
        ps_q = ps("ps_q", [P, H, HD])
        ps_kv = ps("ps_kv", [P, 512])
        ps_s = [ps(f"ps_s{i}", [P, X + SEQ]) for i in range(2)]
        ps_t = [ps(f"ps_t{i}", [P, 512]) for i in range(2)]
        ps_o = ps("ps_o", [P, H, HD])

        qc_w = sb("qc_w", [A0.QC, D])
        qup_w = sb("qup_w", [A0.QC, H * HD])
        group_w = sb("group_w", [64, 2, 2 * P])
        out_w = sb("out_w", [64, 2, D])
        q_w = sb("q_w", [D, H * HD])
        kv_w = sb("kv_w", [D, 2 * HD])
        y_w = sb("y_w", [P, HP, D])
        gain_q = sb("gain_q", [P, 2, HD])
        gain_k = sb("gain_k", [P, 2, HD])
        gain_qk = sb("gain_qk", [P, 2, HD])
        gain_col = sb("gain_col", [P, 1])
        gate_w = sb("gate_w", [P, 3])
        gate_b = sb("gate_b", [P, 3])
        sink = sb("sink", [P, H])
        rope = sb("rope", [P, ST, 2, 32])
        causal = sb("causal", [P, P + SEQ])
        window = sb("window", [P, P + A0.W1])
        extra = sb("extra", [P, ST, H, C])
        any_block = sb("any_block", [P, ST])
        mean_w = sb("mean_w", [P, ST, H * NB])
        diagonal = sb("diagonal", [H * NB, H])

        qk = sb("qk", [P, ST, H + 1, HD])
        sq = sb("sq", [P, ST, H + 1, HD])
        ss = sb("ss", [P, ST, H + 1])
        ms = sb("ms", [P, ST, H + 1])
        rms = sb("rms", [P, ST, H + 1])
        half = sb("half", [P, ST, H + 1])
        rc = sb("rc", [P, H + 1, 32])
        rs = sb("rs", [P, H + 1, 32])
        kd = sb("kd", [P, ST, 2, HD])
        v = sb("v", [P, 2, ST, HD])
        vc = sb("vc", [H * NB, 2, H, HD])
        kc = sb("kc", [P, NB])
        kx = sb("kx", [P, 2, X + SEQ])
        qT = sb("qT", [P, 2, ST, HP, P])
        s_all = sb("s_all", [P, 2, SEQ])
        s_win = sb("s_win", [P, 2, A0.W1])
        low_all = sb("low_all", [P, ST, H])
        low_win = sb("low_win", [P, ST, H])
        p_all = sb("p_all", [P, ST, H, SEQ])
        p_win = sb("p_win", [P, ST, H, A0.W1])
        cg = sb("cg", [P, ST, H, C])
        low_c = sb("low_c", [P, H])
        e_c = sb("e_c", [P, H, NB + 1])
        e_sink = sb("e_sink", [P, H])
        sig = sb("sig", [P, H, 3])
        total = sb("total", [P, ST, 4, H])
        inverse = sb("inverse", [P, 4, H])
        ratio = sb("ratio", [P, 3, H])
        factor = sb("factor", [P, ST, 3, H])
        p_c = sb("p_c", [P, ST, H, NB])
        p_cT = sb("p_cT", [H * NB, P])
        pT = sb("pT", [P, 2, ST, P])
        o = sb("o", [P, H, HD])
        oT = sb("oT", [P, HP, P])

        loaded, made, multiplied, passed = sem("loaded"), sem("made"), sem("multiplied"), sem("passed")
        kv_mm = signal("kv_mm", 1)
        q_mm = signal("q_mm", ST)
        copied = signal("copied", 4 * ST)
        prepared = signal("prepared", 3 * ST + 3)
        turned = signal("turned", 6 * ST)
        front_mm = signal("front_mm", 4)
        front_ev = signal("front_ev", 3)
        norm = Norm(nc, ctx, "mix", x, ident, ST, ps=ps_f,
                    bank_free=lambda c: (front_ev.sem, front_ev.at(c - 1, 3)))
        U = ST * H
        s_mm = signal("s_mm", U)
        least = signal("least", 3 * U)
        exped = signal("exped", 2 * U)
        MIX = 13
        mixing = signal("mixing", MIX * ST)
        mix_exp = signal("mix_exp", 3 * ST)
        weighed = signal("weighed", 2 * U)
        R = H + 2
        p_tr = signal("p_tr", R * ST)
        p_ev = signal("p_ev", R * ST)
        o_mm = signal("o_mm", R * ST)
        o_ev = signal("o_ev", ST)
        added = signal("added", ST)

        pieces = [(qc_w, "a_qc"), (qup_w, "a_qup"), (group_w, "a_group"), (out_w, "a_out"), (kv_w, "a_kv"),
                  (gain_q, "a_gain_q"), (gain_k, "a_gain_k"), (gain_col, "a_gain_col"), (gate_w, "a_gate_w"),
                  (gate_b, "a_gate_b"), (sink, "a_sink"), (rope, "rope"), (causal, "causal"),
                  (window, "window"), (extra, "blocks"), (any_block, "any_block"), (mean_w, "mean_w"),
                  (diagonal, "diagonal")]

        with nc.Block() as block:
            @block.sync
            def _(sp):
                for to, of in pieces:
                    sp.dma_start(to[:], w[of]).then_inc(loaded, 16)

            @block.gpsimd
            def _(pool):
                pool.memset(half[:], -0.5)

            @block.tensor
            def _(pe):
                pe.wait_ge(loaded, 16 * len(pieces))
                pe.matmul(ps_q[:], qc_w[:], qup_w[:], start=True, stop=True).then_inc(multiplied, 1)
                for b in range(HP):
                    last = pe.matmul(ps_f[:, b * P:(b + 1) * P], group_w[:, b // 2, (b % 2) * P:(b % 2 + 1) * P],
                                     out_w[:, b // 2, :], start=True, stop=True)
                last.then_inc(multiplied, 1)

            @block.vector
            def _(dve):
                dve.wait_ge(loaded, 16 * len(pieces))
                dve.memset(kx[:], 0.0).then_inc(made, 1)
                dve.scalar_tensor_tensor(gain_qk[:], gain_q[:], -(HD ** -0.5), gain_k[:], ALU.mult, ALU.mult)
                dve.wait_ge(made, 1)
                for u in range(2):
                    dve.tensor_scalar(kx[:, u, A0.GATE:A0.GATE + 3], gate_w[:], gain_col[:, 0:1], -1.0,
                                      ALU.mult, ALU.mult)
                for t in range(ST):
                    dve.tensor_scalar(extra[:, t, :, A0.SINK], sink[:], -1.0, None, ALU.mult)
                    dve.tensor_scalar(extra[:, t, :, A0.GATE:A0.GATE + 3],
                                      gate_b[:].unsqueeze(1).to_broadcast([P, H, 3]), -1.0, None, ALU.mult)
                dve.wait_ge(multiplied, 2)
                dve.tensor_copy(q_w[:], ps_q[:].rearrange("p h d -> p (h d)"))
                dve.tensor_copy(y_w[:].rearrange("p b d -> p (b d)"), ps_f[:])

        block = ctx.main_block(nc)

        def keys(t):
            return (t + 1) * P

        def reach(t):
            return (0, P, 0) if t == 0 else (P - A0.WINDOW, A0.W1, P)

        @block.gpsimd
        def _(pool):
            norm.start(nc, pool=pool)
            turned.start(pool)

            def project(c, u):
                for t in range(ST):
                    pool.wait_ge(prepared.sem, prepared.at(c, t + 1))
                    pool.sem_inc(norm.turns, 1)
                    pool.tensor_scalar(ms[:, t, :], ss[:, t, :], 1.0 / HD, 1e-6, ALU.mult,
                                       ALU.add).then_inc(turned.sem, 1)
                    pool.wait_ge(turned.sem, turned.at(c, 2 * t + 1))
                    pool.tensor_tensor(rms[:, t, :], ms[:, t, :], half[:, t, :], ALU.pow).then_inc(turned.sem, 1)
                for t in range(ST):
                    k = 2 * ST + 4 * t
                    head = qk[:, t, :, 0:32]
                    pool.wait_ge(prepared.sem, prepared.at(c, ST + t + 1))
                    for n, to in enumerate((rc, rs)):
                        pool.tensor_tensor(to[:], head, rope[:, t, n:n + 1, :].to_broadcast([P, H + 1, 32]),
                                           ALU.mult).then_inc(turned.sem, 1)
                    pool.wait_ge(turned.sem, turned.at(c, k + 2))
                    pool.tensor_tensor(qk[:, t, :, 0:16], rc[:, :, 0:16], rs[:, :, 16:32],
                                       ALU.subtract).then_inc(turned.sem, 1)
                    pool.tensor_tensor(qk[:, t, :, 16:32], rc[:, :, 16:32], rs[:, :, 0:16],
                                       ALU.add).then_inc(turned.sem, 1)
                    pool.wait_ge(turned.sem, turned.at(c, k + 4))

            def main(c, u, f1, f2, f3):
                f1()
                f2()
                f3()

            in_pairs(pool, SEQS, [lambda c, u: norm.on_pool(pool, c), project, lambda c, u: None], main)

        @block.tensor
        def _(pe):
            norm.start(nc, pe=pe)
            for s in (kv_mm, q_mm, front_mm, s_mm, p_tr, o_mm):
                s.start(pe)

            def project(c, u):
                pe.wait_ge(norm.xT_done.sem, norm.xT_done.at(c, 1))
                pe.wait_ge(prepared.sem, prepared.at(c - 1, 3 * ST + 1))
                for t in range(ST):
                    last = pe.matmul(ps_kv[:, t * P:(t + 1) * P], norm.xT[:, u, t * P:(t + 1) * P], kv_w[:],
                                     start=True, stop=True)
                last.then_inc(kv_mm.sem, 1)
                for t in range(ST):
                    pe.wait_ge(copied.sem, copied.at(c, 4 * (t - 1) + 3))
                    pe.matmul(ps_q[:], norm.xT[:, u, t * P:(t + 1) * P], q_w[:], start=True,
                              stop=True).then_inc(q_mm.sem, 1)
                pe.wait_ge(copied.sem, copied.at(c, 4 * (ST - 1) + 2))
                for t in range(ST):
                    last = pe.matmul(ps_kv[0:H * NB, 2 * P:2 * P + HD], mean_w[:, t, :], v[:, u, t, :],
                                     start=(t == 0), stop=(t == ST - 1))
                last.then_inc(front_mm.sem, 1)

            def turn(c, u):
                pe.wait_ge(prepared.sem, prepared.at(c, 3 * ST))
                pe.wait_ge(front_ev.sem, front_ev.at(c - 1, 3))
                for t in range(ST):
                    last = pe.transpose(ps_f[:, t * P:(t + 1) * P], kd[:, t, :, :].rearrange("p a d -> p (a d)"),
                                        ident[:])
                last.then_inc(front_mm.sem, 1)
                for t in range(ST):
                    pe.wait_ge(turned.sem, turned.at(c, 2 * ST + 4 * (t + 1)))
                    pe.wait_ge(front_ev.sem, front_ev.at(c, t + 1))
                    for b in range(HP):
                        last = pe.transpose(ps_f[:, b * P:(b + 1) * P],
                                            qk[:, t, 2 * b:2 * b + 2, :].rearrange("p a d -> p (a d)"), ident[:])
                    last.then_inc(front_mm.sem, 1)

            def scores(c, u, t):
                if t == 0:
                    pe.wait_ge(front_ev.sem, front_ev.at(c, 3))
                    pe.wait_ge(prepared.sem, prepared.at(c, 3 * ST + 3))
                for h in range(H):
                    n = t * H + h
                    r = slice(64 * (h % 2), 64 * (h % 2) + 64)
                    pe.wait_ge(least.sem, least.at(c, 3 * (n - 1)))
                    pe.matmul(ps_s[n % 2][:, 0:X + keys(t)], qT[r, u, t, h // 2, :], kx[r, u, 0:X + keys(t)],
                              start=True, stop=True).then_inc(s_mm.sem, 1)

            def values(c, u, t):
                r = R * t
                bank = ps_t
                pe.wait_ge(mixing.sem, mixing.at(c, MIX * (t + 1)))
                pe.wait_ge(p_ev.sem, p_ev.at(c, r - 1))
                pe.sem_inc(passed, 1)
                pe.transpose(bank[r % 2][0:H * NB, 0:P], p_c[:, t, :, :].rearrange("p h n -> p (h n)"),
                             ident[:]).then_inc(p_tr.sem, 1)

                def turn_p(h):
                    i = r + 1 + h
                    pe.wait_ge(weighed.sem, weighed.at(c, 2 * H * t + min(2 * h + 3, 2 * H)))
                    pe.wait_ge(p_ev.sem, p_ev.at(c, i - 1))
                    for b in range(t + 1):
                        last = pe.transpose(bank[i % 2][:, b * P:(b + 1) * P], p_all[:, t, h, b * P:(b + 1) * P],
                                            ident[:])
                    last.then_inc(p_tr.sem, 1)

                turn_p(0)
                pe.wait_ge(p_ev.sem, p_ev.at(c, r + 1))
                pe.wait_ge(added.sem, added.at(c, t))
                pe.matmul(ps_o[:], p_cT[:], vc[:, u, :, :], start=True, stop=False,
                          skip_group_check=True).then_inc(o_mm.sem, 1)
                for h in range(H):
                    if h + 1 < H:
                        turn_p(h + 1)
                    pe.wait_ge(p_ev.sem, p_ev.at(c, r + 2 + h))
                    for b in range(t + 1):
                        last = pe.matmul(ps_o[:, h, :], pT[:, h % 2, b, :], v[:, u, b, :], start=False,
                                         stop=(h == H - 1 and b == t), skip_group_check=True)
                    last.then_inc(o_mm.sem, 1)
                pe.wait_ge(o_ev.sem, o_ev.at(c, t + 1))
                i = r + 1 + H
                pe.wait_ge(p_ev.sem, p_ev.at(c, i - 1))
                for b in range(HP):
                    last = pe.transpose(bank[i % 2][:, b * P:(b + 1) * P],
                                        o[:, 2 * b:2 * b + 2, :].rearrange("p a d -> p (a d)"), ident[:])
                last.then_inc(p_tr.sem, 1)
                pe.wait_ge(p_ev.sem, p_ev.at(c, i + 1))
                for b in range(HP):
                    last = pe.matmul(ps_o[:, 0:2, :], oT[:, b, :], y_w[:, b, :], start=(b == 0),
                                     stop=(b == HP - 1), skip_group_check=True)
                last.then_inc(o_mm.sem, 1)

            def main(c, u, f1, f2, f3):
                scores(c, u, 0)
                f1()
                scores(c, u, 1)
                f2()
                values(c, u, 0)
                f3()
                values(c, u, 1)

            in_pairs(pe, SEQS, [lambda c, u: norm.on_tensor(pe, c), project, turn], main)

        @block.scalar
        def _(act):
            norm.start(nc, act=act)
            for s in (copied, front_ev, exped, mix_exp, p_ev, o_ev):
                s.start(act)

            def project(c, u):
                act.wait_ge(front_mm.sem, front_mm.at(c - 1, 4))
                act.wait_ge(kv_mm.sem, kv_mm.at(c, 1))
                for t in range(ST):
                    act.activation(qk[:, t, H, :], ps_kv[:, t * P:t * P + HD], ACT.Copy).then_inc(copied.sem, 1)
                    act.activation(v[:, u, t, :], ps_kv[:, t * P + HD:(t + 1) * P], ACT.Copy).then_inc(copied.sem, 1)
                    act.wait_ge(q_mm.sem, q_mm.at(c, t + 1))
                    act.activation(qk[:, t, 0:H, :], ps_q[:], ACT.Copy).then_inc(copied.sem, 1)
                    act.wait_ge(copied.sem, copied.at(c, 4 * t + 3))
                    act.activation(sq[:, t, :, :], qk[:, t, :, :], ACT.Square).then_inc(copied.sem, 1)

            def turn(c, u):
                act.wait_ge(front_mm.sem, front_mm.at(c, 2))
                act.activation(kx[:, u, X:X + SEQ], ps_f[:, 0:SEQ], ACT.Copy).then_inc(front_ev.sem, 1)
                for t in range(ST):
                    act.wait_ge(front_mm.sem, front_mm.at(c, 3 + t))
                    act.activation(qT[:, u, t, :, :], ps_f[:].rearrange("p (b q) -> p b q", b=HP),
                                   ACT.Copy).then_inc(front_ev.sem, 1)

            def scores(c, u, t):
                for h in range(H):
                    n = t * H + h
                    act.wait_ge(least.sem, least.at(c, 3 * n + 2))
                    act.activation(p_all[:, t, h, 0:keys(t)], s_all[:, n % 2, 0:keys(t)], ACT.Exp,
                                   bias=low_all[:, t, h:h + 1], scale=-1.0,
                                   accum_out=total[:, t, 2, h:h + 1]).then_inc(exped.sem, 1)
                    act.wait_ge(least.sem, least.at(c, 3 * n + 3))
                    act.activation(p_win[:, t, h, 0:reach(t)[1]], s_win[:, n % 2, 0:reach(t)[1]], ACT.Exp,
                                   bias=low_win[:, t, h:h + 1], scale=-1.0,
                                   accum_out=total[:, t, 3, h:h + 1]).then_inc(exped.sem, 1)

            def mix(c, u, t):
                act.wait_ge(mixing.sem, mixing.at(c, MIX * t + 2))
                act.activation(e_c[:], e_c[:], ACT.Exp).then_inc(mix_exp.sem, 1)
                act.activation(sig[:], cg[:, t, :, A0.GATE:A0.GATE + 3], ACT.Exp).then_inc(mix_exp.sem, 1)
                act.wait_ge(mixing.sem, mixing.at(c, MIX * t + 3))
                act.activation(e_sink[:], e_sink[:], ACT.Exp).then_inc(mix_exp.sem, 1)

            def values(c, u, t):
                bank = ps_t
                r = R * t
                act.wait_ge(p_tr.sem, p_tr.at(c, r + 1))
                act.activation(p_cT[:], bank[r % 2][0:H * NB, 0:P], ACT.Copy).then_inc(p_ev.sem, 1)
                for h in range(H):
                    i = r + 1 + h
                    act.wait_ge(p_tr.sem, p_tr.at(c, i + 1))
                    act.wait_ge(o_mm.sem, o_mm.at(c, i - 1))
                    act.activation(pT[:, h % 2, 0:t + 1, :],
                                   bank[i % 2][:, 0:keys(t)].rearrange("p (b q) -> p b q", b=t + 1),
                                   ACT.Copy).then_inc(p_ev.sem, 1)
                act.wait_ge(o_mm.sem, o_mm.at(c, r + 1 + H))
                act.activation(o[:], ps_o[:], ACT.Copy).then_inc(o_ev.sem, 1)
                i = r + 1 + H
                act.wait_ge(p_tr.sem, p_tr.at(c, i + 1))
                act.activation(oT[:], bank[i % 2][:].rearrange("p (b q) -> p b q", b=HP),
                               ACT.Copy).then_inc(p_ev.sem, 1)

            def main(c, u, f1, f2, f3):
                scores(c, u, 0)
                mix(c, u, 0)
                f1()
                scores(c, u, 1)
                f2()
                mix(c, u, 1)
                values(c, u, 0)
                f3()
                values(c, u, 1)

            in_pairs(act, SEQS, [lambda c, u: norm.on_scalar(act, c, u, (q_mm.sem, q_mm.at(c - 2, ST))),
                                 project, turn], main)

        @block.vector
        def _(dve):
            norm.start(nc, dve=dve)
            for s in (prepared, least, mixing, weighed, added):
                s.start(dve)

            def first(c, u):
                norm.on_vector(dve, c)
                norm.on_vector_scale(dve, c)

            def project(c, u):
                for t in range(ST):
                    dve.wait_ge(copied.sem, copied.at(c, 4 * t + 4))
                    dve.tensor_reduce(ss[:, t, :], sq[:, t, :, :], AX_X, ALU.add).then_inc(prepared.sem, 1)
                for t in range(ST):
                    dve.wait_ge(turned.sem, turned.at(c, 2 * t + 2))
                    dve.tensor_tensor(qk[:, t, :, :], qk[:, t, :, :],
                                      rms[:, t, :].unsqueeze(2).to_broadcast([P, H + 1, HD]),
                                      ALU.mult).then_inc(prepared.sem, 1)
                for t in range(ST):
                    dve.wait_ge(turned.sem, turned.at(c, 2 * ST + 4 * (t + 1)))
                    dve.tensor_tensor(kd[:, t, :, :], qk[:, t, H:H + 1, :].to_broadcast([P, 2, HD]), gain_qk[:],
                                      ALU.mult).then_inc(prepared.sem, 1)
                dve.wait_ge(front_mm.sem, front_mm.at(c, 1))
                dve.tensor_tensor(vc[:, u, :, :],
                                  ps_kv[0:H * NB, 2 * P:2 * P + HD].unsqueeze(1).to_broadcast([H * NB, H, HD]),
                                  diagonal[:].unsqueeze(2).to_broadcast([H * NB, H, HD]),
                                  ALU.mult).then_inc(prepared.sem, 1)

            def turn(c, u):
                dve.wait_ge(front_ev.sem, front_ev.at(c, 1))
                dve.tensor_reduce(kc[:], kx[:, u, X:X + SEQ].rearrange("p (n k) -> p n k", n=NB), AX_X,
                                  ALU.add).then_inc(prepared.sem, 1)
                dve.wait_ge(prepared.sem, prepared.at(c, 3 * ST + 2))
                dve.tensor_scalar(kx[:, u, 0:NB], kc[:], 1.0 / A0.CR, None, ALU.mult).then_inc(prepared.sem, 1)

            def scores(c, u, t):
                k0, count, col = reach(t)
                for h in range(H):
                    n = t * H + h
                    dve.wait_ge(s_mm.sem, s_mm.at(c, n + 1))
                    dve.wait_ge(exped.sem, exped.at(c, 2 * (n - 1)))
                    dve.tensor_tensor(cg[:, t, h, :], ps_s[n % 2][:, 0:C], extra[:, t, h, :],
                                      ALU.add).then_inc(least.sem, 1)
                    dve.tensor_tensor_reduce(s_all[:, n % 2, 0:keys(t)], ps_s[n % 2][:, X:X + keys(t)],
                                             causal[:, P * t:P * t + keys(t)], 1.0, 3.0e38, ALU.add, ALU.min,
                                             low_all[:, t, h:h + 1]).then_inc(least.sem, 1)
                    dve.tensor_tensor_reduce(s_win[:, n % 2, 0:count], ps_s[n % 2][:, X + k0:X + k0 + count],
                                             window[:, col:col + count], 1.0, extra[:, t, h, A0.SINK:A0.SINK + 1],
                                             ALU.add, ALU.min, low_win[:, t, h:h + 1]).then_inc(least.sem, 1)

            def mix(c, u, t):
                k = MIX * t

                def step(ins):
                    nonlocal k
                    k += 1
                    ins.then_inc(mixing.sem, 1)

                def settled():
                    dve.wait_ge(mixing.sem, mixing.at(c, k))

                def wide(a, n):
                    return a.unsqueeze(2).to_broadcast([P, H, n])

                dve.wait_ge(least.sem, least.at(c, 3 * H * (t + 1)))
                step(dve.tensor_reduce(low_c[:], cg[:, t, :, 0:NB + 1], AX_X, ALU.min))
                settled()
                step(dve.tensor_tensor(e_c[:], wide(low_c[:], NB + 1), cg[:, t, :, 0:NB + 1], ALU.subtract))
                step(dve.tensor_tensor(e_sink[:], sink[:], low_win[:, t, :], ALU.add))
                dve.wait_ge(mix_exp.sem, mix_exp.at(c, 3 * t + 2))
                step(dve.tensor_scalar(sig[:], sig[:], 1.0, None, ALU.add))
                settled()
                step(dve.reciprocal(sig[:], sig[:]))
                settled()
                step(dve.tensor_reduce(total[:, t, 0, :], sig[:], AX_X, ALU.add))
                settled()
                step(dve.tensor_scalar(total[:, t, 0, :], total[:, t, 0, :], 1e-6, None, ALU.max))
                step(dve.tensor_reduce(total[:, t, 1, :], e_c[:], AX_X, ALU.add))
                dve.wait_ge(mix_exp.sem, mix_exp.at(c, 3 * t + 3))
                dve.wait_ge(exped.sem, exped.at(c, 2 * H * (t + 1)))
                step(dve.tensor_tensor(total[:, t, 3, :], total[:, t, 3, :], e_sink[:], ALU.add))
                settled()
                step(dve.reciprocal(inverse[:], total[:, t, :, :]))
                settled()
                step(dve.tensor_tensor(ratio[:], inverse[:, 1:4, :], inverse[:, 0:1, :].to_broadcast([P, 3, H]),
                                       ALU.mult))
                settled()
                step(dve.tensor_tensor(factor[:, t, :, :], ratio[:], sig[:].rearrange("p h g -> p g h"), ALU.mult))
                settled()
                step(dve.scalar_tensor_tensor(p_c[:, t, :, :], e_c[:, :, 0:NB], any_block[:, t:t + 1],
                                              wide(factor[:, t, 0, :], NB), ALU.mult, ALU.mult))
                assert k == MIX * (t + 1)

            def weigh(c, u, t):
                k0, count, _ = reach(t)

                def window_part(h):
                    dve.wait_ge(weighed.sem, weighed.at(c, 2 * H * t + max(2 * h, 1)))
                    dve.scalar_tensor_tensor(p_all[:, t, h, k0:k0 + count], p_win[:, t, h, 0:count],
                                             factor[:, t, 2, h:h + 1], p_all[:, t, h, k0:k0 + count],
                                             ALU.mult, ALU.add).then_inc(weighed.sem, 1)

                dve.wait_ge(mixing.sem, mixing.at(c, MIX * (t + 1)))
                for h in range(H):
                    dve.tensor_scalar(p_all[:, t, h, 0:keys(t)], p_all[:, t, h, 0:keys(t)],
                                      factor[:, t, 1, h:h + 1], None, ALU.mult).then_inc(weighed.sem, 1)
                    if h >= 1:
                        window_part(h - 1)
                    if t == 1 and h == H // 2:
                        finish(c, u, 0)
                window_part(H - 1)

            def finish(c, u, t):
                dve.wait_ge(o_mm.sem, o_mm.at(c, R * (t + 1)))
                rows = x[:, c * ST + t, :]
                dve.tensor_tensor(rows, ps_o[:, 0:2, :].rearrange("p a d -> p (a d)"), rows,
                                  ALU.add).then_inc(added.sem, 1)

            def main(c, u, f1, f2, f3):
                scores(c, u, 0)
                mix(c, u, 0)
                f1()
                scores(c, u, 1)
                f2()
                mix(c, u, 1)
                weigh(c, u, 0)
                f3()
                weigh(c, u, 1)
                finish(c, u, 1)

            in_pairs(dve, SEQS, [first, project, turn], main)

        ctx.clear(nc)


def single_attention(nc, x, ident, w):
    HD = D
    with Phase() as ctx:
        def sb(n, shape):
            return ctx.enter_context(nc.sbuf_tensor(f"one_{n}", shape, F32))

        def ps(n, shape):
            return ctx.enter_context(nc.psum_tensor(f"one_{n}", shape, F32))

        def sem(n):
            return ctx.semaphore(nc, f"one_{n}")

        def signal(n, per):
            return Signal(sem(n), per)

        ps_qk = ps("ps_qk", [P, 2, SEQ])
        ps_v = ps("ps_v", [P, ST, HD])
        ps_s = [ps(f"ps_s{i}", [P, SEQ]) for i in range(2)]
        ps_t = ps("ps_t", [P, SEQ])
        ps_o = ps("ps_o", [P, P])
        ps_y = ps("ps_y", [P, D])
        norm = Norm(nc, ctx, "one", x, ident, ST)

        wq, wk, wv, wo = (sb(n, [P, P]) for n in ("wq", "wk", "wv", "wo"))
        bq, bk = sb("bq", [P, 1]), sb("bk", [P, 1])
        bv, bo = sb("bv", [P, HD]), sb("bo", [P, D])
        causal = sb("causal", [P, P + SEQ])
        qT = sb("qT", [P, 2, SEQ])
        kT = sb("kT", [P, 2, SEQ])
        v = sb("v", [P, 2, ST, HD])
        s_all = sb("s_all", [P, ST, SEQ])
        low = sb("low", [P, ST])
        e = sb("e", [P, ST, SEQ])
        total = sb("total", [P, ST])
        inverse = sb("inverse", [P, ST])
        eT = sb("eT", [P, ST, P])
        oT = sb("oT", [P, P])
        loaded = sem("loaded")
        proj_mm = signal("proj_mm", 2)
        biased = signal("biased", 2 + ST)
        s_mm = signal("s_mm", ST)
        least = signal("least", ST)
        exped = signal("exped", ST)
        inverted = signal("inverted", ST)
        e_tr = signal("e_tr", ST)
        e_ev = signal("e_ev", ST)
        o_mm = signal("o_mm", ST)
        o_ev = signal("o_ev", ST)
        y_mm = signal("y_mm", ST)
        added = signal("added", 2 * ST)
        pieces = [(wq, "b_wq"), (wk, "b_wk"), (wv, "b_wv"), (wo, "b_wo"), (bq, "b_bq"), (bk, "b_bk"),
                  (bv, "b_bv"), (bo, "b_bo"), (causal, "causal")]

        with nc.Block() as block:
            @block.sync
            def _(sp):
                for to, of in pieces:
                    sp.dma_start(to[:], w[of]).then_inc(loaded, 16)
                sp.wait_ge(loaded, 16 * len(pieces))

        block = ctx.main_block(nc)

        @block.gpsimd
        def _(pool):
            norm.start(nc, pool=pool)
            in_pairs(pool, SEQS, [lambda c, u: norm.on_pool(pool, c)], lambda c, u, f: f())

        @block.tensor
        def _(pe):
            norm.start(nc, pe=pe)
            for s in (proj_mm, s_mm, e_tr, o_mm, y_mm):
                s.start(pe)

            def project(c, u):
                pe.wait_ge(norm.xT_done.sem, norm.xT_done.at(c, 1))
                pe.wait_ge(biased.sem, biased.at(c - 1, 2 + ST))
                pe.matmul(ps_qk[:, 0, :], wq[:], norm.xT[:, u, :], start=True, stop=True)
                pe.matmul(ps_qk[:, 1, :], wk[:], norm.xT[:, u, :], start=True, stop=True).then_inc(proj_mm.sem, 1)
                for t in range(ST):
                    last = pe.matmul(ps_v[:, t, :], norm.xT[:, u, t * P:(t + 1) * P], wv[:], start=True, stop=True)
                last.then_inc(proj_mm.sem, 1)

            def main(c, u, first, second):
                pe.wait_ge(biased.sem, biased.at(c, 2 + ST))
                for t in range(ST):
                    pe.wait_ge(least.sem, least.at(c - 1, t + 1))
                    pe.matmul(ps_s[t][:, 0:(t + 1) * P], qT[:, u, t * P:(t + 1) * P], kT[:, u, 0:(t + 1) * P],
                              start=True, stop=True).then_inc(s_mm.sem, 1)
                first()
                second()
                for t in range(ST):
                    pe.wait_ge(exped.sem, exped.at(c, t + 1))
                    pe.wait_ge(e_ev.sem, e_ev.at(c, t))
                    for b in range(t + 1):
                        last = pe.transpose(ps_t[:, b * P:(b + 1) * P], e[:, t, b * P:(b + 1) * P], ident[:])
                    last.then_inc(e_tr.sem, 1)
                    pe.wait_ge(e_ev.sem, e_ev.at(c, t + 1))
                    pe.wait_ge(o_ev.sem, o_ev.at(c, t))
                    for b in range(t + 1):
                        last = pe.matmul(ps_o[:], v[:, u, b, :], eT[:, b, :], start=(b == 0), stop=(b == t))
                    last.then_inc(o_mm.sem, 1)
                    pe.wait_ge(o_ev.sem, o_ev.at(c, t + 1))
                    pe.wait_ge(added.sem, added.at(c, 2 * t))
                    pe.matmul(ps_y[:], oT[:], wo[:], start=True, stop=True).then_inc(y_mm.sem, 1)

            in_pairs(pe, SEQS, [lambda c, u: norm.on_tensor(pe, c), project], main)

        @block.scalar
        def _(act):
            norm.start(nc, act=act)
            for s in (exped, e_ev, o_ev):
                s.start(act)

            def main(c, u, first):
                for t in range(ST):
                    act.wait_ge(least.sem, least.at(c, t + 1))
                    act.activation(e[:, t, 0:(t + 1) * P], s_all[:, t, 0:(t + 1) * P], ACT.Exp, bias=low[:, t:t + 1],
                                   scale=-1.0, accum_out=total[:, t:t + 1]).then_inc(exped.sem, 1)
                first()
                for t in range(ST):
                    act.wait_ge(e_tr.sem, e_tr.at(c, t + 1))
                    act.activation(eT[:, 0:t + 1, :], ps_t[:, 0:(t + 1) * P].rearrange("p (b q) -> p b q", b=t + 1),
                                   ACT.Copy).then_inc(e_ev.sem, 1)
                    act.wait_ge(o_mm.sem, o_mm.at(c, t + 1))
                    act.activation(oT[:], ps_o[:], ACT.Copy).then_inc(o_ev.sem, 1)

            in_pairs(act, SEQS, [lambda c, u: norm.on_scalar(act, c, u, (proj_mm.sem, proj_mm.at(c - 2, 2)))], main)

        @block.vector
        def _(dve):
            norm.start(nc, dve=dve)
            for s in (biased, least, inverted, added):
                s.start(dve)

            def first(c, u):
                norm.on_vector(dve, c)
                norm.on_vector_scale(dve, c)

            def project(c, u):
                dve.wait_ge(proj_mm.sem, proj_mm.at(c, 1))
                dve.tensor_scalar(qT[:, u, :], ps_qk[:, 0, :], bq[:, 0:1], -(float(HD) ** -0.5), ALU.add,
                                  ALU.mult).then_inc(biased.sem, 1)
                dve.tensor_scalar(kT[:, u, :], ps_qk[:, 1, :], bk[:, 0:1], None, ALU.add).then_inc(biased.sem, 1)
                dve.wait_ge(proj_mm.sem, proj_mm.at(c, 2))
                for t in range(ST):
                    dve.tensor_tensor(v[:, u, t, :], ps_v[:, t, :], bv[:], ALU.add).then_inc(biased.sem, 1)

            def main(c, u, f1, f2):
                for t in range(ST):
                    dve.wait_ge(s_mm.sem, s_mm.at(c, t + 1))
                    dve.sem_inc(norm.turns, 1)
                    dve.tensor_tensor_reduce(s_all[:, t, 0:(t + 1) * P], ps_s[t][:, 0:(t + 1) * P],
                                             causal[:, P * t:P * t + (t + 1) * P], 1.0, 3.0e38, ALU.add, ALU.min,
                                             low[:, t:t + 1]).then_inc(least.sem, 1)
                f1()
                f2()
                for t in range(ST):
                    dve.tensor_tensor(x[:, c * ST + t, :], x[:, c * ST + t, :], bo[:], ALU.add).then_inc(added.sem, 1)
                    dve.wait_ge(exped.sem, exped.at(c, t + 1))
                    dve.reciprocal(inverse[:, t:t + 1], total[:, t:t + 1]).then_inc(inverted.sem, 1)
                    dve.wait_ge(y_mm.sem, y_mm.at(c, t + 1))
                    dve.wait_ge(inverted.sem, inverted.at(c, t + 1))
                    dve.wait_ge(added.sem, added.at(c, 2 * t + 1))
                    dve.scalar_tensor_tensor(x[:, c * ST + t, :], ps_y[:], inverse[:, t:t + 1], x[:, c * ST + t, :],
                                             ALU.mult, ALU.add).then_inc(added.sem, 1)

            in_pairs(dve, SEQS, [first, project], main)

        ctx.clear(nc)


class G1:
    H, HD, KVH = 16, 64, 4
    HP = H // 2
    IN = 64
    REP = H // KVH
    OH = 8


def grouped_attention(nc, x, ident, w):
    H, HD, KVH, HP, IN, REP, OH = G1.H, G1.HD, G1.KVH, G1.HP, G1.IN, G1.REP, G1.OH
    F = 3 + HP // 2
    with Phase() as ctx:
        def sb(n, shape):
            return ctx.enter_context(nc.sbuf_tensor(f"grp_{n}", shape, F32))

        def ps(n, shape):
            return ctx.enter_context(nc.psum_tensor(f"grp_{n}", shape, F32))

        def sem(n):
            return ctx.semaphore(nc, f"grp_{n}")

        def signal(n, per):
            return Signal(sem(n), per)

        ps_f = ps("ps_f", [P, 512])
        ps_s = [ps(f"ps_s{i}", [P, SEQ]) for i in range(2)]
        ps_t = [ps(f"ps_t{i}", [P, 512]) for i in range(2)]
        ps_o = ps("ps_o", [P, OH, HD])
        ps_y = ps("ps_y", [P, D])
        ps_n = ps("ps_n", [P, 512])

        wq_in = sb("wq_in", [P, H, HD // 2, 2])
        wq = sb("wq", [P, H * HD])
        turn_a = sb("turn_a", [P, H, HD // 2])
        turn_b = sb("turn_b", [P, H, HD // 2])
        wk = sb("wk", [P, KVH, 2, HD])
        wv = sb("wv", [P, KVH * HD])
        wo = sb("wo", [P, HP, D])
        phase = sb("phase", [P, H])
        wave = sb("wave", [P, 2, H])
        steps = sb("steps", [P, 2, H])
        slope = sb("slope", [P, H])
        keys_at = sb("keys_at", [P, P + SEQ])
        causal = sb("causal", [P, P + SEQ])
        table = sb("table", [P, H, P + SEQ])

        kT = sb("kT", [P, 2, KVH, SEQ])
        v = sb("v", [P, 2, ST, KVH * HD])
        qT = sb("qT", [P, 2, HP, SEQ])
        s_all = sb("s_all", [P, 2, SEQ])
        low = sb("low", [P, ST, H])
        e = sb("e", [P, ST, H, SEQ])
        total = sb("total", [P, ST, H])
        bottom = sb("bottom", [P, ST, H])
        inverse = sb("inverse", [P, ST, H])
        eT = sb("eT", [P, 2, ST, P])
        o = sb("o", [P, OH, HD])
        oT = sb("oT", [P, OH // 2, P])

        loaded, waved, rotated, sloped, passed = (sem(n) for n in ("loaded", "waved", "rotated", "sloped", "passed"))
        front_mm = signal("front_mm", F)
        front_ev = signal("front_ev", F)
        U = ST * H
        s_mm = signal("s_mm", U)
        least = signal("least", U)
        exped = signal("exped", U)
        inverted = signal("inverted", 2 * ST)
        e_tr = signal("e_tr", U)
        e_ev = signal("e_ev", U)
        o_mm = signal("o_mm", U)
        HALVES = ST * H // OH
        o_ev = signal("o_ev", HALVES)
        o_tr = signal("o_tr", HALVES)
        oT_ev = signal("oT_ev", HALVES)
        y_mm = signal("y_mm", HALVES)
        norm = Norm(nc, ctx, "grp", x, ident, ST, ps=ps_n,
                    bank_free=lambda c: (oT_ev.sem, oT_ev.at(c - 2, HALVES)))
        added = signal("added", ST)
        pieces = [(wq_in[IN:P, :, :, :], w["c_wq"]), (wk[IN:P, :, :, :], w["c_wk"]), (wv[0:IN, :], w["c_wv"]),
                  (wo[:], w["c_wo"]), (phase[:], w["c_phase"]), (slope[:], w["c_slope"]),
                  (keys_at[:], w["keys_at"]), (causal[:], w["causal"])]

        with nc.Block() as block:
            @block.sync
            def _(sp):
                for to, of in pieces:
                    sp.dma_start(to, of).then_inc(loaded, 16)

            @block.scalar
            def _(act):
                act.wait_ge(loaded, 16 * len(pieces))
                act.activation(slope[:], slope[:], ACT.Exp).then_inc(sloped, 1)
                act.wait_ge(waved, 7)
                act.activation(wave[:], wave[:], ACT.Sin).then_inc(sloped, 1)

            @block.vector
            def _(dve):
                def step(ins, n):
                    ins.then_inc(waved, 1)
                    dve.wait_ge(waved, n)

                dve.wait_ge(loaded, 16 * len(pieces))
                step(dve.tensor_scalar(wave[:, 0, :], phase[:], 1.0, math.pi / 2, ALU.mult, ALU.add), 1)
                step(dve.tensor_copy(wave[:, 1, :], phase[:]), 2)
                step(dve.tensor_scalar(steps[:], wave[:], 1 / (2 * math.pi), ROUND, ALU.mult, ALU.add), 3)
                step(dve.tensor_scalar(steps[:], steps[:], ROUND, None, ALU.subtract), 4)
                step(dve.scalar_tensor_tensor(wave[:], steps[:], -TURN_HIGH, wave[:], ALU.mult, ALU.add), 5)
                step(dve.scalar_tensor_tensor(wave[:], steps[:], -TURN_LOW, wave[:], ALU.mult, ALU.add), 6)
                step(dve.tensor_scalar(wave[:], wave[:], HALF_TURN, -HALF_TURN, ALU.min, ALU.max), 7)
                dve.wait_ge(sloped, 2)
                step(dve.tensor_scalar(wave[:], wave[:], -(float(HD) ** -0.5), None, ALU.mult), 8)
                even, odd = wq_in[IN:P, :, :, 0], wq_in[IN:P, :, :, 1]
                to = wq[IN:P, :].rearrange("p (h d a) -> p h d a", h=H, a=2)
                cos, sin = (wave[IN:P, n, :].unsqueeze(2).to_broadcast([IN, H, HD // 2]) for n in range(2))
                a, b = turn_a[IN:P, :, :], turn_b[IN:P, :, :]
                step(dve.tensor_tensor(a, even, cos, ALU.mult), 9)
                step(dve.tensor_tensor(b, odd, sin, ALU.mult), 10)
                step(dve.tensor_tensor(to[:, :, :, 0], a, b, ALU.subtract), 11)
                step(dve.tensor_tensor(a, even, sin, ALU.mult), 12)
                step(dve.tensor_tensor(b, odd, cos, ALU.mult), 13)
                step(dve.tensor_tensor(to[:, :, :, 1], a, b, ALU.add), 14)
                for h in range(H):
                    dve.scalar_tensor_tensor(table[:, h, :], keys_at[:], slope[:, h:h + 1], causal[:],
                                             ALU.mult, ALU.add)

        block = ctx.main_block(nc)

        def keys(t):
            return (t + 1) * P

        FIRST = 5

        @block.gpsimd
        def _(pool):
            norm.start(nc, pool=pool)
            in_pairs(pool, SEQS, [lambda c, u: norm.on_pool(pool, c)], lambda c, u, f: f())

        @block.tensor
        def _(pe):
            norm.start(nc, pe=pe)
            for s in (front_mm, s_mm, e_tr, o_mm, o_tr, y_mm):
                s.start(pe)

            def project(c, u, n):
                if n == 0:
                    pe.wait_ge(norm.xT_done.sem, norm.xT_done.at(c, 1))
                pe.wait_ge(front_ev.sem, front_ev.at(c, n))
                for i in range(2):
                    half = ps_f[:, i * SEQ:(i + 1) * SEQ]
                    if n < 2:
                        last = pe.matmul(half, wk[IN:P, 2 * n + i, :, :].rearrange("p a d -> p (a d)"),
                                         norm.xT[IN:P, u, :], start=True, stop=True)
                    elif n == 2:
                        last = pe.matmul(half, norm.xT[0:IN, u, i * P:(i + 1) * P], wv[0:IN, :],
                                         start=True, stop=True)
                    else:
                        b = 2 * (n - 3) + i
                        last = pe.matmul(half, wq[IN:P, b * P:(b + 1) * P], norm.xT[IN:P, u, :],
                                         start=True, stop=True)
                last.then_inc(front_mm.sem, 1)

            def score(c, u, t, h):
                n = t * H + h
                r = slice(64 * (h % 2), 64 * (h % 2) + 64)
                if n == 0:
                    pe.wait_ge(front_ev.sem, front_ev.at(c, F))
                pe.wait_ge(least.sem, least.at(c, n - 1))
                pe.matmul(ps_s[n % 2][:, 0:keys(t)], qT[r, u, h // 2, t * P:(t + 1) * P],
                          kT[r, u, h // REP, 0:keys(t)], start=True, stop=True).then_inc(s_mm.sem, 1)

            def turn_e(c, t, h):
                n = t * H + h
                pe.wait_ge(exped.sem, exped.at(c, n + 1))
                pe.wait_ge(e_ev.sem, e_ev.at(c, n - 1))
                for b in range(t + 1):
                    last = pe.transpose(ps_t[n % 2][:, b * P:(b + 1) * P], e[:, t, h, b * P:(b + 1) * P],
                                        ident[:])
                last.then_inc(e_tr.sem, 1)

            def sum_values(c, u, t, h):
                n = t * H + h
                pe.wait_ge(e_ev.sem, e_ev.at(c, n + 1))
                if h % OH == 0:
                    pe.wait_ge(o_ev.sem, o_ev.at(c, n // OH))
                for b in range(t + 1):
                    g = h // REP
                    last = pe.matmul(ps_o[:, h % OH, :], eT[:, n % 2, b, :], v[:, u, b, g * HD:(g + 1) * HD],
                                     start=(b == 0), stop=(b == t))
                last.then_inc(o_mm.sem, 1)

            def turn_rows(c, m):
                pe.wait_ge(o_ev.sem, o_ev.at(c, m + 1))
                pe.wait_ge(oT_ev.sem, oT_ev.at(c, m))
                pe.wait_ge(norm.xT_done.sem, norm.xT_done.at(c + 1, 1))
                for b in range(OH // 2):
                    last = pe.transpose(ps_n[:, b * P:(b + 1) * P],
                                        o[:, 2 * b:2 * b + 2, :].rearrange("p a d -> p (a d)"), ident[:])
                last.then_inc(o_tr.sem, 1)

            def project_rows(c, t, half):
                m = t * (H // OH) + half
                pe.wait_ge(oT_ev.sem, oT_ev.at(c, m + 1))
                if half == 0:
                    pe.wait_ge(added.sem, added.at(c, t))
                for b in range(OH // 2):
                    last = pe.matmul(ps_y[:], oT[:, b, :], wo[:, half * (OH // 2) + b, :],
                                     start=(half == 0 and b == 0), stop=(half == 1 and b == OH // 2 - 1))
                last.then_inc(y_mm.sem, 1)

            def beside(sc, su, st, c, u, t):
                turn_e(c, t, 0)
                score(sc, su, st, 0)
                for h in range(H):
                    if h + 1 < H:
                        turn_e(c, t, h + 1)
                        score(sc, su, st, h + 1)
                    if t == 0 and h == FIRST - 2:
                        norm.on_tensor(pe, c + 1)
                    if t == 0 and FIRST <= h < FIRST + F:
                        project(c + 1, 1 - u, h - FIRST)
                    sum_values(c, u, t, h)
                    if h == OH:
                        turn_rows(c, 2 * t)
                    if h == OH + 1:
                        project_rows(c, t, 0)
                turn_rows(c, 2 * t + 1)
                project_rows(c, t, 1)

            norm.on_tensor(pe, 0)
            for n in range(F):
                project(0, 0, n)
            for h in range(H):
                score(0, 0, 0, h)

            def main(c, u):
                beside(c, u, 1, c, u, 0)
                beside(c + 1, 1 - u, 0, c, u, 1)

            pairs(pe, main)

        @block.scalar
        def _(act):
            norm.start(nc, act=act)
            for s in (exped, e_ev):
                s.start(act)

            def weigh(c, t, h):
                n = t * H + h
                act.wait_ge(least.sem, least.at(c, n + 1))
                act.activation(e[:, t, h, 0:keys(t)], s_all[:, n % 2, 0:keys(t)], ACT.Exp,
                               bias=low[:, t, h:h + 1], scale=-1.0,
                               accum_out=total[:, t, h:h + 1]).then_inc(exped.sem, 1)

            def turned(c, t, h):
                n = t * H + h
                act.wait_ge(e_tr.sem, e_tr.at(c, n + 1))
                act.wait_ge(o_mm.sem, o_mm.at(c, n - 1))
                act.activation(eT[:, n % 2, 0:t + 1, :],
                               ps_t[n % 2][:, 0:keys(t)].rearrange("p (b q) -> p b q", b=t + 1),
                               ACT.Copy).then_inc(e_ev.sem, 1)

            def normal(c, u):
                norm.on_scalar(act, c, u, (front_mm.sem, front_mm.at(c - 2, F)))

            def beside(sc, st, c, u, t):
                for h in range(H):
                    turned(c, t, h)
                    weigh(sc, st, h)
                    if t == 0 and h == FIRST - 2:
                        normal(c + 1, 1 - u)

            normal(0, 0)
            for h in range(H):
                weigh(0, 0, h)

            def main(c, u):
                beside(c, 1, c, u, 0)
                beside(c + 1, 0, c, u, 1)

            pairs(act, main)

        @block.vector
        def _(dve):
            norm.start(nc, dve=dve)
            for s in (front_ev, least, inverted, o_ev, oT_ev, added):
                s.start(dve)

            def projected(c, u, n):
                if n < 2:
                    to = kT[:, u, 2 * n:2 * n + 2, :]
                elif n == 2:
                    to = v[:, u, :, :]
                else:
                    to = qT[:, u, 2 * (n - 3):2 * (n - 3) + 2, :]
                dve.wait_ge(front_mm.sem, front_mm.at(c, n + 1))
                dve.tensor_copy(to.rearrange("p a k -> p (a k)"), ps_f[:]).then_inc(front_ev.sem, 1)

            def mask(c, t, h):
                n = t * H + h
                dve.wait_ge(s_mm.sem, s_mm.at(c, n + 1))
                dve.wait_ge(exped.sem, exped.at(c, n - 1))
                dve.sem_inc(norm.turns, 1)
                dve.tensor_tensor_reduce(s_all[:, n % 2, 0:keys(t)], ps_s[n % 2][:, 0:keys(t)],
                                         table[:, h, P * t:P * t + keys(t)], 1.0, 3.0e38, ALU.add, ALU.min,
                                         low[:, t, h:h + 1]).then_inc(least.sem, 1)

            def invert(c, t):
                dve.wait_ge(exped.sem, exped.at(c, H * (t + 1)))
                dve.sem_inc(norm.turns, 1)
                dve.tensor_scalar(bottom[:, t, :], total[:, t, :], 1.0, None, ALU.add).then_inc(inverted.sem, 1)
                dve.wait_ge(inverted.sem, inverted.at(c, 2 * t + 1))
                dve.reciprocal(inverse[:, t, :], bottom[:, t, :]).then_inc(inverted.sem, 1)

            def divide(c, t, half):
                m = t * (H // OH) + half
                dve.wait_ge(inverted.sem, inverted.at(c, 2 * t + 2))
                dve.wait_ge(o_mm.sem, o_mm.at(c, (m + 1) * OH))
                dve.wait_ge(o_tr.sem, o_tr.at(c, m))
                dve.tensor_tensor(o[:], ps_o[:],
                                  inverse[:, t, half * OH:(half + 1) * OH].unsqueeze(2).to_broadcast([P, OH, HD]),
                                  ALU.mult).then_inc(o_ev.sem, 1)

            def rows_turned(c, m):
                dve.wait_ge(o_tr.sem, o_tr.at(c, m + 1))
                dve.wait_ge(y_mm.sem, y_mm.at(c, m))
                dve.tensor_copy(oT[:].rearrange("p b q -> p (b q)"), ps_n[:]).then_inc(oT_ev.sem, 1)

            def beside(sc, st, c, u, t):
                if t == 0:
                    norm.on_vector(dve, c + 1)
                for h in range(H):
                    mask(sc, st, h)
                    if h == 0:
                        invert(c, t)
                    if t == 0 and h == 1:
                        norm.on_vector_scale(dve, c + 1)
                    if h == OH:
                        divide(c, t, 0)
                    if h == OH + 1:
                        rows_turned(c, 2 * t)
                    if t == 0 and FIRST <= h < FIRST + F:
                        projected(c + 1, 1 - u, h - FIRST)
                divide(c, t, 1)
                rows_turned(c, 2 * t + 1)
                dve.wait_ge(y_mm.sem, y_mm.at(c, (H // OH) * (t + 1)))
                dve.tensor_tensor(x[:, c * ST + t, :], ps_y[:], x[:, c * ST + t, :], ALU.add).then_inc(added.sem, 1)

            norm.on_vector(dve, 0)
            norm.on_vector_scale(dve, 0)
            for n in range(F):
                projected(0, 0, n)
            for h in range(H):
                mask(0, 0, h)

            def main(c, u):
                beside(c, 1, c, u, 0)
                beside(c + 1, 0, c, u, 1)

            pairs(dve, main)

        ctx.clear(nc)


class H1:
    LAYERS, H, HD = 4, 16, 8
    WRAP = D + HD
    HB = 4 * D // P


def spectral_layers(nc, rows_x, ident, w):
    HD, WRAP, HB = H1.HD, H1.WRAP, H1.HB
    with Phase() as ctx:
        def sb(n, shape):
            return ctx.enter_context(nc.sbuf_tensor(f"spec_{n}", shape, F32))

        def ps(n, shape):
            return ctx.enter_context(nc.psum_tensor(f"spec_{n}", shape, F32))

        def sem(n):
            return ctx.semaphore(nc, f"spec_{n}")

        def signal(n, per):
            return Signal(sem(n), per)

        ps_n = ps("ps_n", [P, SEQ])
        ps_x = ps("ps_x", [P, 3, WRAP])
        ps_d = ps("ps_d", [P, 3, D])
        ps_w = ps("ps_w", [P, SEQ])
        ps_z = ps("ps_z", [P, SEQ])
        ps_y = ps("ps_y", [P, ST, D])
        ps_h = [ps(f"ps_h{i}", [P, 2, SEQ]) for i in range(2)]

        x = sb("y", [P, TILES + 3 * ST, D])
        ln = sb("ln", [P, 4])
        qkv_w = sb("qkv_w", [P, 3, WRAP])
        qkv_b = sb("qkv_b", [P, 3, WRAP])
        proj_w = sb("proj_w", [P, D])
        head_proj = sb("head_proj", [P, D])
        proj_b = sb("proj_b", [P, D])
        fc_w = sb("fc_w", [P, 4 * D])
        fc_b = sb("fc_b", [P, HB])
        mp_w = sb("mp_w", [P, HB, D])
        mp_b = sb("mp_b", [P, D])
        hartley = sb("hartley", [P, P])
        filt = sb("filt", [P, SEQ])
        quarter = sb("quarter", [P, 1])

        dT = sb("dT", [P, 2, SEQ])
        rows = sb("rows", [P, 2, ST, 3, WRAP])
        diff = sb("diff", [P, 2, ST, 3, D])
        cosine = sb("cosine", [P, 2, ST, 3, D])
        turns_of = sb("turns_of", [P, ST, 3, D])
        whole = sb("whole", [P, ST, 3, D])
        part = sb("part", [P, 8, ST, D])
        comp = sb("comp", [P, 4, ST, D])
        product = sb("product", [P, ST, D])
        wT = sb("wT", [P, SEQ])
        z = sb("z", [P, SEQ])
        hT = sb("hT", [P, HB, SEQ])

        tables = sem("tables")
        zeroed, loaded, made = sem("zeroed"), sem("loaded"), sem("made")
        norm_a = Norm(nc, ctx, "spec_a", x, ident, ST, ps=ps_n, gain=ln[:, 0:1], shift=ln[:, 1:2])
        norm_c = Norm(nc, ctx, "spec_c", x, ident, ST, ps=ps_n, gain=ln[:, 2:3], shift=ln[:, 3:4])
        norm_a.bank_free = lambda c: (norm_c.xT_done.sem, norm_c.xT_done.at(max(c - 3, -2) if isinstance(c, int)
                                                                            else c - 3, 1))
        norm_c.bank_free = lambda c: (norm_a.xT_done.sem, norm_a.xT_done.at(c + 2, 1))
        diffed = signal("diffed", 1)
        x_mm = signal("x_mm", ST)
        d_mm = signal("d_mm", ST)
        d_ev = signal("d_ev", ST)
        x_ev = signal("x_ev", ST)
        scaled = signal("scaled", 2)
        parted = signal("parted", 1)
        cosined = signal("cosined", 2)
        HAM = 35
        hamilton = signal("hamilton", HAM)
        w_mm = signal("w_mm", 1)
        w_ev = signal("w_ev", 1)
        z_mm = signal("z_mm", 1)
        filtered = signal("filtered", 1)
        y_mm = signal("y_mm", 1)
        m_mm = signal("m_mm", 1)
        bias_a = signal("bias_a", 1)
        bias_c = signal("bias_c", 1)
        y_add = signal("y_add", 1)
        m_add = signal("m_add", 1)
        h_mm = signal("h_mm", 2)
        h_ev = signal("h_ev", HB)

        row_stats, row_mv, row_rstd = sem("row_stats"), sem("row_mv"), sem("row_rstd")
        stats = sb("stats", [P, TILES, 6])
        mean_var = sb("mean_var", [P, TILES, 2])
        veps = sb("veps", [P, TILES])
        power = sb("power", [P, TILES])
        rstd = sb("rstd", [P, TILES])
        fixed = [(hartley[:], w["hartley"]), (filt[:], w["filter"])]
        with nc.Block() as block:
            @block.sync
            def _(sp):
                for to, of in fixed:
                    sp.dma_start(to, of).then_inc(tables, 16)
                sp.wait_ge(tables, 16 * len(fixed))

            @block.vector
            def _(dve):
                dve.memset(quarter[:], math.pi / 2)
                dve.memset(dT[:], 0.0)
                dve.memset(x[:, TILES:TILES + 3 * ST, :], 0.0)
                for t in range(TILES):
                    dve.bn_stats(stats[:, t, :], rows_x[:, t, :]).then_inc(row_stats, 1)
                for t in range(TILES):
                    dve.wait_ge(row_stats, t + 1)
                    dve.bn_aggr(mean_var[:, t, :], stats[:, t, :]).then_inc(row_mv, 1)
                dve.wait_ge(row_rstd, 3)
                for t in range(TILES):
                    dve.tensor_scalar(x[:, t, :], rows_x[:, t, :], mean_var[:, t, 0:1], rstd[:, t:t + 1],
                                      ALU.subtract, ALU.mult)

            @block.gpsimd
            def _(pool):
                pool.memset(power[:], -0.5).then_inc(row_rstd, 1)
                pool.wait_ge(row_mv, TILES)
                pool.tensor_scalar(veps[:], mean_var[:, :, 1], LN_EPS, None, ALU.add).then_inc(row_rstd, 1)
                pool.wait_ge(row_rstd, 2)
                pool.tensor_tensor(rstd[:], veps[:], power[:], ALU.pow).then_inc(row_rstd, 1)

        with nc.Fori(0, H1.LAYERS) as layer:
            layer_w = [(ln, "d_ln"), (qkv_w, "d_qkv_w"), (qkv_b, "d_qkv_b"), (proj_w, "d_proj_w"),
                       (proj_b, "d_proj_b"), (fc_w, "d_fc_w"), (fc_b, "d_fc_b"), (mp_w, "d_mp_w"), (mp_b, "d_mp_b")]
            with nc.Block() as block:
                @block.sync
                def _(sp):
                    for to, of in layer_w:
                        sp.dma_start(to[:], w[of][layer]).then_inc(loaded, 16)
                    sp.wait_ge(loaded, 16 * len(layer_w))

                @block.tensor
                def _(pe):
                    pe.wait_ge(loaded, 16 * len(layer_w))
                    pe.matmul(ps_y[:, 0, :], hartley[:], proj_w[:], start=True, stop=True).then_inc(made, 1)

                @block.vector
                def _(dve):
                    dve.wait_ge(made, 1)
                    dve.tensor_copy(head_proj[:], ps_y[:, 0, :])

            with nc.Block() as block:
                @block.gpsimd
                def _(pool):
                    norm_a.start(nc, pool=pool)
                    norm_c.start(nc, pool=pool)
                    diffed.start(pool)

                    def differences(c, u):
                        pool.wait_ge(norm_a.xT_done.sem, norm_a.xT_done.at(c, 1))
                        pool.wait_ge(d_mm.sem, d_mm.at(c - 2, ST))
                        pool.tensor_tensor(dT[:, u, 1:SEQ], norm_a.xT[:, u, 1:SEQ], norm_a.xT[:, u, 0:SEQ - 1],
                                           ALU.subtract).then_inc(diffed.sem, 1)

                    for c in range(2):
                        norm_a.on_pool(pool, c)
                        differences(c, c)
                    norm_a.on_pool(pool, 2)

                    def body(c, u):
                        differences(c + 2, u)
                        norm_c.on_pool(pool, c)
                        norm_a.on_pool(pool, c + 3)

                    pairs(pool, body)

                @block.tensor
                def _(pe):
                    norm_a.start(nc, pe=pe)
                    norm_c.start(nc, pe=pe)
                    for s in (x_mm, d_mm, w_mm, z_mm, y_mm, m_mm, h_mm):
                        s.start(pe)

                    def project(c, u, t):
                        pe.wait_ge(norm_a.xT_done.sem, norm_a.xT_done.at(c, 1))
                        pe.wait_ge(x_ev.sem, x_ev.at(c, t))
                        pe.matmul(ps_x[:], norm_a.xT[:, u, t * P:(t + 1) * P], qkv_w[:], start=True,
                                  stop=True).then_inc(x_mm.sem, 1)

                    def project_differences(c, u):
                        pe.wait_ge(diffed.sem, diffed.at(c, 1))
                        for t in range(ST):
                            pe.wait_ge(d_ev.sem, d_ev.at(c, t))
                            pe.matmul(ps_d[:], dT[:, u, t * P:(t + 1) * P], qkv_w[:, :, HD:WRAP], start=True,
                                      stop=True).then_inc(d_mm.sem, 1)

                    def turn(c):
                        pe.wait_ge(hamilton.sem, hamilton.at(c, HAM))
                        pe.wait_ge(w_ev.sem, w_ev.at(c - 1, 1))
                        for t in range(ST):
                            last = pe.transpose(ps_w[:, t * P:(t + 1) * P], product[:, t, :], ident[:])
                        last.then_inc(w_mm.sem, 1)

                    def to_frequencies(c):
                        pe.wait_ge(w_ev.sem, w_ev.at(c, 1))
                        pe.wait_ge(filtered.sem, filtered.at(c - 1, 1))
                        pe.matmul(ps_z[:], hartley[:], wT[:], start=True, stop=True).then_inc(z_mm.sem, 1)

                    def back(c):
                        pe.wait_ge(filtered.sem, filtered.at(c, 1))
                        pe.wait_ge(m_add.sem, m_add.at(c - 1, 1))
                        for t in range(ST):
                            last = pe.matmul(ps_y[:, t, :], z[:, t * P:(t + 1) * P], head_proj[:], start=True,
                                             stop=True)
                        last.then_inc(y_mm.sem, 1)

                    def hidden(c, u):
                        pe.wait_ge(norm_c.xT_done.sem, norm_c.xT_done.at(c, 1))
                        for i in range(2):
                            pe.wait_ge(h_ev.sem, h_ev.at(c - 1, 2 * i + 2))
                            for b in range(2 * i, 2 * i + 2):
                                last = pe.matmul(ps_h[i][:, b % 2, :], fc_w[:, b * P:(b + 1) * P],
                                                 norm_c.xT[:, u, :], start=True, stop=True)
                            last.then_inc(h_mm.sem, 1)

                    def out(c):
                        pe.wait_ge(h_ev.sem, h_ev.at(c, HB))
                        pe.wait_ge(y_add.sem, y_add.at(c, 1))
                        for t in range(ST):
                            for b in range(HB):
                                last = pe.matmul(ps_y[:, t, :], hT[:, b, t * P:(t + 1) * P], mp_w[:, b, :],
                                                 start=(b == 0), stop=(b == HB - 1))
                        last.then_inc(m_mm.sem, 1)

                    for c in range(2):
                        norm_a.on_tensor(pe, c)
                        project(c, c, 0)
                        project_differences(c, c)
                        project(c, c, 1)

                    def body(c, u):
                        turn(c)
                        to_frequencies(c)
                        norm_a.on_tensor(pe, c + 2)
                        back(c)
                        project(c + 2, u, 0)
                        project_differences(c + 2, u)
                        project(c + 2, u, 1)
                        norm_c.on_tensor(pe, c)
                        hidden(c, u)
                        out(c)

                    pairs(pe, body)

                @block.scalar
                def _(act):
                    norm_a.start(nc, act=act)
                    norm_c.start(nc, act=act)
                    for s in (d_ev, scaled, cosined, w_ev, h_ev):
                        s.start(act)

                    def normal(c, u):
                        act.wait_ge(diffed.sem, diffed.at(c - 2, 1))
                        norm_a.on_scalar(act, c, u, (x_mm.sem, x_mm.at(c - 2, ST)))

                    def differences(c, u):
                        act.wait_ge(hamilton.sem, hamilton.at(c - 2, HAM))
                        for t in range(ST):
                            act.wait_ge(d_mm.sem, d_mm.at(c, t + 1))
                            act.activation(diff[:, u, t, :, :], ps_d[:], ACT.Copy).then_inc(d_ev.sem, 1)

                    def turns(c, u):
                        act.wait_ge(x_ev.sem, x_ev.at(c, ST))
                        values = rows[:, u, :, :, HD:WRAP]
                        act.activation(turns_of[:], values, ACT.Copy, scale=1 / (2 * math.pi)).then_inc(scaled.sem, 1)
                        act.activation(whole[:], values, ACT.Copy, scale=1 / (2 * math.pi),
                                       bias=ROUND).then_inc(scaled.sem, 1)

                    def cosines(c, u):
                        act.wait_ge(parted.sem, parted.at(c, 1))
                        act.activation(whole[:], turns_of[:], ACT.Abs).then_inc(cosined.sem, 1)
                        act.wait_ge(cosined.sem, cosined.at(c, 1))
                        act.activation(cosine[:, u, :, :, :], whole[:], ACT.Sin, bias=quarter[:, 0:1],
                                       scale=-2 * math.pi).then_inc(cosined.sem, 1)

                    def turned(c):
                        act.wait_ge(w_mm.sem, w_mm.at(c, 1))
                        act.wait_ge(z_mm.sem, z_mm.at(c - 1, 1))
                        act.activation(wT[:], ps_w[:], ACT.Copy).then_inc(w_ev.sem, 1)

                    def gelu(c):
                        act.wait_ge(m_mm.sem, m_mm.at(c - 1, 1))
                        for b in range(HB):
                            act.wait_ge(h_mm.sem, h_mm.at(c, b // 2 + 1))
                            act.activation(hT[:, b, :], ps_h[b // 2][:, b % 2, :], ACT.Gelu,
                                           bias=fc_b[:, b:b + 1]).then_inc(h_ev.sem, 1)

                    for c in range(2):
                        normal(c, c)
                        differences(c, c)
                        turns(c, c)
                        cosines(c, c)

                    def body(c, u):
                        turned(c)
                        normal(c + 2, u)
                        differences(c + 2, u)
                        norm_c.on_scalar(act, c, u, (h_mm.sem, h_mm.at(c - 2, 2)))
                        turns(c + 2, u)
                        gelu(c)
                        cosines(c + 2, u)

                    pairs(act, body)

                @block.vector
                def _(dve):
                    norm_a.start(nc, dve=dve)
                    norm_c.start(nc, dve=dve)
                    for s in (x_ev, parted, hamilton, filtered, bias_a, bias_c, y_add, m_add):
                        s.start(dve)

                    def two(c):
                        return x[:, bass.ts(c, ST), :]

                    def wide(b):
                        return b[:].unsqueeze(1).to_broadcast([P, ST, D])

                    def scale_a(c):
                        norm_a.on_vector_scale(dve, c)
                        dve.wait_ge(norm_a.xn_done.sem, norm_a.xn_done.at(c, ST))
                        dve.tensor_tensor(two(c), two(c), wide(proj_b), ALU.add).then_inc(bias_a.sem, 1)

                    def add_bias(c, u, t):
                        dve.wait_ge(x_mm.sem, x_mm.at(c, t + 1))
                        dve.tensor_tensor(rows[:, u, t, :, :], ps_x[:], qkv_b[:], ALU.add).then_inc(x_ev.sem, 1)

                    def part_turns(c):
                        dve.wait_ge(scaled.sem, scaled.at(c, 2))
                        dve.scalar_tensor_tensor(turns_of[:].rearrange("p t a d -> p (t a d)"),
                                                 whole[:].rearrange("p t a d -> p (t a d)"), ROUND,
                                                 turns_of[:].rearrange("p t a d -> p (t a d)"), ALU.subtract,
                                                 ALU.subtract).then_inc(parted.sem, 1)

                    def part_of(u, i, n):
                        return (rows[:, u, :, n, HD:WRAP], diff[:, u, :, n, :], rows[:, u, :, n, 0:D],
                                cosine[:, u, :, n, :])[i]

                    SIGNS = [(ALU.subtract, ALU.add, ALU.subtract), (ALU.add, ALU.subtract, ALU.add),
                             (ALU.subtract, ALU.add, ALU.add), (ALU.add, ALU.subtract, ALU.subtract)]

                    def multiply(c, u, i):
                        done = 7 * i
                        p0 = 4 * (i % 2)
                        if i == 0:
                            dve.wait_ge(cosined.sem, cosined.at(c, 2))
                        for j in range(4):
                            dve.tensor_tensor(part[:, p0 + j, :, :], part_of(u, j, 0), part_of(u, i ^ j, 1),
                                              ALU.mult).then_inc(hamilton.sem, 1)
                        dve.wait_ge(hamilton.sem, hamilton.at(c, done + 2))
                        dve.tensor_tensor(part[:, p0, :, :], part[:, p0, :, :], part[:, p0 + 1, :, :],
                                          SIGNS[i][0]).then_inc(hamilton.sem, 1)
                        dve.wait_ge(hamilton.sem, hamilton.at(c, done + 4))
                        dve.tensor_tensor(part[:, p0 + 2, :, :], part[:, p0 + 2, :, :],
                                          part[:, p0 + 3, :, :], SIGNS[i][1]).then_inc(hamilton.sem, 1)
                        dve.wait_ge(hamilton.sem, hamilton.at(c, done + 6))
                        dve.tensor_tensor(comp[:, i, :, :], part[:, p0, :, :], part[:, p0 + 2, :, :],
                                          SIGNS[i][2]).then_inc(hamilton.sem, 1)

                    def multiply_last(c, u):
                        for i in range(4):
                            dve.wait_ge(hamilton.sem, hamilton.at(c, 7 * (i + 1)))
                            dve.tensor_tensor(comp[:, i, :, :], comp[:, i, :, :], part_of(u, i, 2),
                                              ALU.mult).then_inc(hamilton.sem, 1)
                        dve.wait_ge(hamilton.sem, hamilton.at(c, 30))
                        dve.tensor_tensor(comp[:, 0, :, :], comp[:, 0, :, :], comp[:, 1, :, :],
                                          ALU.subtract).then_inc(hamilton.sem, 1)
                        dve.wait_ge(hamilton.sem, hamilton.at(c, 32))
                        dve.tensor_tensor(comp[:, 2, :, :], comp[:, 2, :, :], comp[:, 3, :, :],
                                          ALU.add).then_inc(hamilton.sem, 1)
                        dve.wait_ge(w_mm.sem, w_mm.at(c - 1, 1))
                        dve.wait_ge(hamilton.sem, hamilton.at(c, 34))
                        dve.tensor_tensor(product[:], comp[:, 0, :, :], comp[:, 2, :, :],
                                          ALU.subtract).then_inc(hamilton.sem, 1)

                    def filter_rows(c):
                        dve.wait_ge(z_mm.sem, z_mm.at(c, 1))
                        dve.wait_ge(y_mm.sem, y_mm.at(c - 1, 1))
                        dve.tensor_tensor(z[:], ps_z[:], filt[:], ALU.mult).then_inc(filtered.sem, 1)

                    def add_attention(c):
                        dve.wait_ge(y_mm.sem, y_mm.at(c, 1))
                        dve.wait_ge(bias_a.sem, bias_a.at(c, 1))
                        dve.tensor_tensor(two(c), ps_y[:], two(c), ALU.add).then_inc(y_add.sem, 1)

                    def statistics_c(c):
                        dve.wait_ge(y_add.sem, y_add.at(c, 1))
                        dve.sem_inc(norm_c.turns, 1)
                        norm_c.on_vector(dve, c)

                    def scale_c(c):
                        norm_c.on_vector_scale(dve, c)
                        dve.wait_ge(norm_c.xn_done.sem, norm_c.xn_done.at(c, ST))
                        dve.tensor_tensor(two(c), two(c), wide(mp_b), ALU.add).then_inc(bias_c.sem, 1)

                    def add_gelu(c):
                        dve.wait_ge(m_mm.sem, m_mm.at(c, 1))
                        dve.wait_ge(bias_c.sem, bias_c.at(c, 1))
                        dve.tensor_tensor(two(c), ps_y[:], two(c), ALU.add).then_inc(m_add.sem, 1)

                    for c in range(2):
                        norm_a.on_vector(dve, c)
                        scale_a(c)
                        add_bias(c, c, 0)
                        add_bias(c, c, 1)
                        part_turns(c)
                    norm_a.on_vector(dve, 2)
                    for i in range(4):
                        multiply(0, 0, i)
                    multiply_last(0, 0)

                    def body(c, u):
                        scale_a(c + 2)
                        filter_rows(c)
                        multiply(c + 1, 1 - u, 0)
                        add_attention(c)
                        statistics_c(c)
                        add_bias(c + 2, u, 0)
                        multiply(c + 1, 1 - u, 1)
                        scale_c(c)
                        add_bias(c + 2, u, 1)
                        multiply(c + 1, 1 - u, 2)
                        part_turns(c + 2)
                        multiply(c + 1, 1 - u, 3)
                        norm_a.on_vector(dve, c + 3)
                        multiply_last(c + 1, 1 - u)
                        add_gelu(c)

                    pairs(dve, body)

            ctx.clear(nc)

        with nc.Block() as block:
            @block.vector
            def _(dve):
                dve.tensor_tensor(rows_x[:, 0:TILES, :], rows_x[:, 0:TILES, :], x[:, 0:TILES, :], ALU.add)

        ctx.clear(nc)


def build(nc, a, phases):
    with ExitStack() as ctx:
        def sb(n, shape, dt=F32):
            return ctx.enter_context(nc.sbuf_tensor(n, shape, dt))

        def sem(n):
            return ctx.enter_context(nc.semaphore(n))

        E, EH = 8, 512
        EB = EH // P
        F_H = 384
        FB = F_H // P
        x = sb("x", [P, TILES + CT, D])
        ident = sb("ident", [P, P])
        order = sb("order", [P, CT, E])
        moe_gate = sb("moe_gate", [P, E])
        moe_w1 = sb("moe_w1", [P, E * EH])
        moe_w3 = sb("moe_w3", [P, E * EH])
        moe_w2 = sb("moe_w2", [P, E * EB, D])
        ff_w1 = sb("ff_w1", [P, F_H])
        ff_w3 = sb("ff_w3", [P, F_H])
        ff_w2 = sb("ff_w2", [P, FB, D])
        ff_i1 = sb("ff_i1", [P, F_H], I32)
        ff_i3 = sb("ff_i3", [P, F_H], I32)
        ff_i2 = sb("ff_i2", [P, FB, D], I32)
        loaded = sem("loaded")
        dequant = sem("dequant")
        pad_set = sem("pad_set")
        stored = sem("stored")

        rows = a["h"].rearrange("b (t p) d -> p (b t) d", p=P)

        pieces = [(x[:, 0:TILES, :], rows), (ident[:], a["ident"]), (order[:], a["order"]),
                  (moe_gate[:], a["moe_gate"]), (moe_w1[:], a["moe_w1"]), (moe_w3[:], a["moe_w3"]),
                  (moe_w2[:], a["moe_w2"].rearrange("(n p) d -> p n d", p=P)),
                  (ff_i1[:], a["ff_w1"]), (ff_i3[:], a["ff_w3"]),
                  (ff_i2[:], a["ff_w2"].rearrange("(n p) d -> p n d", p=P))]
        with nc.Block() as block:
            @block.sync
            def _(sp):
                for to, of in pieces:
                    sp.dma_start(to, of).then_inc(loaded, 16)
                sp.wait_ge(loaded, 16 * len(pieces))

            @block.gpsimd
            def _(pool):
                pool.memset(x[:, TILES:TILES + CT, :], 0.0).then_inc(pad_set, 1)

            @block.vector
            def _(dve):
                dve.wait_ge(loaded, 16 * len(pieces))
                for to, of in ((ff_w1, ff_i1), (ff_w3, ff_i3), (ff_w2, ff_i2)):
                    dve.tensor_scalar(to[:], of[:], float(np.float32(1.0 / 127.0)), None,
                                      ALU.mult).then_inc(dequant, 1)

        for n, phase in enumerate(phases):
            if phase == "moe":
                feed_forward(nc, f"moe{n}", x, ident, moe_w1, moe_w3, moe_w2, E, EB, moe_gate, order)
            if phase == "mix":
                mixed_attention(nc, x, ident, a)
            if phase == "one":
                single_attention(nc, x, ident, a)
            if phase == "grp":
                grouped_attention(nc, x, ident, a)
            if phase == "spec":
                spectral_layers(nc, x, ident, a)
            if phase == "ff":
                feed_forward(nc, f"ff{n}", x, ident, ff_w1, ff_w3, ff_w2, 1, FB)

        with nc.Block() as block:
            @block.sync
            def _(sp):
                sp.dma_start(a["out"].rearrange("b (t p) d -> p (b t) d", p=P),
                             x[:, 0:TILES, :]).then_inc(stored, 16)
                sp.wait_ge(stored, 16)


def kernel(**inputs):
    import concourse.bacc as bacc
    from concourse.bass_utils import run_bass_kernel_spmd

    np_in = {k: np.asarray(v) for k, v in inputs.items()}
    f32 = np.float32

    def turned(a, *axes):
        return np.ascontiguousarray(np.transpose(a, axes))

    arrays = {
        "h": np_in["L0_attn_a_h"],
        "ident": np.eye(P, dtype=f32),
        "order": np.broadcast_to(np.arange(8, 0, -1, dtype=f32), (P, CT, 8)).copy(),
        "moe_gate": turned(np_in["L0_ffn_gate_w"], 1, 0),
        "moe_w1": turned(np_in["L0_ffn_w1"], 2, 0, 1).reshape(D, -1),
        "moe_w3": turned(np_in["L0_ffn_w3"], 2, 0, 1).reshape(D, -1),
        "moe_w2": turned(np_in["L0_ffn_w2"], 0, 2, 1).reshape(-1, D),
        "ff_w1": turned(np_in["L1_ffn_w_gate"], 1, 0),
        "ff_w3": turned(np_in["L1_ffn_w_up"], 1, 0),
        "ff_w2": turned(np_in["L1_ffn_w_down"], 1, 0),
    }
    def rows(a):
        return np.broadcast_to(a, (P,) + a.shape).copy()

    q_at = np.arange(SEQ)[:, None]
    k_at = np.arange(SEQ)[None, :]
    masked = np.where(q_at >= k_at, f32(0), f32(BIG)).reshape(ST, P, SEQ)
    outside = np.where((q_at >= k_at) & (q_at - k_at < A0.WINDOW), f32(0), f32(BIG)).reshape(ST, P, SEQ)
    valid = (np.arange(A0.NB)[None, :] + 1) * A0.CR - 1 <= q_at
    some = valid.any(-1, keepdims=True)
    blocks = np.zeros((SEQ, A0.H, A0.C), f32)
    blocks[:, :, 0:A0.NB] = np.where(np.where(some, valid, True), f32(0), f32(BIG))[:, None, :]
    turn = 1.0 / 10000.0 ** (np.arange(16, dtype=f32) * 2.0 / 32)
    angle = (np.arange(SEQ, dtype=f32)[:, None] * turn.astype(f32)[None, :]).astype(f32)
    cs = np.stack([np.tile(np.cos(angle), (1, 2)), np.tile(np.sin(angle), (1, 2))], 1)
    mean_w = np.zeros((SEQ, A0.H, A0.NB), f32)
    mean_w[np.arange(SEQ), :, np.arange(SEQ) // A0.CR] = 1.0 / A0.CR

    def tiled(a):
        return np.ascontiguousarray(a.reshape((ST, P) + a.shape[1:]).swapaxes(0, 1)).astype(f32)

    q_gain = np_in["L0_attn_a_g_qnorm"]
    arrays.update({
        "a_qc": turned(np_in["L0_attn_a_w_qc"], 1, 0),
        "a_qup": np_in["L0_attn_a_w_qup"],
        "a_group": turned(np_in["L0_attn_a_w_out_group"], 2, 0, 1),
        "a_out": turned(np_in["L0_attn_a_w_out"].reshape(2, 64, D), 1, 0, 2),
        "a_kv": np.concatenate([np_in["L0_attn_a_w_k"], np_in["L0_attn_a_w_v"]], 1),
        "a_gain_q": rows(np.stack([q_gain, q_gain])),
        "a_gain_k": rows(np.stack([np_in["L0_attn_a_g_knorm"]] * 2)),
        "a_gain_col": np.concatenate([q_gain, q_gain])[:, None].copy(),
        "a_gate_w": np.concatenate([np_in["L0_attn_a_w_gate"]] * 2, 0),
        "a_gate_b": rows(np_in["L0_attn_a_b_gate"]),
        "a_sink": rows(np_in["L0_attn_a_sink_logit"]),
        "rope": tiled(cs),
        "causal": np.concatenate([masked[0][:, 0:P], masked[1]], 1),
        "window": np.concatenate([outside[0][:, 0:P], outside[1][:, P - A0.WINDOW:]], 1),
        "blocks": tiled(blocks),
        "any_block": tiled(some.astype(f32))[:, :, 0].copy(),
        "mean_w": tiled(mean_w.reshape(SEQ, -1)),
        "diagonal": np.repeat(np.eye(A0.H, dtype=f32), A0.NB, 0),
    })
    b = "L0_attn_b_"
    arrays.update({
        "b_wq": turned(np_in[b + "Wq"], 1, 0), "b_wk": turned(np_in[b + "Wk"], 1, 0),
        "b_wv": turned(np_in[b + "Wv"], 1, 0), "b_wo": turned(np_in[b + "Wo"], 1, 0),
        "b_bq": np_in[b + "bq"][:, None].copy(), "b_bk": np_in[b + "bk"][:, None].copy(),
        "b_bv": rows(np_in[b + "bv"]), "b_bo": rows(np_in[b + "bo"]),
    })
    g = "L1_attn_a_"
    keys_at = np.broadcast_to(np.concatenate([np.arange(P), np.arange(SEQ)]).astype(f32), (P, P + SEQ))
    arrays.update({
        "c_wq": np_in[g + "Wq"].reshape(G1.IN, G1.H, G1.HD // 2, 2),
        "c_wk": np.repeat(np_in[g + "Wk"].reshape(G1.IN, G1.KVH, 1, G1.HD), 2, 2),
        "c_wv": np_in[g + "Wv"],
        "c_wo": turned(np_in[g + "Wo"].reshape(G1.HP, P, D), 1, 0, 2),
        "c_phase": rows(np_in[g + "q_phase_angle"]),
        "c_slope": rows(np_in[g + "alibi_log_slopes"]),
        "keys_at": keys_at.copy(),
    })
    e = "L1_attn_b_"
    LAY = H1.LAYERS

    def spread(a):
        return np.broadcast_to(a[:, None], (LAY, P) + a.shape[1:]).copy()

    def by_part(a):
        a = a.reshape(a.shape[:-1] + (H1.H, 3, H1.HD)).swapaxes(-3, -2)
        return np.concatenate([a[..., -1:, :], a], -2).reshape(a.shape[:-3] + (3, H1.WRAP))

    def hartley(n):
        at = 2 * np.pi * (np.arange(n)[:, None] * np.arange(n)[None, :] % n) / n
        return np.cos(at) + np.sin(at)

    ks = np.fft.fftfreq(SEQ)[:, None, None]
    kh = np.fft.fftfreq(H1.H)[None, :, None]
    kd = np.fft.fftfreq(H1.HD)[None, None, :]
    even = np.cos(np.arctan(np.log(np.sqrt(ks ** 2 + kh ** 2 + kd ** 2 + 1e-10) + 1e-10)))
    lam = np.arange(SEQ, dtype=f32) / f32(SEQ)
    tau = np.arange(SEQ, dtype=f32) * f32(0.1)
    modulation = np.sin(tau + lam) * np.cos(tau - f32(2) * lam + f32(0.5) * lam ** 2)
    filt = even.reshape(SEQ, D) * (1.0 + 0.1 * modulation.astype(np.float64))[:, None] / (H1.H * H1.HD)
    arrays.update({
        "d_ln": np.stack([np_in[e + n] for n in ("ln1_w", "ln1_b", "ln2_w", "ln2_b")], -1),
        "d_qkv_w": np.ascontiguousarray(by_part(np_in[e + "attn_w"])),
        "d_qkv_b": spread(by_part(np_in[e + "attn_b"])),
        "d_proj_w": np_in[e + "aproj_w"],
        "d_proj_b": spread(np_in[e + "aproj_b"]),
        "d_fc_w": np_in[e + "fc_w"],
        "d_fc_b": turned(np_in[e + "fc_b"].reshape(LAY, H1.HB, P), 0, 2, 1),
        "d_mp_w": turned(np_in[e + "mproj_w"].reshape(LAY, H1.HB, P, D), 0, 2, 1, 3),
        "d_mp_b": spread(np_in[e + "mproj_b"]),
        "hartley": np.kron(hartley(H1.H), hartley(H1.HD)).astype(f32),
        "filter": np.ascontiguousarray(filt.T).astype(f32),
    })
    nc = bacc.Bacc("TRN2", target_bir_lowering=False, num_devices=1)
    aps = {k: nc.dram_tensor(f"in_{k}", v.shape, mybir.dt.from_np(v.dtype), kind="ExternalInput").ap()
           for k, v in arrays.items()}
    aps["out"] = nc.dram_tensor("out", (16, SEQ, D), F32, kind="ExternalOutput").ap()
    build(nc, aps, PHASES)
    r = run_bass_kernel_spmd(nc, [{f"in_{k}": v for k, v in arrays.items()}], core_ids=[0])
    return r.results[0]["out"]


PHASES = ['mix', 'moe', 'one', 'moe', 'grp', 'ff', 'spec', 'ff']
```

```python
import math
from contextlib import ExitStack

import numpy as np

import concourse.bass as bass
from concourse import mybir

ALU = mybir.AluOpType
ACT = mybir.ActivationFunctionType
AX_X = mybir.AxisListType.X
F32 = mybir.dt.float32
I32 = mybir.dt.int32
U32 = mybir.dt.uint32

P = 128
D = 128
SEQ = 256
TOKENS = 16 * SEQ
TILES = TOKENS // P
CT = 4
CHUNKS = TILES // CT
CW = CT * P
SEQS = TOKENS // SEQ
ST = SEQ // P
BIG = 1e30
LN_EPS = 1e-5
ROUND = 1.5 * 2.0 ** 23
TURN_HIGH = 6.28125
TURN_LOW = 2 * math.pi - TURN_HIGH
HALF_TURN = 3.1415925


class Signal:

    def __init__(self, sem, per):
        self.sem, self.per = sem, per

    def start(self, eng):
        eng.sem_inc(self.sem, 2 * self.per)

    def at(self, chunk, n):
        return (chunk + 2) * self.per + n


class Alternating:

    def __init__(self, sems, per, ahead=2, used=(0, 0)):
        self.sems, self.per, self.ahead, self.used = sems, per, ahead, used

    def start(self, eng):
        for s in self.sems:
            eng.sem_inc(s, self.ahead // 2 * self.per)

    def done(self, chunk, u):
        return self.sems[u], (chunk - u + self.ahead) * (self.per // 2) + (1 + self.used[u]) * self.per


class Phase(ExitStack):

    def __init__(self):
        super().__init__()
        self.used = []
        self.main = ExitStack()

    def main_block(self, nc):
        return self.main.enter_context(nc.Block())

    def semaphore(self, nc, name):
        self.used.append(self.enter_context(nc.semaphore(name)))
        return self.used[-1]

    def clear(self, nc):
        self.main.close()
        with nc.Block() as block:
            @block.gpsimd
            def _(pool):
                for s in self.used:
                    pool.sem_clear(s)


def pairs(eng, body, count=SEQS):
    with eng.Fori(0, count // 2) as j:
        for u in range(2):
            body(j * 2 + u, u)


class Norm:

    def __init__(self, nc, ctx, name, x, ident, tiles, ps=None, bank_free=None, gain=None, shift=None):
        CT = self.tiles = tiles
        CW = CT * P

        def sb(n, shape):
            return ctx.enter_context(nc.sbuf_tensor(f"{name}_{n}", shape, F32))

        def signal(n, per):
            return Signal(ctx.semaphore(nc, f"{name}_{n}"), per)

        self.x, self.ident, self.gain, self.shift = x, ident, gain, shift
        self.stats = sb("stats", [P, CT, 6])
        self.mv = sb("mean_var", [P, CT, 2])
        self.veps = sb("var_eps", [P, CT])
        self.power = sb("power", [P, CT])
        self.rstd = sb("rstd", [P, CT])
        self.xn = sb("xn", [P, CT, D])
        self.xT = sb("xT", [P, 2, CW])
        self.bank_free = bank_free
        self.ps = ctx.enter_context(nc.psum_tensor(f"{name}_psT", [P, CW], F32)) if ps is None else ps[:, 0:CW]
        self.stat_done = signal("stat_done", CT)
        self.mv_done = signal("mv_done", CT)
        self.pow_done = signal("pow_done", 2)
        self.xn_done = signal("xn_done", CT)
        self.tr_done = signal("tr_done", 1)
        self.xT_done = signal("xT_done", 1)
        self.turns = ctx.semaphore(nc, f"{name}_turns")
        self.power_set = ctx.semaphore(nc, f"{name}_power_set")

    def start(self, nc, dve=None, pool=None, pe=None, act=None):
        if dve is not None:
            for s in (self.stat_done, self.mv_done, self.xn_done):
                s.start(dve)
        if pool is not None:
            self.pow_done.start(pool)
            pool.memset(self.power[:], -0.5).then_inc(self.power_set, 1)
            pool.wait_ge(self.power_set, 1)
        if pe is not None:
            self.tr_done.start(pe)
        if act is not None:
            self.xT_done.start(act)

    def on_vector(self, dve, c):
        CT = self.tiles
        for t in range(CT):
            dve.bn_stats(self.stats[:, t, :], self.x[:, c * CT + t, :]).then_inc(self.stat_done.sem, 1)
        dve.wait_ge(self.pow_done.sem, self.pow_done.at(c - 1, 1))
        dve.wait_ge(self.xn_done.sem, self.xn_done.at(c - 1, CT))
        dve.wait_ge(self.stat_done.sem, self.stat_done.at(c, CT))
        dve.sem_inc(self.turns, 1)
        for t in range(CT):
            dve.bn_aggr(self.mv[:, t, :], self.stats[:, t, :]).then_inc(self.mv_done.sem, 1)

    def on_pool(self, pool, c):
        CT = self.tiles
        pool.wait_ge(self.mv_done.sem, self.mv_done.at(c, CT))
        pool.sem_inc(self.turns, 1)
        pool.tensor_scalar(self.veps[:], self.mv[:, :, 1], LN_EPS, None, ALU.add).then_inc(self.pow_done.sem, 1)
        pool.wait_ge(self.pow_done.sem, self.pow_done.at(c, 1))
        pool.wait_ge(self.xn_done.sem, self.xn_done.at(c - 1, CT))
        pool.tensor_tensor(self.rstd[:], self.veps[:], self.power[:], ALU.pow).then_inc(self.pow_done.sem, 1)

    def on_vector_scale(self, dve, c):
        CT = self.tiles
        dve.wait_ge(self.mv_done.sem, self.mv_done.at(c, CT))
        dve.wait_ge(self.pow_done.sem, self.pow_done.at(c, 2))
        dve.wait_ge(self.tr_done.sem, self.tr_done.at(c - 1, 1))
        for t in range(CT):
            dve.tensor_scalar(self.xn[:, t, :], self.x[:, c * CT + t, :], self.mv[:, t, 0:1],
                              self.rstd[:, t:t + 1], ALU.subtract, ALU.mult).then_inc(self.xn_done.sem, 1)

    def on_tensor(self, pe, c):
        CT = self.tiles
        pe.wait_ge(self.xT_done.sem, self.xT_done.at(c - 1, 1))
        if self.bank_free is not None:
            pe.wait_ge(*self.bank_free(c))
        for t in range(CT):
            pe.wait_ge(self.xn_done.sem, self.xn_done.at(c, t + 1))
            last = pe.transpose(self.ps[:, t * P:(t + 1) * P], self.xn[:, t, :], self.ident[:])
        last.then_inc(self.tr_done.sem, 1)

    def on_scalar(self, act, c, u, xT_free):
        act.wait_ge(self.tr_done.sem, self.tr_done.at(c, 1))
        act.wait_ge(*xT_free)
        if self.gain is None:
            last = act.activation(self.xT[:, u, :], self.ps[:, :], ACT.Copy)
        else:
            last = act.activation(self.xT[:, u, :], self.ps[:, :], ACT.Identity,
                                  bias=self.shift, scale=self.gain)
        last.then_inc(self.xT_done.sem, 1)


def feed_forward(nc, name, x, ident, w1, w3, w2, blocks):
    with Phase() as ctx:
        def sb(n, shape):
            return ctx.enter_context(nc.sbuf_tensor(f"{name}_{n}", shape, F32))

        def ps(n, shape):
            return ctx.enter_context(nc.psum_tensor(f"{name}_{n}", shape, F32))

        def signal(n, per):
            return Signal(ctx.semaphore(nc, f"{name}_{n}"), per)

        norm = Norm(nc, ctx, name, x, ident, CT)
        ps_a = [ps(f"ps_a{i}", [P, CW]) for i in range(2)]
        ps_b = [ps(f"ps_b{i}", [P, CW]) for i in range(2)]
        ps_o = [ps(f"ps_o{i}", [P, CT, D]) for i in range(2)]
        silu = sb("silu", [P, 2, CW])
        hidden = sb("hidden", [P, 2, blocks, CW])
        up_done = signal("up_done", 2 * blocks)
        silu_done = signal("silu_done", blocks)
        hid_done = signal("hid_done", blocks)
        down_done = signal("down_done", 1)
        comb_done = signal("comb_done", CT)

        def bank(u, b):
            return (u * blocks + b) % 2

        block = ctx.main_block(nc)


        @block.gpsimd
        def _(pool):
            norm.start(nc, pool=pool)
            norm.on_pool(pool, 0)
            norm.on_pool(pool, 1)
            pairs(pool, lambda c, u: norm.on_pool(pool, c + 2), CHUNKS)

        @block.tensor
        def _(pe):
            norm.start(nc, pe=pe)
            up_done.start(pe)
            down_done.start(pe)

            def up(c, u, b):
                i = bank(u, b)
                pe.wait_ge(norm.xT_done.sem, norm.xT_done.at(c, 1))
                pe.wait_ge(hid_done.sem, hid_done.at(c, b - 1))
                pe.matmul(ps_a[i][:], w1[:, b * P:(b + 1) * P], norm.xT[:, u, :],
                          start=True, stop=True).then_inc(up_done.sem, 1)
                pe.matmul(ps_b[i][:], w3[:, b * P:(b + 1) * P], norm.xT[:, u, :],
                          start=True, stop=True).then_inc(up_done.sem, 1)

            def down(c, u):
                pe.wait_ge(hid_done.sem, hid_done.at(c, blocks))
                pe.wait_ge(comb_done.sem, comb_done.at(c - 2, CT))
                for t in range(CT):
                    for b in range(blocks):
                        last = pe.matmul(ps_o[u][:, t, :], hidden[:, u, b, t * P:(t + 1) * P],
                                         w2[:, b, :], start=(b == 0), stop=(b == blocks - 1))
                last.then_inc(down_done.sem, 1)

            norm.on_tensor(pe, 0)
            norm.on_tensor(pe, 1)
            for b in range(blocks):
                up(0, 0, b)

            def body(c, u):
                up(c + 1, 1 - u, 0)
                down(c, u)
                norm.on_tensor(pe, c + 2)
                for b in range(1, blocks):
                    up(c + 1, 1 - u, b)

            pairs(pe, body, CHUNKS)

        @block.scalar
        def _(act):
            norm.start(nc, act=act)
            silu_done.start(act)

            def normal(c, u):
                norm.on_scalar(act, c, u, (up_done.sem, up_done.at(c - 2, 2 * blocks)))

            def gate(c, u, b):
                i = bank(u, b)
                act.wait_ge(up_done.sem, up_done.at(c, 2 * b + 1))
                act.wait_ge(hid_done.sem, hid_done.at(c, b - 1))
                act.activation(silu[:, i, :], ps_a[i][:], ACT.Silu).then_inc(silu_done.sem, 1)

            normal(0, 0)
            normal(1, 1)
            for b in range(blocks):
                gate(0, 0, b)

            def body(c, u):
                gate(c + 1, 1 - u, 0)
                normal(c + 2, u)
                for b in range(1, blocks):
                    gate(c + 1, 1 - u, b)

            pairs(act, body, CHUNKS)

        @block.vector
        def _(dve):
            norm.start(nc, dve=dve)
            hid_done.start(dve)
            comb_done.start(dve)

            def multiply(c, u, b):
                i = bank(u, b)
                dve.wait_ge(silu_done.sem, silu_done.at(c, b + 1))
                dve.wait_ge(up_done.sem, up_done.at(c, 2 * b + 2))
                if b == 0:
                    dve.wait_ge(down_done.sem, down_done.at(c - 2, 1))
                dve.tensor_tensor(hidden[:, u, b, :], silu[:, i, :], ps_b[i][:],
                                  ALU.mult).then_inc(hid_done.sem, 1)

            for c in range(2):
                norm.on_vector(dve, c)
                norm.on_vector_scale(dve, c)
            for b in range(blocks):
                multiply(0, 0, b)

            def body(c, u):
                norm.on_vector(dve, c + 2)
                multiply(c + 1, 1 - u, 0)
                norm.on_vector_scale(dve, c + 2)
                dve.wait_ge(down_done.sem, down_done.at(c, 1))
                for t in range(CT):
                    rows = x[:, c * CT + t, :]
                    dve.tensor_tensor(rows, ps_o[u][:, t, :], rows, ALU.add).then_inc(comb_done.sem, 1)
                for b in range(1, blocks):
                    multiply(c + 1, 1 - u, b)

            pairs(dve, body, CHUNKS)

        ctx.clear(nc)


def pairs_from_two(eng, body, groups):
    for g in range(2):
        body(g, g)
    with eng.Fori(1, groups // 2) as j:
        for u in range(2):
            body(j * 2 + u, u)


def early(group):
    return isinstance(group, int) and group < 2


class M0:
    E, EH = 8, 512
    EB = EH // P
    SLOT_TILES = 2 * TOKENS // P + E
    TABLE_TILES = SLOT_TILES + 3
    G = 4
    GROUPS = TILES // G


def routed_experts(nc, name, x, ident, w1, w3, w2, gate_w, consts, slots_in, slots_out, slot, share, scattered):
    E, EH, EB, G, GROUPS, SLOT_TILES = M0.E, M0.EH, M0.EB, M0.G, M0.GROUPS, M0.SLOT_TILES
    order, upper, ones, tile_at = consts
    with Phase() as ctx:
        def sb(n, shape, dt=F32):
            return ctx.enter_context(nc.sbuf_tensor(f"{name}_{n}", shape, dt))

        def ps(n, shape):
            return ctx.enter_context(nc.psum_tensor(f"{name}_{n}", shape, F32))

        def sem(n):
            return ctx.semaphore(nc, f"{name}_{n}")

        def signal(n, per):
            return Signal(sem(n), per)

        ps_g = ps("ps_g", [P, CT, E])
        ps_a = [ps(f"ps_a{i}", [P, EH]) for i in range(2)]
        ps_b = [ps(f"ps_b{i}", [P, EH]) for i in range(2)]
        ps_h = ps("ps_h", [P, EB, P])
        ps_n = ps("ps_n", [P, CW])
        norm = Norm(nc, ctx, name, x, ident, CT, ps=ps_n)

        score = sb("score", [P, TILES, E])
        moments = sb("moments", [P, TILES + CT, 2])
        rstds = sb("rstds", [P, TILES + CT])
        expert = sb("expert", [P, M0.TABLE_TILES], I32)

        score_mm = signal("score_mm", 1)
        scored = signal("scored", 1)
        kept = signal("kept", 2)
        with nc.Block() as block:
            @block.gpsimd
            def _(pool):
                norm.start(nc, pool=pool)
                norm.on_pool(pool, 0)
                pairs(pool, lambda c, u: norm.on_pool(pool, c + 1), CHUNKS)

            @block.tensor
            def _(pe):
                norm.start(nc, pe=pe)
                score_mm.start(pe)

                def body(c, u):
                    pe.wait_ge(norm.xT_done.sem, norm.xT_done.at(c, 1))
                    pe.wait_ge(scored.sem, scored.at(c - 1, 1))
                    for t in range(CT):
                        last = pe.matmul(ps_g[:, t, :], norm.xT[:, u, t * P:(t + 1) * P], gate_w[:],
                                         start=True, stop=True)
                    last.then_inc(score_mm.sem, 1)
                    norm.on_tensor(pe, c + 1)

                norm.on_tensor(pe, 0)
                pairs(pe, body, CHUNKS)

            @block.scalar
            def _(act):
                norm.start(nc, act=act)

                def normal(c, u):
                    norm.on_scalar(act, c, u, (score_mm.sem, score_mm.at(c - 2, 1)))

                normal(0, 0)
                pairs(act, lambda c, u: normal(c + 1, 1 - u), CHUNKS)

            @block.vector
            def _(dve):
                norm.start(nc, dve=dve)
                scored.start(dve)
                kept.start(dve)

                def normalise(c):
                    dve.wait_ge(kept.sem, kept.at(c - 1, 2))
                    dve.sem_inc(norm.turns, 1)
                    norm.on_vector(dve, c)
                    norm.on_vector_scale(dve, c)
                    dve.tensor_copy(moments[:, bass.ts(c, CT), :], norm.mv[:]).then_inc(kept.sem, 1)
                    dve.tensor_copy(rstds[:, bass.ts(c, CT)], norm.rstd[:]).then_inc(kept.sem, 1)

                def body(c, u):
                    normalise(c + 1)
                    dve.wait_ge(score_mm.sem, score_mm.at(c, 1))
                    dve.tensor_copy(score[:, bass.ts(c, CT), :], ps_g[:]).then_inc(scored.sem, 1)

                normalise(0)
                pairs(dve, body, CHUNKS)

        routed, counted, tanh_done = sem("routed"), sem("counted"), sem("tanh_done")
        with ExitStack() as local:
            def tmp(n, shape):
                return local.enter_context(nc.sbuf_tensor(f"{name}_{n}", shape, F32))

            same = tmp("same", [P, TILES, E])
            place = tmp("place", [P, TILES, E])
            best = tmp("best", [P, 2, TILES, E])
            both = tmp("both", [P, TILES, E])
            total = tmp("total", [P, TILES, E])
            run = tmp("run", [P, 2, TILES, E])
            base = tmp("base", [P, TILES, E])
            top = tmp("top", [P, 2, TILES])
            first = tmp("first", [P, TILES])
            gap = tmp("gap", [P, TILES])
            half = tmp("half", [P, TILES])
            tiles_of = tmp("tiles_of", [P, 1, E])
            ends = tmp("ends", [P, 2, 1, E])
            starts = tmp("starts", [P, 1, E])
            before = tmp("before", [P, M0.TABLE_TILES, E])
            tile_expert = tmp("tile_expert", [P, M0.TABLE_TILES])
            slot_f = tmp("slot_f", [P, TILES, 2])
            BEST = 13
            with nc.Block() as block:
                @block.vector
                def _(dve):
                    k = 0

                    def step(ins):
                        nonlocal k
                        k += 1
                        ins.then_inc(routed, 1)
                        dve.wait_ge(routed, k)

                    def wide(a):
                        return a.unsqueeze(2).to_broadcast([P, TILES, E])

                    orders = order[:].unsqueeze(1).to_broadcast([P, TILES, E])
                    for r in range(2):
                        step(dve.tensor_reduce(top[:, r, :], score[:], AX_X, ALU.max))
                        step(dve.tensor_tensor(same[:], score[:], wide(top[:, r, :]), ALU.is_equal))
                        step(dve.tensor_tensor(place[:], same[:], orders, ALU.mult))
                        step(dve.tensor_reduce(first[:], place[:], AX_X, ALU.max))
                        step(dve.tensor_tensor(best[:, r, :, :], place[:], wide(first[:]), ALU.is_equal))
                        if r == 0:
                            step(dve.scalar_tensor_tensor(score[:], best[:, 0, :, :], -1e30, score[:],
                                                          ALU.mult, ALU.add))
                    step(dve.tensor_tensor(gap[:], top[:, 1, :], top[:, 0, :], ALU.subtract))
                    step(dve.tensor_tensor(both[:], best[:, 0, :, :], best[:, 1, :, :], ALU.add))
                    assert k == BEST
                    dve.wait_ge(tanh_done, 1)
                    step(dve.tensor_scalar(share[:, 0, 0:TILES], half[:], -0.5, 0.5, ALU.mult, ALU.add))
                    step(dve.tensor_scalar(share[:, 1, 0:TILES], half[:], 0.5, 0.5, ALU.mult, ALU.add))
                    dve.wait_ge(counted, 2)
                    step(dve.tensor_copy(total[:].rearrange("p t e -> p (t e)"), ps_a[1][:, 0:TILES * E]))
                    step(dve.tensor_copy(run[:, 0, :, :], total[:]))
                    a, shift = 0, 1
                    while shift < TILES:
                        step(dve.tensor_copy(run[:, 1 - a, 0:shift, :], run[:, a, 0:shift, :]))
                        step(dve.tensor_tensor(run[:, 1 - a, shift:, :], run[:, a, shift:, :],
                                               run[:, a, 0:TILES - shift, :], ALU.add))
                        a, shift = 1 - a, 2 * shift
                    step(dve.tensor_scalar(tiles_of[:, 0, :], run[:, a, TILES - 1, :], 1.0 / P,
                                           (P - 1) / P - 0.5 + 0.5 / P, ALU.mult, ALU.add))
                    step(dve.tensor_scalar(tiles_of[:], tiles_of[:], ROUND, None, ALU.add))
                    step(dve.tensor_scalar(tiles_of[:], tiles_of[:], ROUND, None, ALU.subtract))
                    step(dve.tensor_copy(ends[:, 0, :, :], tiles_of[:]))
                    b, shift = 0, 1
                    while shift < E:
                        step(dve.tensor_copy(ends[:, 1 - b, :, 0:shift], ends[:, b, :, 0:shift]))
                        step(dve.tensor_tensor(ends[:, 1 - b, :, shift:], ends[:, b, :, shift:],
                                               ends[:, b, :, 0:E - shift], ALU.add))
                        b, shift = 1 - b, 2 * shift
                    step(dve.tensor_tensor(starts[:], ends[:, b, :, :], tiles_of[:], ALU.subtract))
                    step(dve.tensor_tensor(base[:], run[:, a, :, :], total[:], ALU.subtract))
                    step(dve.tensor_tensor(base[:].rearrange("p t e -> p (t e)"), ps_a[0][:, 0:TILES * E],
                                           base[:].rearrange("p t e -> p (t e)"), ALU.add))
                    step(dve.scalar_tensor_tensor(base[:], starts[:].to_broadcast([P, TILES, E]), float(P), base[:],
                                                  ALU.mult, ALU.add))
                    for r in range(2):
                        step(dve.tensor_tensor(place[:], best[:, r, :, :], base[:], ALU.mult))
                        step(dve.tensor_reduce(slot_f[:, :, r], place[:], AX_X, ALU.add))
                    step(dve.memset(slot[:, TILES:, :], 0))
                    step(dve.memset(share[:, :, TILES:], 0.0))
                    step(dve.tensor_copy(slot[:, 0:TILES, :], slot_f[:]))
                    count = M0.TABLE_TILES
                    step(dve.tensor_tensor(before[:], tile_at[:].unsqueeze(2).to_broadcast([P, count, E]),
                                           ends[:, b, :, :].to_broadcast([P, count, E]), ALU.is_ge))
                    step(dve.tensor_reduce(tile_expert[:], before[:], AX_X, ALU.add))
                    step(dve.tensor_scalar(tile_expert[:], tile_expert[:], float(E - 1), None, ALU.min))
                    step(dve.tensor_copy(expert[:], tile_expert[:]))

                @block.scalar
                def _(act):
                    act.wait_ge(routed, BEST - 1)
                    act.activation(half[:], gap[:], ACT.Tanh, scale=0.5).then_inc(tanh_done, 1)

                @block.tensor
                def _(pe):
                    pe.wait_ge(routed, BEST)
                    for to, of in ((ps_a[0], upper), (ps_a[1], ones)):
                        pe.matmul(to[:, 0:TILES * E], of[:], both[:].rearrange("p t e -> p (t e)"), start=True,
                                  stop=True).then_inc(counted, 1)

        rows_in = sb("rows_in", [P, 2, G, D])
        slot_now = sb("slot_now", [P, 2, G, 2], U32)
        staged = signal("staged", G + 1)
        with nc.Block() as block:
            @block.vector
            def _(dve):
                staged.start(dve)

                def body(g, u):
                    if not early(g):
                        dve.wait_ge(*scattered.done(g - 2, u))
                    dve.tensor_copy(slot_now[:, u, :, :], slot[:, bass.ts(g, G), :]).then_inc(staged.sem, 1)
                    for t in range(G):
                        at = g * G + t
                        dve.tensor_scalar(rows_in[:, u, t, :], x[:, at, :], moments[:, at, 0:1],
                                          rstds[:, bass.ds(at, 1)], ALU.subtract, ALU.mult).then_inc(staged.sem, 1)

                pairs_from_two(dve, body, GROUPS)

            @block.gpsimd
            def _(pool):
                def body(g, u):
                    for t in range(G):
                        pool.wait_ge(staged.sem, staged.at(g, t + 2))
                        pool.sem_inc(norm.turns, 1)
                        for r in range(2):
                            pool.indirect_dma_start(
                                slots_in.rearrange("t p d -> (t p) d"),
                                bass.IndirectOffsetOnAxis(slot_now[:, u, t, r:r + 1], 0),
                                rows_in[:, u, t, :], None).then_inc(scattered.sems[u], 16)

                pairs_from_two(pool, body, GROUPS)
                for u in range(2):
                    pool.wait_ge(*scattered.done(GROUPS - 2 + u, u))

        row = sb("row", [P, 2, D])
        rowT = sb("rowT", [P, 2, P])
        silu = sb("silu", [P, 2, EH])
        hidden = sb("hidden", [P, 2, EH])
        hiddenT = sb("hiddenT", [P, EB, P])
        out = sb("out", [P, 2, D])
        loaded = Alternating([sem(f"loaded{i}") for i in range(2)], 16)
        row_tr = signal("row_tr", 1)
        row_ev = signal("row_ev", 1)
        up_mm = signal("up_mm", 2)
        silu_done = signal("silu_done", 1)
        hid_done = signal("hid_done", 1)
        hid_tr = signal("hid_tr", 1)
        hid_ev = signal("hid_ev", 1)
        down_mm = signal("down_mm", 1)
        out_ev = signal("out_ev", 1)
        stored = Alternating([sem(f"stored{i}") for i in range(2)], 16)
        ps_r = ps_n[:, 0:P]
        ps_o = ps("ps_o", [P, D])

        def walk(eng, a, b, body):
            a(0, 0)
            a(1, 1)
            b(0, 0)
            with eng.Fori(0, SLOT_TILES // 2) as j:
                for u in range(2):
                    body(j * 2 + u, u)

        with nc.Block() as block:
            @block.sync
            def _(sp):
                loaded.start(sp)
                stored.start(sp)

                def load(j, u):
                    sp.wait_ge(row_tr.sem, row_tr.at(j - 2, 1))
                    sp.dma_start(row[:, u, :], slots_in[j]).then_inc(loaded.sems[u], 16)

                def body(j, u):
                    load(j + 3, 1 - u)
                    sp.wait_ge(out_ev.sem, out_ev.at(j, 1))
                    sp.dma_start(slots_out[j], out[:, u, :]).then_inc(stored.sems[u], 16)

                load(0, 0)
                load(1, 1)
                load(2, 0)
                with sp.Fori(0, SLOT_TILES // 2) as j:
                    for u in range(2):
                        body(j * 2 + u, u)
                for u in range(2):
                    sp.wait_ge(*stored.done(SLOT_TILES - 2 + u, u))
                sp.wait_ge(*loaded.done(SLOT_TILES + 2, 0))

            @block.tensor
            def _(pe):
                for s in (row_tr, up_mm, hid_tr, down_mm):
                    s.start(pe)

                def expert_of(j):
                    return pe.value_load(expert[0:1, bass.ds(j, 1)], min_val=0, max_val=E - 1)

                def turn_row(j, u):
                    pe.wait_ge(*loaded.done(j, u))
                    pe.wait_ge(row_ev.sem, row_ev.at(j - 1, 1))
                    pe.transpose(ps_r, row[:, u, :], ident[:]).then_inc(row_tr.sem, 1)

                def up(j, u, e=None):
                    e = expert_of(j) if e is None else e
                    pe.wait_ge(row_ev.sem, row_ev.at(j, 1))
                    pe.wait_ge(hid_done.sem, hid_done.at(j - 2, 1))
                    pe.matmul(ps_a[u][:], rowT[:, u, :], w1[:, bass.ts(e, EH)], start=True,
                              stop=True).then_inc(up_mm.sem, 1)
                    pe.matmul(ps_b[u][:], rowT[:, u, :], w3[:, bass.ts(e, EH)], start=True,
                              stop=True).then_inc(up_mm.sem, 1)

                def turn_hidden(j, u):
                    pe.wait_ge(hid_done.sem, hid_done.at(j, 1))
                    pe.wait_ge(hid_ev.sem, hid_ev.at(j - 1, 1))
                    for b in range(EB):
                        last = pe.transpose(ps_h[:, b, :], hidden[:, u, b * P:(b + 1) * P], ident[:])
                    last.then_inc(hid_tr.sem, 1)

                def down(j, e):
                    pe.wait_ge(hid_ev.sem, hid_ev.at(j, 1))
                    pe.wait_ge(out_ev.sem, out_ev.at(j - 1, 1))
                    for b in range(EB):
                        last = pe.matmul(ps_o[:], hiddenT[:, b, :], w2[:, e * EB + b, :], start=(b == 0),
                                         stop=(b == EB - 1))
                    last.then_inc(down_mm.sem, 1)

                def body(j, u):
                    now, ahead = expert_of(j), expert_of(j + 1)
                    turn_hidden(j, u)
                    turn_row(j + 2, u)
                    up(j + 1, 1 - u, ahead)
                    down(j, now)

                walk(pe, turn_row, up, body)

            @block.scalar
            def _(act):
                for s in (row_ev, silu_done, out_ev):
                    s.start(act)

                def copy_row(j, u):
                    act.wait_ge(row_tr.sem, row_tr.at(j, 1))
                    act.wait_ge(up_mm.sem, up_mm.at(j - 2, 2))
                    act.activation(rowT[:, u, :], ps_r, ACT.Copy).then_inc(row_ev.sem, 1)

                def gate(j, u):
                    act.wait_ge(up_mm.sem, up_mm.at(j, 1))
                    act.wait_ge(hid_done.sem, hid_done.at(j - 2, 1))
                    act.activation(silu[:, u, :], ps_a[u][:], ACT.Silu).then_inc(silu_done.sem, 1)

                def body(j, u):
                    copy_row(j + 2, u)
                    gate(j + 1, 1 - u)
                    act.wait_ge(down_mm.sem, down_mm.at(j, 1))
                    act.wait_ge(*stored.done(j - 2, u))
                    act.activation(out[:, u, :], ps_o[:], ACT.Copy).then_inc(out_ev.sem, 1)

                walk(act, copy_row, gate, body)

            @block.vector
            def _(dve):
                for s in (hid_done, hid_ev):
                    s.start(dve)

                def multiply(j, u):
                    dve.wait_ge(silu_done.sem, silu_done.at(j, 1))
                    dve.wait_ge(up_mm.sem, up_mm.at(j, 2))
                    dve.wait_ge(hid_tr.sem, hid_tr.at(j - 2, 1))
                    dve.tensor_tensor(hidden[:, u, :], silu[:, u, :], ps_b[u][:], ALU.mult).then_inc(hid_done.sem, 1)

                def body(j, u):
                    dve.wait_ge(hid_tr.sem, hid_tr.at(j, 1))
                    dve.wait_ge(down_mm.sem, down_mm.at(j - 1, 1))
                    dve.tensor_copy(hiddenT[:], ps_h[:]).then_inc(hid_ev.sem, 1)
                    multiply(j + 1, 1 - u)

                walk(dve, lambda j, u: None, multiply, body)

        ctx.clear(nc)


class Combine:

    def __init__(self, nc, ctx, name, x, chunks, slot, share, slots_out, gathered):
        self.x, self.chunks, self.slot, self.share, self.gathered = x, chunks, slot, share, gathered
        self.rows = slots_out.rearrange("t p d -> (t p) d")
        self.slot_now = ctx.enter_context(nc.sbuf_tensor(f"{name}_slot_now", [P, 2, ST, 2], U32))
        self.found = ctx.enter_context(nc.sbuf_tensor(f"{name}_found", [P, 2, ST, 2, D], F32))
        self.asked = Signal(ctx.semaphore(nc, f"{name}_asked"), 1)
        self.summed = Signal(ctx.semaphore(nc, f"{name}_summed"), 2 * ST)
        self.turns = ctx.semaphore(nc, f"{name}_combine_turns")

    def start(self, dve):
        self.asked.start(dve)
        self.summed.start(dve)

    def ask(self, dve, c, u):
        if not early(c):
            dve.wait_ge(*self.gathered.done(c - 2, u))
        dve.tensor_copy(self.slot_now[:, u, :, :], self.slot[:, bass.ts(c, ST), :]).then_inc(self.asked.sem, 1)

    def gather(self, pool, c, u):
        pool.wait_ge(self.asked.sem, self.asked.at(c, 1))
        pool.wait_ge(self.summed.sem, self.summed.at(c - 2, 2 * ST))
        pool.sem_inc(self.turns, 1)
        for t in range(ST):
            for r in range(2):
                pool.indirect_dma_start(self.found[:, u, t, r, :], None, self.rows,
                                        bass.IndirectOffsetOnAxis(self.slot_now[:, u, t, r:r + 1], 0)
                                        ).then_inc(self.gathered.sems[u], 16)

    def add(self, dve, c, u, t):
        if t == 0:
            dve.wait_ge(*self.gathered.done(c, u))
        at = c * ST + t
        for r in range(2):
            if r == 1:
                dve.wait_ge(self.summed.sem, self.summed.at(c, 2 * t + 1))
            dve.scalar_tensor_tensor(self.x[:, at, :], self.found[:, u, t, r, :],
                                     self.share[:, r, bass.ds(at, 1)], self.x[:, at, :], ALU.mult,
                                     ALU.add).then_inc(self.summed.sem, 1)

    def settle(self, dve, c):
        dve.wait_ge(self.summed.sem, self.summed.at(c, 2 * ST))
        dve.sem_inc(self.turns, 1)

    def finish(self, pool):
        for c in (self.chunks - 2, self.chunks - 1):
            pool.wait_ge(*self.gathered.done(c, c % 2))


class A0:
    H, HD, QC, CR = 8, 64, 32, 32
    NB = SEQ // CR
    WINDOW = 64
    W1 = P + WINDOW
    X = 16
    SINK, GATE = NB, NB + 1
    C = NB + 4


def mixed_attention(nc, x, ident, w, on_sync):
    H, HD, NB, X, C = A0.H, A0.HD, A0.NB, A0.X, A0.C
    HP = H // 2
    with Phase() as ctx:
        def sb(n, shape):
            return ctx.enter_context(nc.sbuf_tensor(f"mix_{n}", shape, F32))

        def ps(n, shape):
            return ctx.enter_context(nc.psum_tensor(f"mix_{n}", shape, F32))

        def sem(n):
            return ctx.semaphore(nc, f"mix_{n}")

        def signal(n, per):
            return Signal(sem(n), per)

        ps_f = ps("ps_f", [P, 512])
        ps_q = ps("ps_q", [P, H, HD])
        ps_kv = ps("ps_kv", [P, 512])
        ps_s = [ps(f"ps_s{i}", [P, X + SEQ]) for i in range(2)]
        ps_t = [ps(f"ps_t{i}", [P, 512]) for i in range(2)]
        ps_o = ps("ps_o", [P, H, HD])

        qc_w = sb("qc_w", [A0.QC, D])
        qup_w = sb("qup_w", [A0.QC, H * HD])
        group_w = sb("group_w", [64, 2, 2 * P])
        out_w = sb("out_w", [64, 2, D])
        q_w = sb("q_w", [D, H * HD])
        kv_w = sb("kv_w", [D, 2 * HD])
        y_w = sb("y_w", [P, HP, D])
        gain_q = sb("gain_q", [P, 2, HD])
        gain_k = sb("gain_k", [P, 2, HD])
        gain_qk = sb("gain_qk", [P, 2, HD])
        gain_col = sb("gain_col", [P, 1])
        gate_w = sb("gate_w", [P, 3])
        gate_b = sb("gate_b", [P, 3])
        sink = sb("sink", [P, H])
        rope = sb("rope", [P, ST, 2, 32])
        causal = sb("causal", [P, P + SEQ])
        window = sb("window", [P, P + A0.W1])
        extra = sb("extra", [P, ST, H, C])
        any_block = sb("any_block", [P, ST])
        mean_w = sb("mean_w", [P, ST, H * NB])
        diagonal = sb("diagonal", [H * NB, H])

        qk = sb("qk", [P, ST, H + 1, HD])
        sq = sb("sq", [P, ST, H + 1, HD])
        ss = sb("ss", [P, ST, H + 1])
        ms = sb("ms", [P, ST, H + 1])
        rms = sb("rms", [P, ST, H + 1])
        half = sb("half", [P, ST, H + 1])
        rc = sb("rc", [P, H + 1, 32])
        rs = sb("rs", [P, H + 1, 32])
        kd = sb("kd", [P, ST, 2, HD])
        v = sb("v", [P, 2, ST, HD])
        vc = sb("vc", [H * NB, 2, H, HD])
        kc = sb("kc", [P, NB])
        kx = sb("kx", [P, 2, X + SEQ])
        qT = sb("qT", [P, 2, ST, HP, P])
        s_all = sb("s_all", [P, 2, SEQ])
        s_win = sb("s_win", [P, 2, A0.W1])
        low_all = sb("low_all", [P, ST, H])
        low_win = sb("low_win", [P, ST, H])
        p_all = sb("p_all", [P, ST, H, SEQ])
        p_win = sb("p_win", [P, ST, H, A0.W1])
        cg = sb("cg", [P, ST, H, C])
        low_c = sb("low_c", [P, H])
        e_c = sb("e_c", [P, H, NB + 1])
        e_sink = sb("e_sink", [P, H])
        sig = sb("sig", [P, H, 3])
        total = sb("total", [P, ST, 4, H])
        inverse = sb("inverse", [P, 4, H])
        ratio = sb("ratio", [P, 3, H])
        factor = sb("factor", [P, ST, 3, H])
        p_c = sb("p_c", [P, ST, H, NB])
        p_cT = sb("p_cT", [H * NB, P])
        pT = sb("pT", [P, 2, ST, P])
        o = sb("o", [P, H, HD])
        oT = sb("oT", [P, HP, P])

        loaded, made, multiplied, passed = sem("loaded"), sem("made"), sem("multiplied"), sem("passed")
        kv_mm = signal("kv_mm", 1)
        q_mm = signal("q_mm", ST)
        copied = signal("copied", 4 * ST)
        prepared = signal("prepared", 3 * ST + 3)
        turned = signal("turned", 6 * ST)
        front_mm = signal("front_mm", 4)
        front_ev = signal("front_ev", 3)
        norm = Norm(nc, ctx, "mix", x, ident, ST, ps=ps_f,
                    bank_free=lambda c: (front_ev.sem, front_ev.at(c - 1, 3)))
        U = ST * H
        s_mm = signal("s_mm", U)
        least = signal("least", 3 * U)
        exped = signal("exped", 2 * U)
        MIX = 13
        mixing = signal("mixing", MIX * ST)
        mix_exp = signal("mix_exp", 3 * ST)
        weighed = signal("weighed", 2 * U)
        R = H + 2
        p_tr = signal("p_tr", R * ST)
        p_ev = signal("p_ev", R * ST)
        o_mm = signal("o_mm", R * ST)
        o_ev = signal("o_ev", ST)
        added = signal("added", ST)

        pieces = [(qc_w, "a_qc"), (qup_w, "a_qup"), (group_w, "a_group"), (out_w, "a_out"), (kv_w, "a_kv"),
                  (gain_q, "a_gain_q"), (gain_k, "a_gain_k"), (gain_col, "a_gain_col"), (gate_w, "a_gate_w"),
                  (gate_b, "a_gate_b"), (sink, "a_sink"), (rope, "rope"), (causal, "causal"),
                  (window, "window"), (extra, "blocks"), (any_block, "any_block"), (mean_w, "mean_w"),
                  (diagonal, "diagonal")]

        with nc.Block() as block:
            @block.sync
            def _(sp):
                for to, of in pieces:
                    sp.dma_start(to[:], w[of]).then_inc(loaded, 16)

            @block.gpsimd
            def _(pool):
                pool.memset(half[:], -0.5)

            @block.tensor
            def _(pe):
                pe.wait_ge(loaded, 16 * len(pieces))
                pe.matmul(ps_q[:], qc_w[:], qup_w[:], start=True, stop=True).then_inc(multiplied, 1)
                for b in range(HP):
                    last = pe.matmul(ps_f[:, b * P:(b + 1) * P], group_w[:, b // 2, (b % 2) * P:(b % 2 + 1) * P],
                                     out_w[:, b // 2, :], start=True, stop=True)
                last.then_inc(multiplied, 1)

            @block.vector
            def _(dve):
                dve.wait_ge(loaded, 16 * len(pieces))
                dve.memset(kx[:], 0.0).then_inc(made, 1)
                dve.scalar_tensor_tensor(gain_qk[:], gain_q[:], -(HD ** -0.5), gain_k[:], ALU.mult, ALU.mult)
                dve.wait_ge(made, 1)
                for u in range(2):
                    dve.tensor_scalar(kx[:, u, A0.GATE:A0.GATE + 3], gate_w[:], gain_col[:, 0:1], -1.0,
                                      ALU.mult, ALU.mult)
                for t in range(ST):
                    dve.tensor_scalar(extra[:, t, :, A0.SINK], sink[:], -1.0, None, ALU.mult)
                    dve.tensor_scalar(extra[:, t, :, A0.GATE:A0.GATE + 3],
                                      gate_b[:].unsqueeze(1).to_broadcast([P, H, 3]), -1.0, None, ALU.mult)
                dve.wait_ge(multiplied, 2)
                dve.tensor_copy(q_w[:], ps_q[:].rearrange("p h d -> p (h d)"))
                dve.tensor_copy(y_w[:].rearrange("p b d -> p (b d)"), ps_f[:])

        block = ctx.main_block(nc)

        @block.sync
        def _(sp):
            on_sync(sp)

        def keys(t):
            return (t + 1) * P

        def reach(t):
            return (0, P, 0) if t == 0 else (P - A0.WINDOW, A0.W1, P)

        @block.gpsimd
        def _(pool):
            norm.start(nc, pool=pool)
            turned.start(pool)

            def project(c, u):
                for t in range(ST):
                    pool.wait_ge(prepared.sem, prepared.at(c, t + 1))
                    pool.sem_inc(norm.turns, 1)
                    pool.tensor_scalar(ms[:, t, :], ss[:, t, :], 1.0 / HD, 1e-6, ALU.mult,
                                       ALU.add).then_inc(turned.sem, 1)
                    pool.wait_ge(turned.sem, turned.at(c, 2 * t + 1))
                    pool.tensor_tensor(rms[:, t, :], ms[:, t, :], half[:, t, :], ALU.pow).then_inc(turned.sem, 1)
                for t in range(ST):
                    k = 2 * ST + 4 * t
                    head = qk[:, t, :, 0:32]
                    pool.wait_ge(prepared.sem, prepared.at(c, ST + t + 1))
                    for n, to in enumerate((rc, rs)):
                        pool.tensor_tensor(to[:], head, rope[:, t, n:n + 1, :].to_broadcast([P, H + 1, 32]),
                                           ALU.mult).then_inc(turned.sem, 1)
                    pool.wait_ge(turned.sem, turned.at(c, k + 2))
                    pool.tensor_tensor(qk[:, t, :, 0:16], rc[:, :, 0:16], rs[:, :, 16:32],
                                       ALU.subtract).then_inc(turned.sem, 1)
                    pool.tensor_tensor(qk[:, t, :, 16:32], rc[:, :, 16:32], rs[:, :, 0:16],
                                       ALU.add).then_inc(turned.sem, 1)
                    pool.wait_ge(turned.sem, turned.at(c, k + 4))

            norm.on_pool(pool, 0)
            project(0, 0)
            norm.on_pool(pool, 1)

            def main(c, u):
                project(c + 1, 1 - u)
                norm.on_pool(pool, c + 2)

            pairs(pool, main)

        @block.tensor
        def _(pe):
            norm.start(nc, pe=pe)
            for s in (kv_mm, q_mm, front_mm, s_mm, p_tr, o_mm):
                s.start(pe)

            def project_keys(c, u):
                pe.wait_ge(norm.xT_done.sem, norm.xT_done.at(c, 1))
                pe.wait_ge(prepared.sem, prepared.at(c - 1, 3 * ST + 1))
                for t in range(ST):
                    last = pe.matmul(ps_kv[:, t * P:(t + 1) * P], norm.xT[:, u, t * P:(t + 1) * P], kv_w[:],
                                     start=True, stop=True)
                last.then_inc(kv_mm.sem, 1)

            def project_queries(c, u, t):
                pe.wait_ge(copied.sem, copied.at(c, 4 * (t - 1) + 3))
                pe.matmul(ps_q[:], norm.xT[:, u, t * P:(t + 1) * P], q_w[:], start=True,
                          stop=True).then_inc(q_mm.sem, 1)

            def mean_values(c, u):
                pe.wait_ge(copied.sem, copied.at(c, 4 * (ST - 1) + 2))
                for t in range(ST):
                    last = pe.matmul(ps_kv[0:H * NB, 2 * P:2 * P + HD], mean_w[:, t, :], v[:, u, t, :],
                                     start=(t == 0), stop=(t == ST - 1))
                last.then_inc(front_mm.sem, 1)

            def turn_keys(c, u):
                pe.wait_ge(prepared.sem, prepared.at(c, 3 * ST))
                pe.wait_ge(front_ev.sem, front_ev.at(c - 1, 3))
                for t in range(ST):
                    last = pe.transpose(ps_f[:, t * P:(t + 1) * P], kd[:, t, :, :].rearrange("p a d -> p (a d)"),
                                        ident[:])
                last.then_inc(front_mm.sem, 1)

            def turn_queries(c, t):
                pe.wait_ge(turned.sem, turned.at(c, 2 * ST + 4 * (t + 1)))
                pe.wait_ge(front_ev.sem, front_ev.at(c, t + 1))
                for b in range(HP):
                    last = pe.transpose(ps_f[:, b * P:(b + 1) * P],
                                        qk[:, t, 2 * b:2 * b + 2, :].rearrange("p a d -> p (a d)"), ident[:])
                last.then_inc(front_mm.sem, 1)

            def score(c, u, t, h):
                n = t * H + h
                if n == 0:
                    pe.wait_ge(front_ev.sem, front_ev.at(c, 3))
                    pe.wait_ge(prepared.sem, prepared.at(c, 3 * ST + 3))
                r = slice(64 * (h % 2), 64 * (h % 2) + 64)
                pe.wait_ge(least.sem, least.at(c, 3 * (n - 1)))
                pe.matmul(ps_s[n % 2][:, 0:X + keys(t)], qT[r, u, t, h // 2, :], kx[r, u, 0:X + keys(t)],
                          start=True, stop=True).then_inc(s_mm.sem, 1)

            def beside(sc, su, st, c, u, t, fc, fu, ft):
                if t == 0:
                    project_keys(c + 1, 1 - u)
                    project_queries(c + 1, 1 - u, 0)
                r = R * t
                bank = ps_t
                pe.wait_ge(mixing.sem, mixing.at(c, MIX * (t + 1)))
                pe.wait_ge(p_ev.sem, p_ev.at(c, r - 1))
                pe.sem_inc(passed, 1)
                pe.transpose(bank[r % 2][0:H * NB, 0:P], p_c[:, t, :, :].rearrange("p h n -> p (h n)"),
                             ident[:]).then_inc(p_tr.sem, 1)

                def turn_p(h):
                    i = r + 1 + h
                    pe.wait_ge(weighed.sem, weighed.at(c, 2 * H * t + min(2 * h + 3, 2 * H)))
                    pe.wait_ge(p_ev.sem, p_ev.at(c, i - 1))
                    for b in range(t + 1):
                        last = pe.transpose(bank[i % 2][:, b * P:(b + 1) * P], p_all[:, t, h, b * P:(b + 1) * P],
                                            ident[:])
                    last.then_inc(p_tr.sem, 1)

                turn_p(0)
                pe.wait_ge(p_ev.sem, p_ev.at(c, r + 1))
                pe.wait_ge(added.sem, added.at(c, t))
                pe.matmul(ps_o[:], p_cT[:], vc[:, u, :, :], start=True, stop=False,
                          skip_group_check=True).then_inc(o_mm.sem, 1)
                for h in range(H):
                    if h + 1 < H:
                        turn_p(h + 1)
                    if h + 2 < H:
                        score(sc, su, st, h + 2)
                    if t == 0 and h == 1:
                        project_queries(c + 1, 1 - u, 1)
                    if t == 0 and h == 3:
                        mean_values(c + 1, 1 - u)
                    if t == 0 and h == 5:
                        turn_keys(c + 1, 1 - u)
                    if t == 0 and h >= 6:
                        turn_queries(c + 1, h - 6)
                    if t == 1 and h == 4:
                        norm.on_tensor(pe, c + 2)
                    pe.wait_ge(p_ev.sem, p_ev.at(c, r + 2 + h))
                    for b in range(t + 1):
                        last = pe.matmul(ps_o[:, h, :], pT[:, h % 2, b, :], v[:, u, b, :], start=False,
                                         stop=(h == H - 1 and b == t), skip_group_check=True)
                    last.then_inc(o_mm.sem, 1)
                score(fc, fu, ft, 0)
                pe.wait_ge(o_ev.sem, o_ev.at(c, t + 1))
                i = r + 1 + H
                pe.wait_ge(p_ev.sem, p_ev.at(c, i - 1))
                for b in range(HP):
                    last = pe.transpose(bank[i % 2][:, b * P:(b + 1) * P],
                                        o[:, 2 * b:2 * b + 2, :].rearrange("p a d -> p (a d)"), ident[:])
                last.then_inc(p_tr.sem, 1)
                score(fc, fu, ft, 1)
                pe.wait_ge(p_ev.sem, p_ev.at(c, i + 1))
                for b in range(HP):
                    last = pe.matmul(ps_o[:, 0:2, :], oT[:, b, :], y_w[:, b, :], start=(b == 0),
                                     stop=(b == HP - 1), skip_group_check=True)
                last.then_inc(o_mm.sem, 1)

            norm.on_tensor(pe, 0)
            project_keys(0, 0)
            project_queries(0, 0, 0)
            project_queries(0, 0, 1)
            mean_values(0, 0)
            turn_keys(0, 0)
            turn_queries(0, 0)
            turn_queries(0, 1)
            norm.on_tensor(pe, 1)
            for h in range(H):
                score(0, 0, 0, h)
            score(0, 0, 1, 0)
            score(0, 0, 1, 1)

            def main(c, u):
                beside(c, u, 1, c, u, 0, c + 1, 1 - u, 0)
                beside(c + 1, 1 - u, 0, c, u, 1, c + 1, 1 - u, 1)

            pairs(pe, main)

        @block.scalar
        def _(act):
            norm.start(nc, act=act)
            for s in (copied, front_ev, exped, mix_exp, p_ev, o_ev):
                s.start(act)

            def project(c, u, t):
                act.wait_ge(front_mm.sem, front_mm.at(c - 1, 4))
                act.wait_ge(kv_mm.sem, kv_mm.at(c, 1))
                act.activation(qk[:, t, H, :], ps_kv[:, t * P:t * P + HD], ACT.Copy).then_inc(copied.sem, 1)
                act.activation(v[:, u, t, :], ps_kv[:, t * P + HD:(t + 1) * P], ACT.Copy).then_inc(copied.sem, 1)
                act.wait_ge(q_mm.sem, q_mm.at(c, t + 1))
                act.activation(qk[:, t, 0:H, :], ps_q[:], ACT.Copy).then_inc(copied.sem, 1)
                act.wait_ge(copied.sem, copied.at(c, 4 * t + 3))
                act.activation(sq[:, t, :, :], qk[:, t, :, :], ACT.Square).then_inc(copied.sem, 1)

            def turn_keys(c, u):
                act.wait_ge(front_mm.sem, front_mm.at(c, 2))
                act.activation(kx[:, u, X:X + SEQ], ps_f[:, 0:SEQ], ACT.Copy).then_inc(front_ev.sem, 1)

            def turn_queries(c, u, t):
                act.wait_ge(front_mm.sem, front_mm.at(c, 3 + t))
                act.activation(qT[:, u, t, :, :], ps_f[:].rearrange("p (b q) -> p b q", b=HP),
                               ACT.Copy).then_inc(front_ev.sem, 1)

            def weigh(c, t, h):
                n = t * H + h
                act.wait_ge(least.sem, least.at(c, 3 * n + 2))
                act.activation(p_all[:, t, h, 0:keys(t)], s_all[:, n % 2, 0:keys(t)], ACT.Exp,
                               bias=low_all[:, t, h:h + 1], scale=-1.0,
                               accum_out=total[:, t, 2, h:h + 1]).then_inc(exped.sem, 1)
                act.wait_ge(least.sem, least.at(c, 3 * n + 3))
                act.activation(p_win[:, t, h, 0:reach(t)[1]], s_win[:, n % 2, 0:reach(t)[1]], ACT.Exp,
                               bias=low_win[:, t, h:h + 1], scale=-1.0,
                               accum_out=total[:, t, 3, h:h + 1]).then_inc(exped.sem, 1)

            def mix(c, t):
                act.wait_ge(mixing.sem, mixing.at(c, MIX * t + 2))
                act.activation(e_c[:], e_c[:], ACT.Exp).then_inc(mix_exp.sem, 1)
                act.activation(sig[:], cg[:, t, :, A0.GATE:A0.GATE + 3], ACT.Exp).then_inc(mix_exp.sem, 1)
                act.wait_ge(mixing.sem, mixing.at(c, MIX * t + 3))
                act.activation(e_sink[:], e_sink[:], ACT.Exp).then_inc(mix_exp.sem, 1)

            def normal(c, u):
                norm.on_scalar(act, c, u, (q_mm.sem, q_mm.at(c - 2, ST)))

            def beside(sc, st, c, u, t, fc, ft):
                bank = ps_t
                r = R * t
                act.wait_ge(p_tr.sem, p_tr.at(c, r + 1))
                act.activation(p_cT[:], bank[r % 2][0:H * NB, 0:P], ACT.Copy).then_inc(p_ev.sem, 1)
                for h in range(H):
                    i = r + 1 + h
                    act.wait_ge(p_tr.sem, p_tr.at(c, i + 1))
                    act.wait_ge(o_mm.sem, o_mm.at(c, i - 1))
                    act.activation(pT[:, h % 2, 0:t + 1, :],
                                   bank[i % 2][:, 0:keys(t)].rearrange("p (b q) -> p b q", b=t + 1),
                                   ACT.Copy).then_inc(p_ev.sem, 1)
                    if h + 1 < H:
                        weigh(sc, st, h + 1)
                    if t == 0 and h < ST:
                        project(c + 1, 1 - u, h)
                    if t == 0 and h == 5:
                        turn_keys(c + 1, 1 - u)
                    if t == 0 and h >= 6:
                        turn_queries(c + 1, 1 - u, h - 6)
                    if t == 1 and h == 4:
                        normal(c + 2, u)
                act.wait_ge(o_mm.sem, o_mm.at(c, r + 1 + H))
                act.activation(o[:], ps_o[:], ACT.Copy).then_inc(o_ev.sem, 1)
                mix(sc, st)
                i = r + 1 + H
                act.wait_ge(p_tr.sem, p_tr.at(c, i + 1))
                act.activation(oT[:], bank[i % 2][:].rearrange("p (b q) -> p b q", b=HP),
                               ACT.Copy).then_inc(p_ev.sem, 1)

                weigh(fc, ft, 0)

            normal(0, 0)
            project(0, 0, 0)
            project(0, 0, 1)
            turn_keys(0, 0)
            turn_queries(0, 0, 0)
            turn_queries(0, 0, 1)
            normal(1, 1)
            for h in range(H):
                weigh(0, 0, h)
            mix(0, 0)
            weigh(0, 1, 0)

            def main(c, u):
                beside(c, 1, c, u, 0, c + 1, 0)
                beside(c + 1, 0, c, u, 1, c + 1, 1)

            pairs(act, main)

        @block.vector
        def _(dve):
            norm.start(nc, dve=dve)
            for s in (prepared, least, mixing, weighed, added):
                s.start(dve)

            def square_sums(c):
                for t in range(ST):
                    dve.wait_ge(copied.sem, copied.at(c, 4 * t + 4))
                    dve.tensor_reduce(ss[:, t, :], sq[:, t, :, :], AX_X, ALU.add).then_inc(prepared.sem, 1)

            def scale_rows(c):
                for t in range(ST):
                    dve.wait_ge(turned.sem, turned.at(c, 2 * t + 2))
                    dve.tensor_tensor(qk[:, t, :, :], qk[:, t, :, :],
                                      rms[:, t, :].unsqueeze(2).to_broadcast([P, H + 1, HD]),
                                      ALU.mult).then_inc(prepared.sem, 1)

            def gain_keys(c):
                for t in range(ST):
                    dve.wait_ge(turned.sem, turned.at(c, 2 * ST + 4 * (t + 1)))
                    dve.tensor_tensor(kd[:, t, :, :], qk[:, t, H:H + 1, :].to_broadcast([P, 2, HD]), gain_qk[:],
                                      ALU.mult).then_inc(prepared.sem, 1)

            def block_values(c, u):
                dve.wait_ge(front_mm.sem, front_mm.at(c, 1))
                dve.tensor_tensor(vc[:, u, :, :],
                                  ps_kv[0:H * NB, 2 * P:2 * P + HD].unsqueeze(1).to_broadcast([H * NB, H, HD]),
                                  diagonal[:].unsqueeze(2).to_broadcast([H * NB, H, HD]),
                                  ALU.mult).then_inc(prepared.sem, 1)

            def block_keys(c, u):
                dve.wait_ge(front_ev.sem, front_ev.at(c, 1))
                dve.tensor_reduce(kc[:], kx[:, u, X:X + SEQ].rearrange("p (n k) -> p n k", n=NB), AX_X,
                                  ALU.add).then_inc(prepared.sem, 1)
                dve.wait_ge(prepared.sem, prepared.at(c, 3 * ST + 2))
                dve.tensor_scalar(kx[:, u, 0:NB], kc[:], 1.0 / A0.CR, None, ALU.mult).then_inc(prepared.sem, 1)

            def mask(c, t, h):
                k0, count, col = reach(t)
                n = t * H + h
                dve.wait_ge(s_mm.sem, s_mm.at(c, n + 1))
                dve.wait_ge(exped.sem, exped.at(c, 2 * (n - 1)))
                dve.tensor_tensor(cg[:, t, h, :], ps_s[n % 2][:, 0:C], extra[:, t, h, :],
                                  ALU.add).then_inc(least.sem, 1)
                dve.tensor_tensor_reduce(s_all[:, n % 2, 0:keys(t)], ps_s[n % 2][:, X:X + keys(t)],
                                         causal[:, P * t:P * t + keys(t)], 1.0, 3.0e38, ALU.add, ALU.min,
                                         low_all[:, t, h:h + 1]).then_inc(least.sem, 1)
                dve.tensor_tensor_reduce(s_win[:, n % 2, 0:count], ps_s[n % 2][:, X + k0:X + k0 + count],
                                         window[:, col:col + count], 1.0, extra[:, t, h, A0.SINK:A0.SINK + 1],
                                         ALU.add, ALU.min, low_win[:, t, h:h + 1]).then_inc(least.sem, 1)

            def mix(c, t):
                k = MIX * t

                def step(ins):
                    nonlocal k
                    k += 1
                    ins.then_inc(mixing.sem, 1)

                def settled():
                    dve.wait_ge(mixing.sem, mixing.at(c, k))

                def wide(a, n):
                    return a.unsqueeze(2).to_broadcast([P, H, n])

                dve.wait_ge(least.sem, least.at(c, 3 * H * (t + 1)))
                step(dve.tensor_reduce(low_c[:], cg[:, t, :, 0:NB + 1], AX_X, ALU.min))
                settled()
                step(dve.tensor_tensor(e_c[:], wide(low_c[:], NB + 1), cg[:, t, :, 0:NB + 1], ALU.subtract))
                step(dve.tensor_tensor(e_sink[:], sink[:], low_win[:, t, :], ALU.add))
                dve.wait_ge(mix_exp.sem, mix_exp.at(c, 3 * t + 2))
                step(dve.tensor_scalar(sig[:], sig[:], 1.0, None, ALU.add))
                settled()
                step(dve.reciprocal(sig[:], sig[:]))
                settled()
                step(dve.tensor_reduce(total[:, t, 0, :], sig[:], AX_X, ALU.add))
                settled()
                step(dve.tensor_scalar(total[:, t, 0, :], total[:, t, 0, :], 1e-6, None, ALU.max))
                step(dve.tensor_reduce(total[:, t, 1, :], e_c[:], AX_X, ALU.add))
                dve.wait_ge(mix_exp.sem, mix_exp.at(c, 3 * t + 3))
                dve.wait_ge(exped.sem, exped.at(c, 2 * H * (t + 1)))
                step(dve.tensor_tensor(total[:, t, 3, :], total[:, t, 3, :], e_sink[:], ALU.add))
                settled()
                step(dve.reciprocal(inverse[:], total[:, t, :, :]))
                settled()
                step(dve.tensor_tensor(ratio[:], inverse[:, 1:4, :], inverse[:, 0:1, :].to_broadcast([P, 3, H]),
                                       ALU.mult))
                settled()
                step(dve.tensor_tensor(factor[:, t, :, :], ratio[:], sig[:].rearrange("p h g -> p g h"), ALU.mult))
                settled()
                step(dve.scalar_tensor_tensor(p_c[:, t, :, :], e_c[:, :, 0:NB], any_block[:, t:t + 1],
                                              wide(factor[:, t, 0, :], NB), ALU.mult, ALU.mult))
                assert k == MIX * (t + 1)

            def scale_all(c, t, h):
                dve.wait_ge(mixing.sem, mixing.at(c, MIX * (t + 1)))
                dve.tensor_scalar(p_all[:, t, h, 0:keys(t)], p_all[:, t, h, 0:keys(t)],
                                  factor[:, t, 1, h:h + 1], None, ALU.mult).then_inc(weighed.sem, 1)

            def add_window(c, t, h):
                k0, count, _ = reach(t)
                dve.wait_ge(weighed.sem, weighed.at(c, 2 * H * t + max(2 * h, 1)))
                dve.scalar_tensor_tensor(p_all[:, t, h, k0:k0 + count], p_win[:, t, h, 0:count],
                                         factor[:, t, 2, h:h + 1], p_all[:, t, h, k0:k0 + count],
                                         ALU.mult, ALU.add).then_inc(weighed.sem, 1)

            def finish(c, t):
                dve.wait_ge(o_mm.sem, o_mm.at(c, R * (t + 1)))
                rows = x[:, c * ST + t, :]
                dve.tensor_tensor(rows, ps_o[:, 0:2, :].rearrange("p a d -> p (a d)"), rows,
                                  ALU.add).then_inc(added.sem, 1)

            def beside(sc, st, c, u, t, fc, ft):
                scale_all(c, t, 0)
                scale_all(c, t, 1)
                add_window(c, t, 0)
                for h in range(H):
                    if h + 2 < H:
                        scale_all(c, t, h + 2)
                    if h + 1 < H:
                        add_window(c, t, h + 1)
                        mask(sc, st, h + 1)
                    if t == 0 and h == 2:
                        square_sums(c + 1)
                    if t == 0 and h == 3:
                        scale_rows(c + 1)
                    if t == 0 and h == 5:
                        gain_keys(c + 1)
                        block_values(c + 1, 1 - u)
                    if t == 1 and h == 1:
                        norm.on_vector(dve, c + 2)
                    if t == 1 and h == 3:
                        norm.on_vector_scale(dve, c + 2)
                if t == 0:
                    block_keys(c + 1, 1 - u)
                mix(sc, st)
                mask(fc, ft, 0)
                finish(c, t)

            norm.on_vector(dve, 0)
            norm.on_vector_scale(dve, 0)
            square_sums(0)
            scale_rows(0)
            gain_keys(0)
            block_values(0, 0)
            block_keys(0, 0)
            norm.on_vector(dve, 1)
            norm.on_vector_scale(dve, 1)
            for h in range(H):
                mask(0, 0, h)
            mix(0, 0)
            mask(0, 1, 0)

            def main(c, u):
                beside(c, 1, c, u, 0, c + 1, 0)
                beside(c + 1, 0, c, u, 1, c + 1, 1)

            pairs(dve, main)

        ctx.clear(nc)


def single_attention(nc, x, ident, w, results):
    HD = D
    with Phase() as ctx:
        def sb(n, shape):
            return ctx.enter_context(nc.sbuf_tensor(f"one_{n}", shape, F32))

        def ps(n, shape):
            return ctx.enter_context(nc.psum_tensor(f"one_{n}", shape, F32))

        def sem(n):
            return ctx.semaphore(nc, f"one_{n}")

        def signal(n, per):
            return Signal(sem(n), per)

        ps_qk = ps("ps_qk", [P, 2, SEQ])
        ps_v = ps("ps_v", [P, ST, HD])
        ps_s = [ps(f"ps_s{i}", [P, SEQ]) for i in range(2)]
        ps_t = ps("ps_t", [P, 3, P])
        ps_o = ps("ps_o", [P, ST, P])
        ps_y = ps("ps_y", [P, ST, D])
        norm = Norm(nc, ctx, "one", x, ident, ST)

        wq, wk, wv, wo = (sb(n, [P, P]) for n in ("wq", "wk", "wv", "wo"))
        bq, bk = sb("bq", [P, 1]), sb("bk", [P, 1])
        bv, bo = sb("bv", [P, HD]), sb("bo", [P, D])
        causal = sb("causal", [P, P + SEQ])
        qT = sb("qT", [P, 2, SEQ])
        kT = sb("kT", [P, 2, SEQ])
        v = sb("v", [P, 2, ST, HD])
        s_all = sb("s_all", [P, ST, SEQ])
        low = sb("low", [P, ST])
        e = sb("e", [P, 2, ST, SEQ])
        total = sb("total", [P, 2, ST])
        inverse = sb("inverse", [P, ST])
        eT = sb("eT", [P, 3, P])
        oT = sb("oT", [P, ST, P])
        loaded = sem("loaded")
        proj_mm = signal("proj_mm", 2)
        biased = signal("biased", 3)
        s_mm = signal("s_mm", ST)
        least = signal("least", ST)
        exped = signal("exped", ST)
        inverted = signal("inverted", 1)
        e_tr = signal("e_tr", 1)
        e_ev = signal("e_ev", 1)
        o_mm = signal("o_mm", 1)
        o_ev = signal("o_ev", 1)
        y_mm = signal("y_mm", 1)
        added = signal("added", 1 + ST)
        pieces = [(wq, "b_wq"), (wk, "b_wk"), (wv, "b_wv"), (wo, "b_wo"), (bq, "b_bq"), (bk, "b_bk"),
                  (bv, "b_bv"), (bo, "b_bo"), (causal, "causal")]

        with nc.Block() as block:
            @block.sync
            def _(sp):
                for to, of in pieces:
                    sp.dma_start(to[:], w[of]).then_inc(loaded, 16)
                sp.wait_ge(loaded, 16 * len(pieces))

        combine = Combine(nc, ctx, "one", x, SEQS + 3, *results)
        block = ctx.main_block(nc)

        BLOCKS = ((0, 0), (1, 0), (1, 1))

        @block.gpsimd
        def _(pool):
            norm.start(nc, pool=pool)
            combine.gather(pool, 0, 0)
            combine.gather(pool, 1, 1)
            norm.on_pool(pool, 0)
            norm.on_pool(pool, 1)
            combine.gather(pool, 2, 0)

            def body(c, u):
                norm.on_pool(pool, c + 2)
                combine.gather(pool, c + 3, 1 - u)

            pairs(pool, body)
            combine.finish(pool)

        @block.tensor
        def _(pe):
            norm.start(nc, pe=pe)
            for s in (proj_mm, s_mm, e_tr, o_mm, y_mm):
                s.start(pe)

            def project(c, u):
                pe.wait_ge(norm.xT_done.sem, norm.xT_done.at(c, 1))
                pe.wait_ge(biased.sem, biased.at(c - 1, 3))
                pe.matmul(ps_qk[:, 0, :], wq[:], norm.xT[:, u, :], start=True, stop=True)
                pe.matmul(ps_qk[:, 1, :], wk[:], norm.xT[:, u, :], start=True, stop=True).then_inc(proj_mm.sem, 1)
                for t in range(ST):
                    last = pe.matmul(ps_v[:, t, :], norm.xT[:, u, t * P:(t + 1) * P], wv[:], start=True, stop=True)
                last.then_inc(proj_mm.sem, 1)

            def scores(c, u):
                pe.wait_ge(biased.sem, biased.at(c, 3))
                for t in range(ST):
                    pe.wait_ge(least.sem, least.at(c - 1, t + 1))
                    pe.matmul(ps_s[t][:, 0:(t + 1) * P], qT[:, u, t * P:(t + 1) * P], kT[:, u, 0:(t + 1) * P],
                              start=True, stop=True).then_inc(s_mm.sem, 1)

            def turn_e(c, u):
                pe.wait_ge(exped.sem, exped.at(c, ST))
                pe.wait_ge(e_ev.sem, e_ev.at(c - 1, 1))
                for n, (t, k) in enumerate(BLOCKS):
                    last = pe.transpose(ps_t[:, n, :], e[:, u, t, k * P:(k + 1) * P], ident[:])
                last.then_inc(e_tr.sem, 1)

            def sum_values(c, u):
                pe.wait_ge(e_ev.sem, e_ev.at(c, 1))
                pe.wait_ge(o_ev.sem, o_ev.at(c - 1, 1))
                for n, (t, k) in enumerate(BLOCKS):
                    last = pe.matmul(ps_o[:, t, :], v[:, u, k, :], eT[:, n, :], start=(k == 0), stop=(k == t))
                last.then_inc(o_mm.sem, 1)

            def project_rows(c):
                pe.wait_ge(o_ev.sem, o_ev.at(c, 1))
                pe.wait_ge(added.sem, added.at(c - 1, 1 + ST))
                for t in range(ST):
                    last = pe.matmul(ps_y[:, t, :], oT[:, t, :], wo[:], start=True, stop=True)
                last.then_inc(y_mm.sem, 1)

            for c in range(2):
                norm.on_tensor(pe, c)
                project(c, c)
            scores(0, 0)

            def body(c, u):
                turn_e(c, u)
                scores(c + 1, 1 - u)
                sum_values(c, u)
                norm.on_tensor(pe, c + 2)
                project_rows(c)
                project(c + 2, u)

            pairs(pe, body)

        @block.scalar
        def _(act):
            norm.start(nc, act=act)
            for s in (exped, e_ev, o_ev):
                s.start(act)

            def normal(c, u):
                norm.on_scalar(act, c, u, (proj_mm.sem, proj_mm.at(c - 2, 2)))

            def weigh(c, u):
                for t in range(ST):
                    act.wait_ge(least.sem, least.at(c, t + 1))
                    act.activation(e[:, u, t, 0:(t + 1) * P], s_all[:, t, 0:(t + 1) * P], ACT.Exp,
                                   bias=low[:, t:t + 1], scale=-1.0,
                                   accum_out=total[:, u, t:t + 1]).then_inc(exped.sem, 1)

            normal(0, 0)
            normal(1, 1)
            weigh(0, 0)

            def body(c, u):
                act.wait_ge(e_tr.sem, e_tr.at(c, 1))
                act.wait_ge(o_mm.sem, o_mm.at(c - 1, 1))
                act.activation(eT[:], ps_t[:], ACT.Copy).then_inc(e_ev.sem, 1)
                weigh(c + 1, 1 - u)
                act.wait_ge(o_mm.sem, o_mm.at(c, 1))
                act.wait_ge(y_mm.sem, y_mm.at(c - 1, 1))
                act.activation(oT[:], ps_o[:], ACT.Copy).then_inc(o_ev.sem, 1)
                normal(c + 2, u)

            pairs(act, body)

        @block.vector
        def _(dve):
            norm.start(nc, dve=dve)
            combine.start(dve)
            for s in (biased, least, inverted, added):
                s.start(dve)

            def statistics(c, u):
                for t in range(ST):
                    combine.add(dve, c, u, t)
                combine.settle(dve, c)
                norm.on_vector(dve, c)

            def project(c, u):
                dve.wait_ge(proj_mm.sem, proj_mm.at(c, 1))
                dve.tensor_scalar(qT[:, u, :], ps_qk[:, 0, :], bq[:, 0:1], -(float(HD) ** -0.5), ALU.add,
                                  ALU.mult).then_inc(biased.sem, 1)
                dve.tensor_scalar(kT[:, u, :], ps_qk[:, 1, :], bk[:, 0:1], None, ALU.add).then_inc(biased.sem, 1)
                dve.wait_ge(proj_mm.sem, proj_mm.at(c, 2))
                dve.tensor_tensor(v[:, u, :, :], ps_v[:], bv[:].unsqueeze(1).to_broadcast([P, ST, HD]),
                                  ALU.add).then_inc(biased.sem, 1)

            def mask(c):
                for t in range(ST):
                    dve.wait_ge(s_mm.sem, s_mm.at(c, t + 1))
                    dve.wait_ge(exped.sem, exped.at(c - 1, t + 1))
                    dve.sem_inc(norm.turns, 1)
                    dve.tensor_tensor_reduce(s_all[:, t, 0:(t + 1) * P], ps_s[t][:, 0:(t + 1) * P],
                                             causal[:, P * t:P * t + (t + 1) * P], 1.0, 3.0e38, ALU.add, ALU.min,
                                             low[:, t:t + 1]).then_inc(least.sem, 1)

            def add_rows(c):
                dve.wait_ge(y_mm.sem, y_mm.at(c, 1))
                dve.wait_ge(inverted.sem, inverted.at(c, 1))
                dve.wait_ge(added.sem, added.at(c, 1))
                for t in range(ST):
                    dve.scalar_tensor_tensor(x[:, c * ST + t, :], ps_y[:, t, :], inverse[:, t:t + 1],
                                             x[:, c * ST + t, :], ALU.mult, ALU.add).then_inc(added.sem, 1)

            combine.ask(dve, 0, 0)
            combine.ask(dve, 1, 1)
            for c in range(2):
                statistics(c, c)
                norm.on_vector_scale(dve, c)
                if c == 0:
                    combine.ask(dve, 2, 0)
                project(c, c)
            mask(0)

            def body(c, u):
                combine.ask(dve, c + 3, 1 - u)
                statistics(c + 2, u)
                mask(c + 1)
                norm.on_vector_scale(dve, c + 2)
                dve.wait_ge(exped.sem, exped.at(c, ST))
                dve.reciprocal(inverse[:], total[:, u, :]).then_inc(inverted.sem, 1)
                dve.tensor_tensor(x[:, bass.ts(c, ST), :], x[:, bass.ts(c, ST), :],
                                  bo[:].unsqueeze(1).to_broadcast([P, ST, D]), ALU.add).then_inc(added.sem, 1)
                add_rows(c)
                project(c + 2, u)

            pairs(dve, body)

        ctx.clear(nc)


class G1:
    H, HD, KVH = 16, 64, 4
    HP = H // 2
    IN = 64
    REP = H // KVH
    OH = 8


def grouped_attention(nc, x, ident, w, results):
    H, HD, KVH, HP, IN, REP, OH = G1.H, G1.HD, G1.KVH, G1.HP, G1.IN, G1.REP, G1.OH
    F = 3 + HP // 2
    with Phase() as ctx:
        def sb(n, shape):
            return ctx.enter_context(nc.sbuf_tensor(f"grp_{n}", shape, F32))

        def ps(n, shape):
            return ctx.enter_context(nc.psum_tensor(f"grp_{n}", shape, F32))

        def sem(n):
            return ctx.semaphore(nc, f"grp_{n}")

        def signal(n, per):
            return Signal(sem(n), per)

        ps_f = ps("ps_f", [P, 512])
        ps_s = [ps(f"ps_s{i}", [P, SEQ]) for i in range(2)]
        ps_t = [ps(f"ps_t{i}", [P, 512]) for i in range(2)]
        ps_o = ps("ps_o", [P, OH, HD])
        ps_y = ps("ps_y", [P, D])
        ps_n = ps("ps_n", [P, 512])

        wq_in = sb("wq_in", [P, H, HD // 2, 2])
        wq = sb("wq", [P, H * HD])
        turn_a = sb("turn_a", [P, H, HD // 2])
        turn_b = sb("turn_b", [P, H, HD // 2])
        wk = sb("wk", [P, KVH, 2, HD])
        wv = sb("wv", [P, KVH * HD])
        wo = sb("wo", [P, HP, D])
        phase = sb("phase", [P, H])
        wave = sb("wave", [P, 2, H])
        steps = sb("steps", [P, 2, H])
        slope = sb("slope", [P, H])
        keys_at = sb("keys_at", [P, P + SEQ])
        causal = sb("causal", [P, P + SEQ])
        table = sb("table", [P, H, P + SEQ])

        kT = sb("kT", [P, 2, KVH, SEQ])
        v = sb("v", [P, 2, ST, KVH * HD])
        qT = sb("qT", [P, 2, HP, SEQ])
        s_all = sb("s_all", [P, 2, SEQ])
        low = sb("low", [P, ST, H])
        e = sb("e", [P, ST, H, SEQ])
        total = sb("total", [P, ST, H])
        bottom = sb("bottom", [P, ST, H])
        inverse = sb("inverse", [P, ST, H])
        eT = sb("eT", [P, 2, ST, P])
        o = sb("o", [P, OH, HD])
        oT = sb("oT", [P, OH // 2, P])

        loaded, waved, sloped = (sem(n) for n in ("loaded", "waved", "sloped"))
        front_mm = signal("front_mm", F)
        front_ev = signal("front_ev", F)
        U = ST * H
        s_mm = signal("s_mm", U)
        least = signal("least", U)
        exped = signal("exped", U)
        inverted = signal("inverted", 2 * ST)
        e_tr = signal("e_tr", U)
        e_ev = signal("e_ev", U)
        o_mm = signal("o_mm", U)
        HALVES = ST * H // OH
        o_ev = signal("o_ev", HALVES)
        o_tr = signal("o_tr", HALVES)
        oT_ev = signal("oT_ev", HALVES)
        y_mm = signal("y_mm", HALVES)
        norm = Norm(nc, ctx, "grp", x, ident, ST, ps=ps_n,
                    bank_free=lambda c: (oT_ev.sem, oT_ev.at(c - 2, HALVES)))
        added = signal("added", ST)
        pieces = [(wq_in[IN:P, :, :, :], w["c_wq"]), (wk[IN:P, :, :, :], w["c_wk"]), (wv[0:IN, :], w["c_wv"]),
                  (wo[:], w["c_wo"]), (phase[:], w["c_phase"]), (slope[:], w["c_slope"]),
                  (keys_at[:], w["keys_at"]), (causal[:], w["causal"])]

        with nc.Block() as block:
            @block.sync
            def _(sp):
                for to, of in pieces:
                    sp.dma_start(to, of).then_inc(loaded, 16)

            @block.scalar
            def _(act):
                act.wait_ge(loaded, 16 * len(pieces))
                act.activation(slope[:], slope[:], ACT.Exp).then_inc(sloped, 1)
                act.wait_ge(waved, 7)
                act.activation(wave[:], wave[:], ACT.Sin).then_inc(sloped, 1)

            @block.vector
            def _(dve):
                def step(ins, n):
                    ins.then_inc(waved, 1)
                    dve.wait_ge(waved, n)

                dve.wait_ge(loaded, 16 * len(pieces))
                step(dve.tensor_scalar(wave[:, 0, :], phase[:], 1.0, math.pi / 2, ALU.mult, ALU.add), 1)
                step(dve.tensor_copy(wave[:, 1, :], phase[:]), 2)
                step(dve.tensor_scalar(steps[:], wave[:], 1 / (2 * math.pi), ROUND, ALU.mult, ALU.add), 3)
                step(dve.tensor_scalar(steps[:], steps[:], ROUND, None, ALU.subtract), 4)
                step(dve.scalar_tensor_tensor(wave[:], steps[:], -TURN_HIGH, wave[:], ALU.mult, ALU.add), 5)
                step(dve.scalar_tensor_tensor(wave[:], steps[:], -TURN_LOW, wave[:], ALU.mult, ALU.add), 6)
                step(dve.tensor_scalar(wave[:], wave[:], HALF_TURN, -HALF_TURN, ALU.min, ALU.max), 7)
                dve.wait_ge(sloped, 2)
                step(dve.tensor_scalar(wave[:], wave[:], -(float(HD) ** -0.5), None, ALU.mult), 8)
                even, odd = wq_in[IN:P, :, :, 0], wq_in[IN:P, :, :, 1]
                to = wq[IN:P, :].rearrange("p (h d a) -> p h d a", h=H, a=2)
                cos, sin = (wave[IN:P, n, :].unsqueeze(2).to_broadcast([IN, H, HD // 2]) for n in range(2))
                a, b = turn_a[IN:P, :, :], turn_b[IN:P, :, :]
                step(dve.tensor_tensor(a, even, cos, ALU.mult), 9)
                step(dve.tensor_tensor(b, odd, sin, ALU.mult), 10)
                step(dve.tensor_tensor(to[:, :, :, 0], a, b, ALU.subtract), 11)
                step(dve.tensor_tensor(a, even, sin, ALU.mult), 12)
                step(dve.tensor_tensor(b, odd, cos, ALU.mult), 13)
                step(dve.tensor_tensor(to[:, :, :, 1], a, b, ALU.add), 14)
                for h in range(H):
                    dve.scalar_tensor_tensor(table[:, h, :], keys_at[:], slope[:, h:h + 1], causal[:],
                                             ALU.mult, ALU.add)

        combine = Combine(nc, ctx, "grp", x, SEQS + 2, *results)
        block = ctx.main_block(nc)

        def keys(t):
            return (t + 1) * P

        FIRST = 5

        @block.gpsimd
        def _(pool):
            norm.start(nc, pool=pool)
            combine.gather(pool, 0, 0)
            combine.gather(pool, 1, 1)
            norm.on_pool(pool, 0)

            def main(c, u):
                norm.on_pool(pool, c + 1)
                combine.gather(pool, c + 2, u)

            pairs(pool, main)
            combine.finish(pool)

        @block.tensor
        def _(pe):
            norm.start(nc, pe=pe)
            for s in (front_mm, s_mm, e_tr, o_mm, o_tr, y_mm):
                s.start(pe)

            def project(c, u, n):
                if n == 0:
                    pe.wait_ge(norm.xT_done.sem, norm.xT_done.at(c, 1))
                pe.wait_ge(front_ev.sem, front_ev.at(c, n))
                for i in range(2):
                    half = ps_f[:, i * SEQ:(i + 1) * SEQ]
                    if n < 2:
                        last = pe.matmul(half, wk[IN:P, 2 * n + i, :, :].rearrange("p a d -> p (a d)"),
                                         norm.xT[IN:P, u, :], start=True, stop=True)
                    elif n == 2:
                        last = pe.matmul(half, norm.xT[0:IN, u, i * P:(i + 1) * P], wv[0:IN, :],
                                         start=True, stop=True)
                    else:
                        b = 2 * (n - 3) + i
                        last = pe.matmul(half, wq[IN:P, b * P:(b + 1) * P], norm.xT[IN:P, u, :],
                                         start=True, stop=True)
                last.then_inc(front_mm.sem, 1)

            def score(c, u, t, h):
                n = t * H + h
                r = slice(64 * (h % 2), 64 * (h % 2) + 64)
                if n == 0:
                    pe.wait_ge(front_ev.sem, front_ev.at(c, F))
                pe.wait_ge(least.sem, least.at(c, n - 1))
                pe.matmul(ps_s[n % 2][:, 0:keys(t)], qT[r, u, h // 2, t * P:(t + 1) * P],
                          kT[r, u, h // REP, 0:keys(t)], start=True, stop=True).then_inc(s_mm.sem, 1)

            def turn_e(c, t, h):
                n = t * H + h
                pe.wait_ge(exped.sem, exped.at(c, n + 1))
                pe.wait_ge(e_ev.sem, e_ev.at(c, n - 1))
                for b in range(t + 1):
                    last = pe.transpose(ps_t[n % 2][:, b * P:(b + 1) * P], e[:, t, h, b * P:(b + 1) * P],
                                        ident[:])
                last.then_inc(e_tr.sem, 1)

            def sum_values(c, u, t, h):
                n = t * H + h
                pe.wait_ge(e_ev.sem, e_ev.at(c, n + 1))
                if h % OH == 0:
                    pe.wait_ge(o_ev.sem, o_ev.at(c, n // OH))
                for b in range(t + 1):
                    g = h // REP
                    last = pe.matmul(ps_o[:, h % OH, :], eT[:, n % 2, b, :], v[:, u, b, g * HD:(g + 1) * HD],
                                     start=(b == 0), stop=(b == t))
                last.then_inc(o_mm.sem, 1)

            def turn_rows(c, m):
                pe.wait_ge(o_ev.sem, o_ev.at(c, m + 1))
                pe.wait_ge(oT_ev.sem, oT_ev.at(c, m))
                pe.wait_ge(norm.xT_done.sem, norm.xT_done.at(c + 1, 1))
                for b in range(OH // 2):
                    last = pe.transpose(ps_n[:, b * P:(b + 1) * P],
                                        o[:, 2 * b:2 * b + 2, :].rearrange("p a d -> p (a d)"), ident[:])
                last.then_inc(o_tr.sem, 1)

            def project_rows(c, t, half):
                m = t * (H // OH) + half
                pe.wait_ge(oT_ev.sem, oT_ev.at(c, m + 1))
                if half == 0:
                    pe.wait_ge(added.sem, added.at(c, t))
                for b in range(OH // 2):
                    last = pe.matmul(ps_y[:], oT[:, b, :], wo[:, half * (OH // 2) + b, :],
                                     start=(half == 0 and b == 0), stop=(half == 1 and b == OH // 2 - 1))
                last.then_inc(y_mm.sem, 1)

            def beside(sc, su, st, c, u, t):
                turn_e(c, t, 0)
                score(sc, su, st, 0)
                for h in range(H):
                    if h + 1 < H:
                        turn_e(c, t, h + 1)
                        score(sc, su, st, h + 1)
                    if t == 0 and h == FIRST - 1:
                        norm.on_tensor(pe, c + 1)
                    if t == 0 and FIRST <= h < FIRST + F:
                        project(c + 1, 1 - u, h - FIRST)
                    sum_values(c, u, t, h)
                    if h == OH:
                        turn_rows(c, 2 * t)
                    if h == OH + 1:
                        project_rows(c, t, 0)
                turn_rows(c, 2 * t + 1)
                project_rows(c, t, 1)

            norm.on_tensor(pe, 0)
            for n in range(F):
                project(0, 0, n)
            for h in range(H):
                score(0, 0, 0, h)

            def main(c, u):
                beside(c, u, 1, c, u, 0)
                beside(c + 1, 1 - u, 0, c, u, 1)

            pairs(pe, main)

        @block.scalar
        def _(act):
            norm.start(nc, act=act)
            for s in (exped, e_ev):
                s.start(act)

            def weigh(c, t, h):
                n = t * H + h
                act.wait_ge(least.sem, least.at(c, n + 1))
                act.activation(e[:, t, h, 0:keys(t)], s_all[:, n % 2, 0:keys(t)], ACT.Exp,
                               bias=low[:, t, h:h + 1], scale=-1.0,
                               accum_out=total[:, t, h:h + 1]).then_inc(exped.sem, 1)

            def turned(c, t, h):
                n = t * H + h
                act.wait_ge(e_tr.sem, e_tr.at(c, n + 1))
                act.wait_ge(o_mm.sem, o_mm.at(c, n - 1))
                act.activation(eT[:, n % 2, 0:t + 1, :],
                               ps_t[n % 2][:, 0:keys(t)].rearrange("p (b q) -> p b q", b=t + 1),
                               ACT.Copy).then_inc(e_ev.sem, 1)

            def normal(c, u):
                norm.on_scalar(act, c, u, (front_mm.sem, front_mm.at(c - 2, F)))

            def beside(sc, st, c, u, t):
                for h in range(H):
                    turned(c, t, h)
                    weigh(sc, st, h)
                    if t == 0 and h == FIRST - 1:
                        normal(c + 1, 1 - u)

            normal(0, 0)
            for h in range(H):
                weigh(0, 0, h)

            def main(c, u):
                beside(c, 1, c, u, 0)
                beside(c + 1, 0, c, u, 1)

            pairs(act, main)

        @block.vector
        def _(dve):
            norm.start(nc, dve=dve)
            combine.start(dve)
            for s in (front_ev, least, inverted, o_ev, oT_ev, added):
                s.start(dve)

            def projected(c, u, n):
                if n < 2:
                    to = kT[:, u, 2 * n:2 * n + 2, :]
                elif n == 2:
                    to = v[:, u, :, :]
                else:
                    to = qT[:, u, 2 * (n - 3):2 * (n - 3) + 2, :]
                dve.wait_ge(front_mm.sem, front_mm.at(c, n + 1))
                dve.tensor_copy(to.rearrange("p a k -> p (a k)"), ps_f[:]).then_inc(front_ev.sem, 1)

            def mask(c, t, h):
                n = t * H + h
                dve.wait_ge(s_mm.sem, s_mm.at(c, n + 1))
                dve.wait_ge(exped.sem, exped.at(c, n - 1))
                dve.sem_inc(norm.turns, 1)
                dve.tensor_tensor_reduce(s_all[:, n % 2, 0:keys(t)], ps_s[n % 2][:, 0:keys(t)],
                                         table[:, h, P * t:P * t + keys(t)], 1.0, 3.0e38, ALU.add, ALU.min,
                                         low[:, t, h:h + 1]).then_inc(least.sem, 1)

            def invert(c, t):
                dve.wait_ge(exped.sem, exped.at(c, H * (t + 1)))
                dve.sem_inc(norm.turns, 1)
                dve.tensor_scalar(bottom[:, t, :], total[:, t, :], 1.0, None, ALU.add).then_inc(inverted.sem, 1)
                dve.wait_ge(inverted.sem, inverted.at(c, 2 * t + 1))
                dve.reciprocal(inverse[:, t, :], bottom[:, t, :]).then_inc(inverted.sem, 1)

            def divide(c, t, half):
                m = t * (H // OH) + half
                dve.wait_ge(inverted.sem, inverted.at(c, 2 * t + 2))
                dve.wait_ge(o_mm.sem, o_mm.at(c, (m + 1) * OH))
                dve.wait_ge(o_tr.sem, o_tr.at(c, m))
                dve.tensor_tensor(o[:], ps_o[:],
                                  inverse[:, t, half * OH:(half + 1) * OH].unsqueeze(2).to_broadcast([P, OH, HD]),
                                  ALU.mult).then_inc(o_ev.sem, 1)

            def rows_turned(c, m):
                dve.wait_ge(o_tr.sem, o_tr.at(c, m + 1))
                dve.wait_ge(y_mm.sem, y_mm.at(c, m))
                dve.tensor_copy(oT[:].rearrange("p b q -> p (b q)"), ps_n[:]).then_inc(oT_ev.sem, 1)

            def beside(sc, st, c, u, t):
                for h in range(H):
                    mask(sc, st, h)
                    if h == 0:
                        invert(c, t)
                    if t == 0 and h < ST:
                        combine.add(dve, c + 1, 1 - u, h)
                    if t == 0 and h == 2:
                        combine.settle(dve, c + 1)
                        norm.on_vector(dve, c + 1)
                    if t == 0 and h == 3:
                        norm.on_vector_scale(dve, c + 1)
                    if t == 1 and h == 4:
                        combine.ask(dve, c + 2, u)
                    if h == OH:
                        divide(c, t, 0)
                    if h == OH + 1:
                        rows_turned(c, 2 * t)
                    if t == 0 and FIRST <= h < FIRST + F:
                        projected(c + 1, 1 - u, h - FIRST)
                divide(c, t, 1)
                rows_turned(c, 2 * t + 1)
                dve.wait_ge(y_mm.sem, y_mm.at(c, (H // OH) * (t + 1)))
                dve.tensor_tensor(x[:, c * ST + t, :], ps_y[:], x[:, c * ST + t, :], ALU.add).then_inc(added.sem, 1)

            combine.ask(dve, 0, 0)
            combine.ask(dve, 1, 1)
            for t in range(ST):
                combine.add(dve, 0, 0, t)
            combine.settle(dve, 0)
            norm.on_vector(dve, 0)
            norm.on_vector_scale(dve, 0)
            for n in range(F):
                projected(0, 0, n)
            for h in range(H):
                mask(0, 0, h)

            def main(c, u):
                beside(c, 1, c, u, 0)
                beside(c + 1, 0, c, u, 1)

            pairs(dve, main)

        ctx.clear(nc)


class H1:
    LAYERS, H, HD = 4, 16, 8
    WRAP = D + HD
    HB = 4 * D // P


def spectral_layers(nc, rows_x, ident, w):
    HD, WRAP, HB = H1.HD, H1.WRAP, H1.HB
    with Phase() as ctx:
        def sb(n, shape):
            return ctx.enter_context(nc.sbuf_tensor(f"spec_{n}", shape, F32))

        def ps(n, shape):
            return ctx.enter_context(nc.psum_tensor(f"spec_{n}", shape, F32))

        def sem(n):
            return ctx.semaphore(nc, f"spec_{n}")

        def signal(n, per):
            return Signal(sem(n), per)

        ps_n = ps("ps_n", [P, SEQ])
        ps_x = ps("ps_x", [P, 3, WRAP])
        ps_d = ps("ps_d", [P, 3, D])
        ps_w = ps("ps_w", [P, SEQ])
        ps_z = ps("ps_z", [P, SEQ])
        ps_y = ps("ps_y", [P, ST, D])
        ps_h = [ps(f"ps_h{i}", [P, 2, SEQ]) for i in range(2)]

        x = sb("y", [P, TILES + 3 * ST, D])
        ln = sb("ln", [P, 4])
        qkv_w = sb("qkv_w", [P, 3, WRAP])
        qkv_b = sb("qkv_b", [P, 3, WRAP])
        proj_w = sb("proj_w", [P, D])
        head_proj = sb("head_proj", [P, D])
        proj_b = sb("proj_b", [1, D])
        fc_w = sb("fc_w", [P, 4 * D])
        fc_b = sb("fc_b", [P, HB])
        mp_w = sb("mp_w", [P, HB, D])
        mp_b = sb("mp_b", [1, D])
        one = sb("one", [1, P])
        hartley = sb("hartley", [P, P])
        filt = sb("filt", [P, SEQ])
        quarter = sb("quarter", [P, 1])

        dT = sb("dT", [P, 2, SEQ])
        rows = sb("rows", [P, 2, ST, 3, WRAP])
        diff = sb("diff", [P, 2, ST, 3, D])
        cosine = sb("cosine", [P, 2, ST, 3, D])
        turns_of = sb("turns_of", [P, ST, 3, D])
        whole = sb("whole", [P, ST, 3, D])
        part = sb("part", [P, 8, ST, D])
        cross = sb("cross", [P, 4, ST, D])
        comp = sb("comp", [P, 4, ST, D])
        product = sb("product", [P, ST, D])
        wT = sb("wT", [P, SEQ])
        z = sb("z", [P, SEQ])
        hT = sb("hT", [P, HB, SEQ])

        tables = sem("tables")
        loaded, made = sem("loaded"), sem("made")
        norm_a = Norm(nc, ctx, "spec_a", x, ident, ST, ps=ps_n, gain=ln[:, 0:1], shift=ln[:, 1:2])
        norm_c = Norm(nc, ctx, "spec_c", x, ident, ST, ps=ps_n, gain=ln[:, 2:3], shift=ln[:, 3:4])
        norm_a.bank_free = lambda c: (norm_c.xT_done.sem, norm_c.xT_done.at(max(c - 3, -2) if isinstance(c, int)
                                                                            else c - 3, 1))
        norm_c.bank_free = lambda c: (norm_a.xT_done.sem, norm_a.xT_done.at(c + 2, 1))
        diffed = signal("diffed", 1)
        x_mm = signal("x_mm", ST)
        d_mm = signal("d_mm", ST)
        d_ev = signal("d_ev", ST)
        x_ev = signal("x_ev", ST)
        scaled = signal("scaled", 2)
        parted = signal("parted", 1)
        cosined = signal("cosined", 2)
        HAM = 28
        hamilton = signal("hamilton", HAM)
        crossed = signal("crossed", 7)
        w_mm = signal("w_mm", 1)
        w_ev = signal("w_ev", 1)
        z_mm = signal("z_mm", 1)
        filtered = signal("filtered", 1)
        y_mm = signal("y_mm", 1)
        m_mm = signal("m_mm", 1)
        y_add = signal("y_add", 1)
        m_add = signal("m_add", 1)
        h_mm = signal("h_mm", 2)
        h_ev = signal("h_ev", HB)

        row_stats, row_mv, row_rstd = sem("row_stats"), sem("row_mv"), sem("row_rstd")
        stats = sb("stats", [P, TILES, 6])
        mean_var = sb("mean_var", [P, TILES, 2])
        veps = sb("veps", [P, TILES])
        power = sb("power", [P, TILES])
        rstd = sb("rstd", [P, TILES])
        fixed = [(hartley[:], w["hartley"]), (filt[:], w["filter"])]
        with nc.Block() as block:
            @block.sync
            def _(sp):
                for to, of in fixed:
                    sp.dma_start(to, of).then_inc(tables, 16)
                sp.wait_ge(tables, 16 * len(fixed))

            @block.vector
            def _(dve):
                dve.memset(quarter[:], math.pi / 2)
                dve.memset(one[:], 1.0)
                dve.memset(dT[:], 0.0)
                dve.memset(x[:, TILES:TILES + 3 * ST, :], 0.0)
                for t in range(TILES):
                    dve.bn_stats(stats[:, t, :], rows_x[:, t, :]).then_inc(row_stats, 1)
                for t in range(TILES):
                    dve.wait_ge(row_stats, t + 1)
                    dve.bn_aggr(mean_var[:, t, :], stats[:, t, :]).then_inc(row_mv, 1)
                dve.wait_ge(row_rstd, 3)
                for t in range(TILES):
                    dve.tensor_scalar(x[:, t, :], rows_x[:, t, :], mean_var[:, t, 0:1], rstd[:, t:t + 1],
                                      ALU.subtract, ALU.mult)

            @block.gpsimd
            def _(pool):
                pool.memset(power[:], -0.5).then_inc(row_rstd, 1)
                pool.wait_ge(row_mv, TILES)
                pool.tensor_scalar(veps[:], mean_var[:, :, 1], LN_EPS, None, ALU.add).then_inc(row_rstd, 1)
                pool.wait_ge(row_rstd, 2)
                pool.tensor_tensor(rstd[:], veps[:], power[:], ALU.pow).then_inc(row_rstd, 1)

        with nc.Fori(0, H1.LAYERS) as layer:
            layer_w = [(ln, "d_ln"), (qkv_w, "d_qkv_w"), (qkv_b, "d_qkv_b"), (proj_w, "d_proj_w"),
                       (proj_b, "d_proj_b"), (fc_w, "d_fc_w"), (fc_b, "d_fc_b"), (mp_w, "d_mp_w"), (mp_b, "d_mp_b")]
            with nc.Block() as block:
                @block.sync
                def _(sp):
                    for to, of in layer_w:
                        sp.dma_start(to[:], w[of][layer]).then_inc(loaded, 16)
                    sp.wait_ge(loaded, 16 * len(layer_w))

                @block.tensor
                def _(pe):
                    pe.wait_ge(loaded, 16 * len(layer_w))
                    pe.matmul(ps_y[:, 0, :], hartley[:], proj_w[:], start=True, stop=True).then_inc(made, 1)

                @block.vector
                def _(dve):
                    dve.wait_ge(made, 1)
                    dve.tensor_copy(head_proj[:], ps_y[:, 0, :])

            def part_of(u, i, n):
                return (rows[:, u, :, n, HD:WRAP], diff[:, u, :, n, :], rows[:, u, :, n, 0:D],
                        cosine[:, u, :, n, :])[i]

            with nc.Block() as block:
                @block.gpsimd
                def _(pool):
                    norm_a.start(nc, pool=pool)
                    norm_c.start(nc, pool=pool)
                    diffed.start(pool)
                    crossed.start(pool)

                    def differences(c, u):
                        pool.wait_ge(norm_a.xT_done.sem, norm_a.xT_done.at(c, 1))
                        pool.wait_ge(d_mm.sem, d_mm.at(c - 2, ST))
                        pool.tensor_tensor(dT[:, u, 1:SEQ], norm_a.xT[:, u, 1:SEQ], norm_a.xT[:, u, 0:SEQ - 1],
                                           ALU.subtract).then_inc(diffed.sem, 1)

                    def multiply(c, u):
                        pool.wait_ge(cosined.sem, cosined.at(c, 2))
                        pool.wait_ge(crossed.sem, crossed.at(c - 1, 7))
                        for j in range(4):
                            pool.tensor_tensor(cross[:, j, :, :], part_of(u, j, 0), part_of(u, 3 ^ j, 1),
                                               ALU.mult).then_inc(crossed.sem, 1)

                    def multiplied(c):
                        pool.wait_ge(crossed.sem, crossed.at(c, 4))
                        pool.tensor_tensor(cross[:, 0, :, :], cross[:, 0, :, :], cross[:, 1, :, :],
                                           ALU.add).then_inc(crossed.sem, 1)
                        pool.tensor_tensor(cross[:, 2, :, :], cross[:, 2, :, :], cross[:, 3, :, :],
                                           ALU.subtract).then_inc(crossed.sem, 1)
                        pool.wait_ge(crossed.sem, crossed.at(c, 6))
                        pool.wait_ge(hamilton.sem, hamilton.at(c - 1, HAM))
                        pool.tensor_tensor(comp[:, 3, :, :], cross[:, 0, :, :], cross[:, 2, :, :],
                                           ALU.subtract).then_inc(crossed.sem, 1)

                    for c in range(2):
                        norm_a.on_pool(pool, c)
                        differences(c, c)
                    norm_a.on_pool(pool, 2)
                    multiply(0, 0)
                    multiplied(0)

                    def body(c, u):
                        multiply(c + 1, 1 - u)
                        differences(c + 2, u)
                        multiplied(c + 1)
                        norm_c.on_pool(pool, c)
                        norm_a.on_pool(pool, c + 3)

                    pairs(pool, body)

                @block.tensor
                def _(pe):
                    norm_a.start(nc, pe=pe)
                    norm_c.start(nc, pe=pe)
                    for s in (x_mm, d_mm, w_mm, z_mm, y_mm, m_mm, h_mm):
                        s.start(pe)

                    def project(c, u, t):
                        pe.wait_ge(norm_a.xT_done.sem, norm_a.xT_done.at(c, 1))
                        pe.wait_ge(x_ev.sem, x_ev.at(c, t))
                        pe.matmul(ps_x[:], norm_a.xT[:, u, t * P:(t + 1) * P], qkv_w[:], start=True,
                                  stop=True).then_inc(x_mm.sem, 1)

                    def project_differences(c, u):
                        pe.wait_ge(diffed.sem, diffed.at(c, 1))
                        for t in range(ST):
                            pe.wait_ge(d_ev.sem, d_ev.at(c, t))
                            pe.matmul(ps_d[:], dT[:, u, t * P:(t + 1) * P], qkv_w[:, :, HD:WRAP], start=True,
                                      stop=True).then_inc(d_mm.sem, 1)

                    def turn(c):
                        pe.wait_ge(hamilton.sem, hamilton.at(c, HAM))
                        pe.wait_ge(w_ev.sem, w_ev.at(c - 1, 1))
                        for t in range(ST):
                            last = pe.transpose(ps_w[:, t * P:(t + 1) * P], product[:, t, :], ident[:])
                        last.then_inc(w_mm.sem, 1)

                    def to_frequencies(c):
                        pe.wait_ge(w_ev.sem, w_ev.at(c, 1))
                        pe.wait_ge(filtered.sem, filtered.at(c - 1, 1))
                        pe.matmul(ps_z[:], hartley[:], wT[:], start=True, stop=True).then_inc(z_mm.sem, 1)

                    def bias(b):
                        pe.matmul(ps_y[:], one[0:1, :], b[0:1, :].unsqueeze(1).to_broadcast([1, ST, D]),
                                  start=True, stop=False, skip_group_check=True)

                    def back(c):
                        pe.wait_ge(filtered.sem, filtered.at(c, 1))
                        for t in range(ST):
                            last = pe.matmul(ps_y[:, t, :], z[:, t * P:(t + 1) * P], head_proj[:], start=False,
                                             stop=(t == ST - 1), skip_group_check=True)
                        last.then_inc(y_mm.sem, 1)

                    def hidden(c, u):
                        pe.wait_ge(norm_c.xT_done.sem, norm_c.xT_done.at(c, 1))
                        for i in range(2):
                            pe.wait_ge(h_ev.sem, h_ev.at(c - 1, 2 * i + 2))
                            for b in range(2 * i, 2 * i + 2):
                                last = pe.matmul(ps_h[i][:, b % 2, :], fc_w[:, b * P:(b + 1) * P],
                                                 norm_c.xT[:, u, :], start=True, stop=True)
                            last.then_inc(h_mm.sem, 1)

                    def out(c):
                        pe.wait_ge(y_add.sem, y_add.at(c, 1))
                        bias(mp_b)
                        for b in range(HB):
                            pe.wait_ge(h_ev.sem, h_ev.at(c, b + 1))
                            for t in range(ST):
                                last = pe.matmul(ps_y[:, t, :], hT[:, b, t * P:(t + 1) * P], mp_w[:, b, :],
                                                 start=False, stop=(t == ST - 1 and b == HB - 1),
                                                 skip_group_check=True)
                        last.then_inc(m_mm.sem, 1)

                    for c in range(2):
                        norm_a.on_tensor(pe, c)
                        project(c, c, 0)
                        project_differences(c, c)
                        project(c, c, 1)

                    def body(c, u):
                        turn(c)
                        pe.wait_ge(m_add.sem, m_add.at(c - 1, 1))
                        bias(proj_b)
                        to_frequencies(c)
                        norm_a.on_tensor(pe, c + 2)
                        back(c)
                        project(c + 2, u, 0)
                        project_differences(c + 2, u)
                        project(c + 2, u, 1)
                        norm_c.on_tensor(pe, c)
                        hidden(c, u)
                        out(c)

                    pairs(pe, body)

                @block.scalar
                def _(act):
                    norm_a.start(nc, act=act)
                    norm_c.start(nc, act=act)
                    for s in (d_ev, scaled, cosined, w_ev, h_ev):
                        s.start(act)

                    def normal(c, u):
                        act.wait_ge(diffed.sem, diffed.at(c - 2, 1))
                        norm_a.on_scalar(act, c, u, (x_mm.sem, x_mm.at(c - 2, ST)))

                    def differences(c, u):
                        act.wait_ge(hamilton.sem, hamilton.at(c - 2, HAM))
                        for t in range(ST):
                            act.wait_ge(d_mm.sem, d_mm.at(c, t + 1))
                            act.activation(diff[:, u, t, :, :], ps_d[:], ACT.Copy).then_inc(d_ev.sem, 1)

                    def turns(c, u):
                        act.wait_ge(x_ev.sem, x_ev.at(c, ST))
                        values = rows[:, u, :, :, HD:WRAP]
                        act.activation(turns_of[:], values, ACT.Copy, scale=1 / (2 * math.pi)).then_inc(scaled.sem, 1)
                        act.activation(whole[:], values, ACT.Copy, scale=1 / (2 * math.pi),
                                       bias=ROUND).then_inc(scaled.sem, 1)

                    def cosines(c, u):
                        act.wait_ge(parted.sem, parted.at(c, 1))
                        act.activation(whole[:], turns_of[:], ACT.Abs).then_inc(cosined.sem, 1)
                        act.wait_ge(cosined.sem, cosined.at(c, 1))
                        act.activation(cosine[:, u, :, :, :], whole[:], ACT.Sin, bias=quarter[:, 0:1],
                                       scale=-2 * math.pi).then_inc(cosined.sem, 1)

                    def turned(c):
                        act.wait_ge(w_mm.sem, w_mm.at(c, 1))
                        act.wait_ge(z_mm.sem, z_mm.at(c - 1, 1))
                        act.activation(wT[:], ps_w[:], ACT.Copy).then_inc(w_ev.sem, 1)

                    def gelu(c):
                        act.wait_ge(m_mm.sem, m_mm.at(c - 1, 1))
                        for b in range(HB):
                            act.wait_ge(h_mm.sem, h_mm.at(c, b // 2 + 1))
                            act.activation(hT[:, b, :], ps_h[b // 2][:, b % 2, :], ACT.Gelu,
                                           bias=fc_b[:, b:b + 1]).then_inc(h_ev.sem, 1)

                    for c in range(2):
                        normal(c, c)
                        differences(c, c)
                        turns(c, c)
                        cosines(c, c)

                    def body(c, u):
                        turned(c)
                        normal(c + 2, u)
                        differences(c + 2, u)
                        norm_c.on_scalar(act, c, u, (h_mm.sem, h_mm.at(c - 2, 2)))
                        turns(c + 2, u)
                        gelu(c)
                        cosines(c + 2, u)

                    pairs(act, body)

                @block.vector
                def _(dve):
                    norm_a.start(nc, dve=dve)
                    norm_c.start(nc, dve=dve)
                    for s in (x_ev, parted, hamilton, filtered, y_add, m_add):
                        s.start(dve)

                    def two(c):
                        return x[:, bass.ts(c, ST), :]

                    def add_bias(c, u, t):
                        dve.wait_ge(x_mm.sem, x_mm.at(c, t + 1))
                        dve.tensor_tensor(rows[:, u, t, :, :], ps_x[:], qkv_b[:], ALU.add).then_inc(x_ev.sem, 1)

                    def part_turns(c):
                        dve.wait_ge(scaled.sem, scaled.at(c, 2))
                        dve.scalar_tensor_tensor(turns_of[:].rearrange("p t a d -> p (t a d)"),
                                                 whole[:].rearrange("p t a d -> p (t a d)"), ROUND,
                                                 turns_of[:].rearrange("p t a d -> p (t a d)"), ALU.subtract,
                                                 ALU.subtract).then_inc(parted.sem, 1)

                    SIGNS = [(ALU.subtract, ALU.add, ALU.subtract), (ALU.add, ALU.subtract, ALU.add),
                             (ALU.subtract, ALU.add, ALU.add)]


                    def products(c, u, i):
                        p0 = 4 * (i % 2)
                        if i == 0:
                            dve.wait_ge(d_ev.sem, d_ev.at(c, ST))
                        for j in range(4):
                            if i == 0 and j == 3:
                                dve.wait_ge(cosined.sem, cosined.at(c, 2))
                            dve.tensor_tensor(part[:, p0 + j, :, :], part_of(u, j, 0), part_of(u, i ^ j, 1),
                                              ALU.mult).then_inc(hamilton.sem, 1)

                    def sums(c, i):
                        p0 = 4 * (i % 2)
                        done = 7 * i
                        dve.wait_ge(hamilton.sem, hamilton.at(c, done + 2))
                        dve.tensor_tensor(part[:, p0, :, :], part[:, p0, :, :], part[:, p0 + 1, :, :],
                                          SIGNS[i][0]).then_inc(hamilton.sem, 1)
                        dve.wait_ge(hamilton.sem, hamilton.at(c, done + 4))
                        dve.tensor_tensor(part[:, p0 + 2, :, :], part[:, p0 + 2, :, :],
                                          part[:, p0 + 3, :, :], SIGNS[i][1]).then_inc(hamilton.sem, 1)
                        dve.wait_ge(hamilton.sem, hamilton.at(c, done + 6))
                        dve.tensor_tensor(comp[:, i, :, :], part[:, p0, :, :], part[:, p0 + 2, :, :],
                                          SIGNS[i][2]).then_inc(hamilton.sem, 1)

                    def multiply(c, u, i):
                        products(c, u, i)
                        sums(c, i)

                    def multiply_last(c, u):
                        for i in range(4):
                            if i < 3:
                                dve.wait_ge(hamilton.sem, hamilton.at(c, 7 * (i + 1)))
                            else:
                                dve.wait_ge(crossed.sem, crossed.at(c, 7))
                            dve.tensor_tensor(comp[:, i, :, :], comp[:, i, :, :], part_of(u, i, 2),
                                              ALU.mult).then_inc(hamilton.sem, 1)
                        dve.wait_ge(hamilton.sem, hamilton.at(c, 23))
                        dve.tensor_tensor(comp[:, 0, :, :], comp[:, 0, :, :], comp[:, 1, :, :],
                                          ALU.subtract).then_inc(hamilton.sem, 1)
                        dve.wait_ge(hamilton.sem, hamilton.at(c, 25))
                        dve.tensor_tensor(comp[:, 2, :, :], comp[:, 2, :, :], comp[:, 3, :, :],
                                          ALU.add).then_inc(hamilton.sem, 1)
                        dve.wait_ge(w_mm.sem, w_mm.at(c - 1, 1))
                        dve.wait_ge(hamilton.sem, hamilton.at(c, 27))
                        dve.tensor_tensor(product[:], comp[:, 0, :, :], comp[:, 2, :, :],
                                          ALU.subtract).then_inc(hamilton.sem, 1)

                    def filter_rows(c):
                        dve.wait_ge(z_mm.sem, z_mm.at(c, 1))
                        dve.wait_ge(y_mm.sem, y_mm.at(c - 1, 1))
                        dve.tensor_tensor(z[:], ps_z[:], filt[:], ALU.mult).then_inc(filtered.sem, 1)

                    def add_attention(c):
                        dve.wait_ge(y_mm.sem, y_mm.at(c, 1))
                        dve.tensor_tensor(two(c), ps_y[:], two(c), ALU.add).then_inc(y_add.sem, 1)

                    def statistics_c(c):
                        dve.wait_ge(y_add.sem, y_add.at(c, 1))
                        dve.sem_inc(norm_c.turns, 1)
                        norm_c.on_vector(dve, c)

                    def add_gelu(c):
                        dve.wait_ge(m_mm.sem, m_mm.at(c, 1))
                        dve.tensor_tensor(two(c), ps_y[:], two(c), ALU.add).then_inc(m_add.sem, 1)

                    for c in range(2):
                        norm_a.on_vector(dve, c)
                        norm_a.on_vector_scale(dve, c)
                        add_bias(c, c, 0)
                        add_bias(c, c, 1)
                        part_turns(c)
                    norm_a.on_vector(dve, 2)
                    for i in range(3):
                        multiply(0, 0, i)
                    multiply_last(0, 0)
                    norm_a.on_vector_scale(dve, 2)

                    def body(c, u):
                        products(c + 1, 1 - u, 0)
                        filter_rows(c)
                        sums(c + 1, 0)
                        add_attention(c)
                        statistics_c(c)
                        add_bias(c + 2, u, 0)
                        multiply(c + 1, 1 - u, 1)
                        norm_c.on_vector_scale(dve, c)
                        add_bias(c + 2, u, 1)
                        multiply(c + 1, 1 - u, 2)
                        part_turns(c + 2)
                        norm_a.on_vector(dve, c + 3)
                        multiply_last(c + 1, 1 - u)
                        norm_a.on_vector_scale(dve, c + 3)
                        add_gelu(c)

                    pairs(dve, body)

            ctx.clear(nc)

        with nc.Block() as block:
            @block.vector
            def _(dve):
                dve.tensor_tensor(rows_x[:, 0:TILES, :], rows_x[:, 0:TILES, :], x[:, 0:TILES, :], ALU.add)

        ctx.clear(nc)


def build(nc, a):
    with ExitStack() as ctx:
        def sb(n, shape, dt=F32):
            return ctx.enter_context(nc.sbuf_tensor(n, shape, dt))

        def sem(n):
            return ctx.enter_context(nc.semaphore(n))

        E, EH, EB = M0.E, M0.EH, M0.EB
        F_H = 384
        FB = F_H // P
        x = sb("x", [P, TILES + 2 * CT, D])
        ident = sb("ident", [P, P])
        order = sb("order", [P, E])
        upper = sb("upper", [P, P])
        ones = sb("ones", [P, P])
        tile_at = sb("tile_at", [P, M0.TABLE_TILES])
        zeros = sb("zeros", [P, D])
        moe_gate = sb("moe_gate", [P, E])
        moe_w1 = sb("moe_w1", [P, E * EH])
        moe_w3 = sb("moe_w3", [P, E * EH])
        moe_w2 = sb("moe_w2", [P, E * EB, D])
        ff_w1 = sb("ff_w1", [P, F_H])
        ff_w3 = sb("ff_w3", [P, F_H])
        ff_w2 = sb("ff_w2", [P, FB, D])
        ff_i1 = sb("ff_i1", [P, F_H], I32)
        ff_i3 = sb("ff_i3", [P, F_H], I32)
        ff_i2 = sb("ff_i2", [P, FB, D], I32)
        loaded = sem("loaded")
        dequant = sem("dequant")
        later_loaded = sem("later_loaded")
        scatter_sems = [sem(f"scattered{i}") for i in range(2)]
        gather_sems = [sem(f"gathered{i}") for i in range(2)]
        slot = sb("slot", [P, TILES + 2 * CT, 2], U32)
        share = sb("share", [P, 2, TILES + 2 * CT])
        slots_in = nc.dram_tensor("slots_in", (M0.TABLE_TILES, P, D), F32).ap()
        slots_out = nc.dram_tensor("slots_out", (M0.SLOT_TILES, P, D), F32).ap()
        stored = sem("stored")

        rows = a["h"].rearrange("b (t p) d -> p (b t) d", p=P)

        first = [(x[:, 0:TILES, :], rows), (ident[:], a["ident"])]
        later = [(slots_in.rearrange("t p d -> p t d"), zeros[:].unsqueeze(1).to_broadcast([P, M0.TABLE_TILES, D])),
                 (order[:], a["order"]), (upper[:], a["upper"]), (tile_at[:], a["tile_at"]),
                 (moe_gate[:], a["moe_gate"]), (moe_w1[:], a["moe_w1"]), (moe_w3[:], a["moe_w3"]),
                 (moe_w2[:], a["moe_w2"].rearrange("(n p) d -> p n d", p=P)),
                 (ff_i1[:], a["ff_w1"]), (ff_i3[:], a["ff_w3"]),
                 (ff_i2[:], a["ff_w2"].rearrange("(n p) d -> p n d", p=P))]
        with nc.Block() as block:
            @block.sync
            def _(sp):
                for to, of in first:
                    sp.dma_start(to, of).then_inc(loaded, 16)
                sp.wait_ge(loaded, 16 * len(first))

            @block.gpsimd
            def _(pool):
                pool.memset(x[:, TILES:TILES + 2 * CT, :], 0.0)
                pool.memset(ones[:], 1.0)
                pool.memset(zeros[:], 0.0)

        def load_later(sp):
            for to, of in later:
                sp.dma_start(to, of).then_inc(later_loaded, 16)

        mixed_attention(nc, x, ident, a, load_later)

        with nc.Block() as block:
            @block.sync
            def _(sp):
                sp.wait_ge(later_loaded, 16 * len(later))

            @block.vector
            def _(dve):
                dve.wait_ge(later_loaded, 16 * len(later))
                for to, of in ((ff_w1, ff_i1), (ff_w3, ff_i3), (ff_w2, ff_i2)):
                    dve.tensor_scalar(to[:], of[:], float(np.float32(1.0 / 127.0)), None,
                                      ALU.mult).then_inc(dequant, 1)

        groups = M0.GROUPS // 2
        gathers = [0, 0]
        for n in range(2):
            routed_experts(nc, f"moe{n}", x, ident, moe_w1, moe_w3, moe_w2, moe_gate,
                           (order, upper, ones, tile_at), slots_in, slots_out, slot, share,
                           Alternating(scatter_sems, 16 * 2 * M0.G, ahead=0, used=[n * groups] * 2))
            results = (slot, share, slots_out,
                       Alternating(gather_sems, 16 * 2 * ST, ahead=0, used=gathers))
            if n == 0:
                single_attention(nc, x, ident, a, results)
                gathers = [(SEQS + 4) // 2, (SEQS + 3) // 2]
            else:
                grouped_attention(nc, x, ident, a, results)
        feed_forward(nc, "ff0", x, ident, ff_w1, ff_w3, ff_w2, FB)
        spectral_layers(nc, x, ident, a)
        feed_forward(nc, "ff1", x, ident, ff_w1, ff_w3, ff_w2, FB)

        with nc.Block() as block:
            @block.sync
            def _(sp):
                sp.dma_start(a["out"].rearrange("b (t p) d -> p (b t) d", p=P),
                             x[:, 0:TILES, :]).then_inc(stored, 16)
                sp.wait_ge(stored, 16)


def kernel(**inputs):
    import concourse.bacc as bacc
    from concourse.bass_utils import run_bass_kernel_spmd

    np_in = {k: np.asarray(v) for k, v in inputs.items()}
    f32 = np.float32

    def turned(a, *axes):
        return np.ascontiguousarray(np.transpose(a, axes))

    arrays = {
        "h": np_in["L0_attn_a_h"],
        "ident": np.eye(P, dtype=f32),
        "order": np.broadcast_to(np.arange(8, 0, -1, dtype=f32), (P, 8)).copy(),
        "upper": np.triu(np.ones((P, P), f32), 1),
        "tile_at": np.broadcast_to(np.arange(M0.TABLE_TILES, dtype=f32), (P, M0.TABLE_TILES)).copy(),
        "moe_gate": turned(np_in["L0_ffn_gate_w"], 1, 0),
        "moe_w1": turned(np_in["L0_ffn_w1"], 2, 0, 1).reshape(D, -1),
        "moe_w3": turned(np_in["L0_ffn_w3"], 2, 0, 1).reshape(D, -1),
        "moe_w2": turned(np_in["L0_ffn_w2"], 0, 2, 1).reshape(-1, D),
        "ff_w1": turned(np_in["L1_ffn_w_gate"], 1, 0),
        "ff_w3": turned(np_in["L1_ffn_w_up"], 1, 0),
        "ff_w2": turned(np_in["L1_ffn_w_down"], 1, 0),
    }
    def rows(a):
        return np.broadcast_to(a, (P,) + a.shape).copy()

    q_at = np.arange(SEQ)[:, None]
    k_at = np.arange(SEQ)[None, :]
    masked = np.where(q_at >= k_at, f32(0), f32(BIG)).reshape(ST, P, SEQ)
    outside = np.where((q_at >= k_at) & (q_at - k_at < A0.WINDOW), f32(0), f32(BIG)).reshape(ST, P, SEQ)
    valid = (np.arange(A0.NB)[None, :] + 1) * A0.CR - 1 <= q_at
    some = valid.any(-1, keepdims=True)
    blocks = np.zeros((SEQ, A0.H, A0.C), f32)
    blocks[:, :, 0:A0.NB] = np.where(np.where(some, valid, True), f32(0), f32(BIG))[:, None, :]
    turn = 1.0 / 10000.0 ** (np.arange(16, dtype=f32) * 2.0 / 32)
    angle = (np.arange(SEQ, dtype=f32)[:, None] * turn.astype(f32)[None, :]).astype(f32)
    cs = np.stack([np.tile(np.cos(angle), (1, 2)), np.tile(np.sin(angle), (1, 2))], 1)
    mean_w = np.zeros((SEQ, A0.H, A0.NB), f32)
    mean_w[np.arange(SEQ), :, np.arange(SEQ) // A0.CR] = 1.0 / A0.CR

    def tiled(a):
        return np.ascontiguousarray(a.reshape((ST, P) + a.shape[1:]).swapaxes(0, 1)).astype(f32)

    q_gain = np_in["L0_attn_a_g_qnorm"]
    arrays.update({
        "a_qc": turned(np_in["L0_attn_a_w_qc"], 1, 0),
        "a_qup": np_in["L0_attn_a_w_qup"],
        "a_group": turned(np_in["L0_attn_a_w_out_group"], 2, 0, 1),
        "a_out": turned(np_in["L0_attn_a_w_out"].reshape(2, 64, D), 1, 0, 2),
        "a_kv": np.concatenate([np_in["L0_attn_a_w_k"], np_in["L0_attn_a_w_v"]], 1),
        "a_gain_q": rows(np.stack([q_gain, q_gain])),
        "a_gain_k": rows(np.stack([np_in["L0_attn_a_g_knorm"]] * 2)),
        "a_gain_col": np.concatenate([q_gain, q_gain])[:, None].copy(),
        "a_gate_w": np.concatenate([np_in["L0_attn_a_w_gate"]] * 2, 0),
        "a_gate_b": rows(np_in["L0_attn_a_b_gate"]),
        "a_sink": rows(np_in["L0_attn_a_sink_logit"]),
        "rope": tiled(cs),
        "causal": np.concatenate([masked[0][:, 0:P], masked[1]], 1),
        "window": np.concatenate([outside[0][:, 0:P], outside[1][:, P - A0.WINDOW:]], 1),
        "blocks": tiled(blocks),
        "any_block": tiled(some.astype(f32))[:, :, 0].copy(),
        "mean_w": tiled(mean_w.reshape(SEQ, -1)),
        "diagonal": np.repeat(np.eye(A0.H, dtype=f32), A0.NB, 0),
    })
    b = "L0_attn_b_"
    arrays.update({
        "b_wq": turned(np_in[b + "Wq"], 1, 0), "b_wk": turned(np_in[b + "Wk"], 1, 0),
        "b_wv": turned(np_in[b + "Wv"], 1, 0), "b_wo": turned(np_in[b + "Wo"], 1, 0),
        "b_bq": np_in[b + "bq"][:, None].copy(), "b_bk": np_in[b + "bk"][:, None].copy(),
        "b_bv": rows(np_in[b + "bv"]), "b_bo": rows(np_in[b + "bo"]),
    })
    g = "L1_attn_a_"
    keys_at = np.broadcast_to(np.concatenate([np.arange(P), np.arange(SEQ)]).astype(f32), (P, P + SEQ))
    arrays.update({
        "c_wq": np_in[g + "Wq"].reshape(G1.IN, G1.H, G1.HD // 2, 2),
        "c_wk": np.repeat(np_in[g + "Wk"].reshape(G1.IN, G1.KVH, 1, G1.HD), 2, 2),
        "c_wv": np_in[g + "Wv"],
        "c_wo": turned(np_in[g + "Wo"].reshape(G1.HP, P, D), 1, 0, 2),
        "c_phase": rows(np_in[g + "q_phase_angle"]),
        "c_slope": rows(np_in[g + "alibi_log_slopes"]),
        "keys_at": keys_at.copy(),
    })
    e = "L1_attn_b_"
    LAY = H1.LAYERS

    def spread(a):
        return np.broadcast_to(a[:, None], (LAY, P) + a.shape[1:]).copy()

    def by_part(a):
        a = a.reshape(a.shape[:-1] + (H1.H, 3, H1.HD)).swapaxes(-3, -2)
        return np.concatenate([a[..., -1:, :], a], -2).reshape(a.shape[:-3] + (3, H1.WRAP))

    def hartley(n):
        at = 2 * np.pi * (np.arange(n)[:, None] * np.arange(n)[None, :] % n) / n
        return np.cos(at) + np.sin(at)

    ks = np.fft.fftfreq(SEQ)[:, None, None]
    kh = np.fft.fftfreq(H1.H)[None, :, None]
    kd = np.fft.fftfreq(H1.HD)[None, None, :]
    even = np.cos(np.arctan(np.log(np.sqrt(ks ** 2 + kh ** 2 + kd ** 2 + 1e-10) + 1e-10)))
    lam = np.arange(SEQ, dtype=f32) / f32(SEQ)
    tau = np.arange(SEQ, dtype=f32) * f32(0.1)
    modulation = np.sin(tau + lam) * np.cos(tau - f32(2) * lam + f32(0.5) * lam ** 2)
    filt = even.reshape(SEQ, D) * (1.0 + 0.1 * modulation.astype(np.float64))[:, None] / (H1.H * H1.HD)
    arrays.update({
        "d_ln": np.stack([np_in[e + n] for n in ("ln1_w", "ln1_b", "ln2_w", "ln2_b")], -1),
        "d_qkv_w": np.ascontiguousarray(by_part(np_in[e + "attn_w"])),
        "d_qkv_b": spread(by_part(np_in[e + "attn_b"])),
        "d_proj_w": np_in[e + "aproj_w"],
        "d_proj_b": np_in[e + "aproj_b"][:, None].copy(),
        "d_fc_w": np_in[e + "fc_w"],
        "d_fc_b": turned(np_in[e + "fc_b"].reshape(LAY, H1.HB, P), 0, 2, 1),
        "d_mp_w": turned(np_in[e + "mproj_w"].reshape(LAY, H1.HB, P, D), 0, 2, 1, 3),
        "d_mp_b": np_in[e + "mproj_b"][:, None].copy(),
        "hartley": np.kron(hartley(H1.H), hartley(H1.HD)).astype(f32),
        "filter": np.ascontiguousarray(filt.T).astype(f32),
    })
    nc = bacc.Bacc("TRN2", target_bir_lowering=False, num_devices=1)
    aps = {k: nc.dram_tensor(f"in_{k}", v.shape, mybir.dt.from_np(v.dtype), kind="ExternalInput").ap()
           for k, v in arrays.items()}
    aps["out"] = nc.dram_tensor("out", (16, SEQ, D), F32, kind="ExternalOutput").ap()
    build(nc, aps)
    r = run_bass_kernel_spmd(nc, [{f"in_{k}": v for k, v in arrays.items()}], core_ids=[0])
    return r.results[0]["out"]
```
